# Optimizing a Trainium2 kernel written in Bass

```python
import numpy as np
import jax
import jax.numpy as jnp

def _softmax(x, axis=-1):
    return jax.nn.softmax(x, axis=axis)

def _gelu(x):
    return jax.nn.gelu(x, approximate=True)

def _silu(x):
    return jax.nn.silu(x)

def _sigmoid(x):
    return jax.nn.sigmoid(x)

def _layernorm(x, axis=-1, eps=1e-05):
    m = jnp.mean(x, axis=axis, keepdims=True)
    v = jnp.var(x, axis=axis, keepdims=True)
    return (x - m) / jnp.sqrt(v + eps)

def _scatter_add(tgt, idx, src, axis=0):
    return tgt.at[idx].add(src)

def _segment_sum(src, seg, n):
    return jax.ops.segment_sum(src, seg, n)
kernel_name = 'mk_sandwich_d2_jaxref_r8_f50fb9'

def setup_inputs(seed: int=0):
    np.random.seed(seed)
    _w = jnp.asarray

    def _L0_attn_setup():
        import jax, jax.numpy as jnp
        import numpy as np
        from jax import lax
        H = 512
        DIN = 1024
        N = 16
        K = 4
        R = 32
        B_SZ = 2
        L = 256
        EPS = 1e-06

        def rmsnorm(x, w):
            return x * lax.rsqrt(jnp.mean(x * x, axis=-1, keepdims=True) + EPS) * w

        def _selective_scan(x, dt, A, Bm, Cm):
            xT = jnp.transpose(x, (2, 0, 1))
            dtT = jnp.transpose(dt, (2, 0, 1))
            BT = jnp.transpose(Bm, (2, 0, 1))
            CT = jnp.transpose(Cm, (2, 0, 1))

            def step(h, inp):
                x_t, dt_t, B_t, C_t = inp
                dA = jnp.exp(dt_t[..., None] * A)
                dBx = dt_t[..., None] * B_t[:, None, :] * x_t[..., None]
                h = dA * h + dBx
                y = jnp.einsum('bdn,bn->bd', h, C_t)
                return (h, y)
            h0 = jnp.zeros((x.shape[0], x.shape[1], A.shape[1]), dtype=x.dtype)
            _, ys = lax.scan(step, h0, (xT, dtT, BT, CT))
            return jnp.transpose(ys, (1, 2, 0))
        key = jax.random.key(seed)
        ks = jax.random.split(key, 8)
        hidden_states = jax.random.normal(ks[0], (B_SZ, L, H), dtype=jnp.float32)
        s = 0.02
        in_proj_w = jax.random.normal(ks[1], (H, 2 * DIN), dtype=jnp.float32) * s
        conv_w = jax.random.normal(ks[2], (DIN, K), dtype=jnp.float32) * 0.2
        conv_b = jax.random.normal(ks[3], (DIN,), dtype=jnp.float32) * 0.02
        x_proj_w = jax.random.normal(ks[4], (R + 2 * N, DIN), dtype=jnp.float32) * s
        dt_proj_w = jax.random.normal(ks[5], (DIN, R), dtype=jnp.float32) * s
        dt_bias = jax.random.normal(ks[6], (DIN,), dtype=jnp.float32) * 0.5 - 4.0
        A_log = jnp.log(jnp.broadcast_to(jnp.arange(1, N + 1, dtype=jnp.float32)[None, :], (DIN, N)))
        D_param = jnp.ones((DIN,), dtype=jnp.float32)
        out_proj_w = jax.random.normal(ks[7], (H, DIN), dtype=jnp.float32) * s
        dt_ln_w = jnp.ones((R,), dtype=jnp.float32)
        B_ln_w = jnp.ones((N,), dtype=jnp.float32)
        C_ln_w = jnp.ones((N,), dtype=jnp.float32)
        return dict(hidden_states=hidden_states, in_proj_w=in_proj_w, conv_w=conv_w, conv_b=conv_b, x_proj_w=x_proj_w, dt_proj_w=dt_proj_w, dt_bias=dt_bias, A_log=A_log, D_param=D_param, out_proj_w=out_proj_w, dt_ln_w=dt_ln_w, B_ln_w=B_ln_w, C_ln_w=C_ln_w)
    _L0_attn_in = _L0_attn_setup()

    def _L0_ffn_setup():
        import jax, jax.numpy as jnp
        import numpy as np
        B, S, D, O, E, R = (4, 256, 512, 512, 8, 16)
        SCALING = 32.0 / 16.0
        MAX_THRESHOLD = 0.125
        key = jax.random.key(seed)
        ks = jax.random.split(key, 8)
        return {'x': jax.random.normal(ks[0], (B, S, D), jnp.float32), 'W_base': jax.random.normal(ks[1], (O, D), jnp.float32) * (1.0 / np.sqrt(D)), 'b_base': jax.random.normal(ks[2], (O,), jnp.float32) * 0.02, 'W_gate': jax.random.normal(ks[3], (E, D), jnp.float32) * (1.0 / np.sqrt(D)), 'W_thr': jax.random.normal(ks[4], (D,), jnp.float32) * (1.0 / np.sqrt(D)), 'b_thr': jax.random.normal(ks[5], (1,), jnp.float32) * 0.02, 'A_w': jax.random.normal(ks[6], (E, R, D), jnp.float32) * (1.0 / np.sqrt(D)), 'B_w': jax.random.normal(ks[7], (E, O, R), jnp.float32) * (1.0 / np.sqrt(R))}
    _L0_ffn_in = _L0_ffn_setup()

    def _L1_attn_setup():
        import jax, jax.numpy as jnp
        import numpy as np
        H_M, P_M, G_M, N_M, K_CONV, CHUNK = (128, 64, 8, 128, 4, 128)
        D_MODEL = 512
        D_INNER = H_M * P_M
        CONV_DIM = D_INNER + 2 * G_M * N_M
        PROJ_DIM = D_INNER + CONV_DIM + H_M
        EPS = 1e-05

        def segsum(x):
            l = x.shape[-1]
            xe = jnp.broadcast_to(x[..., None], x.shape + (l,))
            m1 = jnp.tril(jnp.ones((l, l), dtype=bool), -1)
            s = jnp.cumsum(jnp.where(m1, xe, 0.0), axis=-2)
            m2 = jnp.tril(jnp.ones((l, l), dtype=bool), 0)
            return jnp.where(m2, s, -jnp.inf)

        def causal_conv(x, w, bconv):
            k = w.shape[1]
            s = x.shape[1]
            xp = jnp.pad(x, ((0, 0), (k - 1, 0), (0, 0)))
            y = sum((xp[:, i:i + s, :] * w[:, i] for i in range(k)))
            return y + bconv
        key = jax.random.key(seed)
        ks = jax.random.split(key, 8)
        B_, S = (1, 256)
        sc = 0.02
        return {'x': jax.random.normal(ks[0], (B_, S, D_MODEL), dtype=jnp.float32), 'norm_w': jnp.ones((D_MODEL,), dtype=jnp.float32), 'in_proj_w': jax.random.normal(ks[1], (PROJ_DIM, D_MODEL), dtype=jnp.float32) * sc, 'conv_w': jax.random.normal(ks[2], (CONV_DIM, K_CONV), dtype=jnp.float32) * 0.2, 'conv_b': jnp.zeros((CONV_DIM,), dtype=jnp.float32), 'dt_bias': jax.random.uniform(ks[3], (H_M,), dtype=jnp.float32) * 0.1, 'A_log': jnp.log(1.0 + 15.0 * jax.random.uniform(ks[4], (H_M,), dtype=jnp.float32)), 'Dp': jnp.ones((H_M,), dtype=jnp.float32), 'gnorm_w': jnp.ones((D_INNER,), dtype=jnp.float32), 'out_proj_w': jax.random.normal(ks[5], (D_MODEL, D_INNER), dtype=jnp.float32) * sc}
    _L1_attn_in = _L1_attn_setup()

    def _L1_ffn_setup():
        import jax, jax.numpy as jnp
        import numpy as np
        BS = 128
        FP8_MAX = 448.0

        def act_quant(x):
            T, K = x.shape
            xb = x.reshape(T, K // BS, BS)
            amax = jnp.max(jnp.abs(xb), axis=-1)
            scale = amax / FP8_MAX + 1e-12
            xq = (xb / scale[:, :, None]).reshape(T, K)
            return (xq, scale)

        def linear_dsv3(x, wq, w_scale):
            T, K = x.shape
            N = wq.shape[0]
            xq, xs = act_quant(x)
            xdq = (xq.reshape(T, K // BS, BS) * xs[:, :, None]).reshape(T, K)
            wdq = (wq.reshape(N // BS, BS, K // BS, BS) * w_scale[:, None, :, None]).reshape(N, K)
            return xdq @ wdq.T
        key = jax.random.key(seed)
        ks = jax.random.split(key, 4)
        DIM, INTER = (512, 1792)

        def make_qweight(k, n, m):
            w = jax.random.normal(k, (n, m), dtype=jnp.float32) * 0.02
            wb = w.reshape(n // BS, BS, m // BS, BS)
            amax = jnp.max(jnp.abs(wb), axis=(1, 3))
            scale = amax / FP8_MAX + 1e-12
            wq = (wb / scale[:, None, :, None]).reshape(n, m)
            return (wq, scale)
        x = jax.random.normal(ks[0], (2, 128, DIM), dtype=jnp.float32)
        w1, w1_scale = make_qweight(ks[1], INTER, DIM)
        w3, w3_scale = make_qweight(ks[2], INTER, DIM)
        w2, w2_scale = make_qweight(ks[3], DIM, INTER)
        return {'x': x, 'w1': w1, 'w1_scale': w1_scale, 'w3': w3, 'w3_scale': w3_scale, 'w2': w2, 'w2_scale': w2_scale}
    _L1_ffn_in = _L1_ffn_setup()
    _d = {'L0_attn_hidden_states': _L0_attn_in['hidden_states'], 'L0_attn_in_proj_w': _L0_attn_in['in_proj_w'], 'L0_attn_conv_w': _L0_attn_in['conv_w'], 'L0_attn_conv_b': _L0_attn_in['conv_b'], 'L0_attn_x_proj_w': _L0_attn_in['x_proj_w'], 'L0_attn_dt_proj_w': _L0_attn_in['dt_proj_w'], 'L0_attn_dt_bias': _L0_attn_in['dt_bias'], 'L0_attn_A_log': _L0_attn_in['A_log'], 'L0_attn_D_param': _L0_attn_in['D_param'], 'L0_attn_out_proj_w': _L0_attn_in['out_proj_w'], 'L0_attn_dt_ln_w': _L0_attn_in['dt_ln_w'], 'L0_attn_B_ln_w': _L0_attn_in['B_ln_w'], 'L0_attn_C_ln_w': _L0_attn_in['C_ln_w'], 'L0_ffn_W_base': _L0_ffn_in['W_base'], 'L0_ffn_b_base': _L0_ffn_in['b_base'], 'L0_ffn_W_gate': _L0_ffn_in['W_gate'], 'L0_ffn_W_thr': _L0_ffn_in['W_thr'], 'L0_ffn_b_thr': _L0_ffn_in['b_thr'], 'L0_ffn_A_w': _L0_ffn_in['A_w'], 'L0_ffn_B_w': _L0_ffn_in['B_w'], 'L1_attn_norm_w': _L1_attn_in['norm_w'], 'L1_attn_in_proj_w': _L1_attn_in['in_proj_w'], 'L1_attn_conv_w': _L1_attn_in['conv_w'], 'L1_attn_conv_b': _L1_attn_in['conv_b'], 'L1_attn_dt_bias': _L1_attn_in['dt_bias'], 'L1_attn_A_log': _L1_attn_in['A_log'], 'L1_attn_Dp': _L1_attn_in['Dp'], 'L1_attn_gnorm_w': _L1_attn_in['gnorm_w'], 'L1_attn_out_proj_w': _L1_attn_in['out_proj_w'], 'L1_ffn_w1': _L1_ffn_in['w1'], 'L1_ffn_w1_scale': _L1_ffn_in['w1_scale'], 'L1_ffn_w3': _L1_ffn_in['w3'], 'L1_ffn_w3_scale': _L1_ffn_in['w3_scale'], 'L1_ffn_w2': _L1_ffn_in['w2'], 'L1_ffn_w2_scale': _L1_ffn_in['w2_scale']}
    _x0 = _d['L0_attn_hidden_states']
    _d['L0_attn_hidden_states'] = jax.random.normal(jax.random.fold_in(jax.random.key(seed), 1), (4, 256, 512), dtype=_x0.dtype)
    del _x0
    return _d

def reference(L0_attn_hidden_states, L0_attn_in_proj_w, L0_attn_conv_w, L0_attn_conv_b, L0_attn_x_proj_w, L0_attn_dt_proj_w, L0_attn_dt_bias, L0_attn_A_log, L0_attn_D_param, L0_attn_out_proj_w, L0_attn_dt_ln_w, L0_attn_B_ln_w, L0_attn_C_ln_w, L0_ffn_W_base, L0_ffn_b_base, L0_ffn_W_gate, L0_ffn_W_thr, L0_ffn_b_thr, L0_ffn_A_w, L0_ffn_B_w, L1_attn_norm_w, L1_attn_in_proj_w, L1_attn_conv_w, L1_attn_conv_b, L1_attn_dt_bias, L1_attn_A_log, L1_attn_Dp, L1_attn_gnorm_w, L1_attn_out_proj_w, L1_ffn_w1, L1_ffn_w1_scale, L1_ffn_w3, L1_ffn_w3_scale, L1_ffn_w2, L1_ffn_w2_scale):

    def _L0_attn_ref(hidden_states, in_proj_w, conv_w, conv_b, x_proj_w, dt_proj_w, dt_bias, A_log, D_param, out_proj_w, dt_ln_w, B_ln_w, C_ln_w):
        import jax, jax.numpy as jnp
        import numpy as np
        from jax import lax
        H = 512
        DIN = 1024
        N = 16
        K = 4
        R = 32
        B_SZ = 2
        L = 256
        EPS = 1e-06

        def rmsnorm(x, w):
            return x * lax.rsqrt(jnp.mean(x * x, axis=-1, keepdims=True) + EPS) * w

        def _selective_scan(x, dt, A, Bm, Cm):
            xT = jnp.transpose(x, (2, 0, 1))
            dtT = jnp.transpose(dt, (2, 0, 1))
            BT = jnp.transpose(Bm, (2, 0, 1))
            CT = jnp.transpose(Cm, (2, 0, 1))

            def step(h, inp):
                x_t, dt_t, B_t, C_t = inp
                dA = jnp.exp(dt_t[..., None] * A)
                dBx = dt_t[..., None] * B_t[:, None, :] * x_t[..., None]
                h = dA * h + dBx
                y = jnp.einsum('bdn,bn->bd', h, C_t)
                return (h, y)
            h0 = jnp.zeros((x.shape[0], x.shape[1], A.shape[1]), dtype=x.dtype)
            _, ys = lax.scan(step, h0, (xT, dtT, BT, CT))
            return jnp.transpose(ys, (1, 2, 0))
        proj = hidden_states @ in_proj_w
        x, z = jnp.split(proj, 2, axis=-1)
        x = jnp.transpose(x, (0, 2, 1))
        z = jnp.transpose(z, (0, 2, 1))
        Lq = x.shape[-1]
        xp = jnp.pad(x, ((0, 0), (0, 0), (K - 1, 0)))
        xc = conv_b[None, :, None]
        for k in range(K):
            xc = xc + conv_w[None, :, k:k + 1] * xp[:, :, k:k + Lq]
        xc = jax.nn.silu(xc)
        ssm_p = jnp.einsum('bdl,ed->ble', xc, x_proj_w)
        dt_r = rmsnorm(ssm_p[..., :R], dt_ln_w)
        Bm = rmsnorm(ssm_p[..., R:R + N], B_ln_w)
        Cm = rmsnorm(ssm_p[..., R + N:], C_ln_w)
        dt = jnp.einsum('blr,dr->bdl', dt_r, dt_proj_w)
        dt = jax.nn.softplus(dt + dt_bias[None, :, None])
        A = -jnp.exp(A_log)
        Bm = jnp.transpose(Bm, (0, 2, 1))
        Cm = jnp.transpose(Cm, (0, 2, 1))
        ys = _selective_scan(xc, dt, A, Bm, Cm)
        y = (ys + D_param[None, :, None] * xc) * jax.nn.silu(z)
        return jnp.einsum('bdl,hd->blh', y, out_proj_w)

    def _L0_ffn_ref(x, W_base, b_base, W_gate, W_thr, b_thr, A_w, B_w):
        import jax, jax.numpy as jnp
        import numpy as np
        B, S, D, O, E, R = (4, 256, 512, 512, 8, 16)
        SCALING = 32.0 / 16.0
        MAX_THRESHOLD = 0.125
        base = jnp.einsum('bsd,od->bso', x, W_base) + b_base
        xf = x.reshape(-1, D)
        gate = jax.nn.softmax(xf @ W_gate.T, axis=-1)
        thr = jax.nn.sigmoid(xf @ W_thr + b_thr[0]) * MAX_THRESHOLD
        adapted = gate - thr[:, None]
        selected = (adapted >= 0).astype(x.dtype)
        w = adapted * selected
        wsum = jnp.sum(w, axis=-1, keepdims=True)
        wsum = jnp.where(wsum == 0, jnp.ones_like(wsum), wsum)
        w = w / wsum
        h = jnp.einsum('nd,erd->ner', xf, A_w)
        moe = jnp.einsum('ner,ne,eor->no', h, w, B_w) * SCALING
        return base + moe.reshape(base.shape)

    def _L1_attn_ref(x, norm_w, in_proj_w, conv_w, conv_b, dt_bias, A_log, Dp, gnorm_w, out_proj_w):
        import jax, jax.numpy as jnp
        import numpy as np
        H_M, P_M, G_M, N_M, K_CONV, CHUNK = (128, 64, 8, 128, 4, 128)
        D_MODEL = 512
        D_INNER = H_M * P_M
        CONV_DIM = D_INNER + 2 * G_M * N_M
        PROJ_DIM = D_INNER + CONV_DIM + H_M
        EPS = 1e-05

        def segsum(x):
            l = x.shape[-1]
            xe = jnp.broadcast_to(x[..., None], x.shape + (l,))
            m1 = jnp.tril(jnp.ones((l, l), dtype=bool), -1)
            s = jnp.cumsum(jnp.where(m1, xe, 0.0), axis=-2)
            m2 = jnp.tril(jnp.ones((l, l), dtype=bool), 0)
            return jnp.where(m2, s, -jnp.inf)

        def causal_conv(x, w, bconv):
            k = w.shape[1]
            s = x.shape[1]
            xp = jnp.pad(x, ((0, 0), (k - 1, 0), (0, 0)))
            y = sum((xp[:, i:i + s, :] * w[:, i] for i in range(k)))
            return y + bconv
        b, s, _ = x.shape
        residual = x
        h = x * jax.lax.rsqrt(jnp.mean(x * x, axis=-1, keepdims=True) + EPS) * norm_w
        proj = jnp.einsum('bsd,od->bso', h, in_proj_w)
        gate = proj[..., :D_INNER]
        hBC = proj[..., D_INNER:D_INNER + CONV_DIM]
        dt = proj[..., D_INNER + CONV_DIM:]
        hBC = jax.nn.silu(causal_conv(hBC, conv_w, conv_b))
        hid = hBC[..., :D_INNER].reshape(b, s, H_M, P_M)
        B = hBC[..., D_INNER:D_INNER + G_M * N_M].reshape(b, s, G_M, N_M)
        C = hBC[..., D_INNER + G_M * N_M:].reshape(b, s, G_M, N_M)
        dt = jax.nn.softplus(dt + dt_bias)
        A = -jnp.exp(A_log)
        pad = -s % CHUNK
        D_res = Dp[None, None, :, None] * hid
        hid_dt = hid * dt[..., None]
        A_full = A[None, None, :] * dt

        def padseq(t):
            return jnp.pad(t, [(0, 0), (0, pad)] + [(0, 0)] * (t.ndim - 2))
        hid_dt, A_full, Bp, Cp = (padseq(hid_dt), padseq(A_full), padseq(B), padseq(C))
        S = s + pad
        c, l = (S // CHUNK, CHUNK)
        hc = hid_dt.reshape(b, c, l, H_M, P_M)
        Ac = A_full.reshape(b, c, l, H_M).transpose(0, 3, 1, 2)
        rep = H_M // G_M
        Bh = jnp.repeat(Bp.reshape(b, c, l, G_M, N_M), rep, axis=3)
        Ch = jnp.repeat(Cp.reshape(b, c, l, G_M, N_M), rep, axis=3)
        A_cs = jnp.cumsum(Ac, axis=-1)
        L = jnp.exp(segsum(Ac))
        M = jnp.einsum('bcihn,bcjhn->bcijh', Ch, Bh) * jnp.transpose(L, (0, 2, 3, 4, 1))
        Y_diag = jnp.einsum('bcijh,bcjhp->bcihp', M, hc)
        decay_states = jnp.exp(A_cs[..., -1:] - A_cs)
        states = jnp.einsum('bclhn,bhcl,bclhp->bchpn', Bh, decay_states, hc)
        A_last = jnp.pad(A_cs[..., -1], ((0, 0), (0, 0), (1, 0)))
        decay_chunk = jnp.exp(segsum(A_last))
        states_cat = jnp.concatenate([jnp.zeros_like(states[:, :1]), states], axis=1)
        prev_states = jnp.einsum('bhij,bjhpn->bihpn', decay_chunk, states_cat)[:, :-1]
        Y_off = jnp.einsum('bclhn,bchpn,bhcl->bclhp', Ch, prev_states, jnp.exp(A_cs))
        y = (Y_diag + Y_off).reshape(b, S, H_M, P_M)[:, :s] + D_res
        y = y.reshape(b, s, D_INNER)
        yg = y * jax.nn.silu(gate)
        gsz = D_INNER // G_M
        ygr = yg.reshape(b, s, G_M, gsz)
        ygr = ygr * jax.lax.rsqrt(jnp.mean(ygr * ygr, axis=-1, keepdims=True) + EPS)
        y = ygr.reshape(b, s, D_INNER) * gnorm_w
        out = jnp.einsum('bsd,od->bso', y, out_proj_w)
        return residual + out

    def _L1_ffn_ref(x, w1, w1_scale, w3, w3_scale, w2, w2_scale):
        import jax, jax.numpy as jnp
        import numpy as np
        BS = 128
        FP8_MAX = 448.0

        def act_quant(x):
            T, K = x.shape
            xb = x.reshape(T, K // BS, BS)
            amax = jnp.max(jnp.abs(xb), axis=-1)
            scale = amax / FP8_MAX + 1e-12
            xq = (xb / scale[:, :, None]).reshape(T, K)
            return (xq, scale)

        def linear_dsv3(x, wq, w_scale):
            T, K = x.shape
            N = wq.shape[0]
            xq, xs = act_quant(x)
            xdq = (xq.reshape(T, K // BS, BS) * xs[:, :, None]).reshape(T, K)
            wdq = (wq.reshape(N // BS, BS, K // BS, BS) * w_scale[:, None, :, None]).reshape(N, K)
            return xdq @ wdq.T
        B, S, D = x.shape
        xf = x.reshape(-1, D)
        g = linear_dsv3(xf, w1, w1_scale)
        u = linear_dsv3(xf, w3, w3_scale)
        h = jax.nn.silu(g) * u
        y = linear_dsv3(h, w2, w2_scale)
        return y.reshape(B, S, D)
    x = L0_attn_hidden_states
    x = x + _layernorm(_L0_attn_ref(_layernorm(x, axis=-1), L0_attn_in_proj_w, L0_attn_conv_w, L0_attn_conv_b, L0_attn_x_proj_w, L0_attn_dt_proj_w, L0_attn_dt_bias, L0_attn_A_log, L0_attn_D_param, L0_attn_out_proj_w, L0_attn_dt_ln_w, L0_attn_B_ln_w, L0_attn_C_ln_w), axis=-1)
    x = x + _layernorm(_L0_ffn_ref(_layernorm(x, axis=-1), L0_ffn_W_base, L0_ffn_b_base, L0_ffn_W_gate, L0_ffn_W_thr, L0_ffn_b_thr, L0_ffn_A_w, L0_ffn_B_w), axis=-1)
    x = x + _layernorm(_L1_attn_ref(_layernorm(x, axis=-1), L1_attn_norm_w, L1_attn_in_proj_w, L1_attn_conv_w, L1_attn_conv_b, L1_attn_dt_bias, L1_attn_A_log, L1_attn_Dp, L1_attn_gnorm_w, L1_attn_out_proj_w), axis=-1)
    x = x + _layernorm(_L1_ffn_ref(_layernorm(x, axis=-1), L1_ffn_w1, L1_ffn_w1_scale, L1_ffn_w3, L1_ffn_w3_scale, L1_ffn_w2, L1_ffn_w2_scale), axis=-1)
    return x

_drawn_inputs = setup_inputs


def setup_inputs(seed=0):
    import zlib

    import numpy as np

    out = dict(_drawn_inputs(seed))
    spreads = {'L0_attn_D_param': (1.0, 0.2),
     'L0_attn_dt_ln_w': (1.0, 0.6),
     'L0_attn_B_ln_w': (1.0, 0.2),
     'L0_attn_C_ln_w': (1.0, 0.2),
     'L1_attn_norm_w': (1.0, 0.2),
     'L1_attn_conv_b': (0.0, 0.1),
     'L1_attn_Dp': (1.0, 0.2),
     'L1_attn_gnorm_w': (1.0, 0.2)}
    factors = {'L0_ffn_b_base': 6.799,
     'L1_attn_dt_bias': 8.0,
     'L1_attn_A_log': 8.0,
     'L1_ffn_w2_scale': 2.773}
    for name, (base, spread) in spreads.items():
        noise = np.random.default_rng([zlib.crc32(name.encode()), seed]).standard_normal(out[name].shape)
        drawn = base * np.exp(spread * noise) if base else spread * noise
        out[name] = jnp.asarray(drawn.astype(out[name].dtype))
    for name, factor in factors.items():
        out[name] = (out[name] * factor).astype(out[name].dtype)
    return out
```

```python
from contextlib import ExitStack

import concourse.bass as bass
from concourse import mybir

F32 = mybir.dt.float32
F32R = mybir.dt.float32r
ALU = mybir.AluOpType
ACT = mybir.ActivationFunctionType
AX_X = mybir.AxisListType.X

P = 128
BATCH, SEQ, DM = 4, 256, 512
TOK = BATCH * SEQ
MT = TOK // P
KD = DM // P
HALF = 512
NH = TOK // HALF
BPH = HALF // SEQ
LN_EPS = 1e-5

DIN, NST, RNK, TAPS = 1024, 16, 32, 4
CD = DIN // P
NX = RNK + 2 * NST
SCAN_EPS = 1e-6
NE, ER = 8, 16
MAX_THR, MOE_SCALE = 0.125, 2.0
GW = NE + 2
NHEAD, HP, NG, NS = 128, 64, 8, 128
DI1 = NHEAD * HP
PAIRS = DI1 // P // NG
GRP = DI1 // NG
MIX_EPS = 1e-5
INTER, QB, FP8_MAX, Q_EPS = 1792, 128, 448.0, 1e-12
FC = INTER // (2 * QB)

C_ID, C_MASK, C_BLK, C_INV, C_ONE = 0, 128, 384, 448, 449
C_N = 450


class Chain:

    def __init__(self, eng, sem, base=0):
        self.eng, self.sem, self.base, self.n = eng, sem, base, 0

    def mark(self, ins):
        self.n += 1
        ins.then_inc(self.sem, 1)
        return self.n

    def wait(self, n=None):
        self.eng.wait_ge(self.sem, self.base + (self.n if n is None else n))

    def link(self, ins):
        self.mark(ins)
        self.wait()


def mm3(pe, out, lhs, rhs, start, stop):
    pe.matmul(out, lhs[0], rhs[0], start=start, stop=False)
    pe.matmul(out, lhs[0], rhs[1], start=False, stop=False)
    return pe.matmul(out, lhs[1], rhs[0], start=False, stop=stop)


def build(nc, I, out):
    with ExitStack() as top:
        sems = {}

        def sem(name):
            if name not in sems:
                sems[name] = top.enter_context(nc.semaphore(name))
            return sems[name]

        def scope():
            return ExitStack()

        def sb(ctx, name, shape, dt=F32):
            return ctx.enter_context(nc.sbuf_tensor(name, shape, dt))

        def banks(ctx, name, n):
            return [ctx.enter_context(nc.psum_tensor(f"{name}{i}", [P, HALF], F32)) for i in range(n)]

        x_tok = I["x"].rearrange("(m p) d -> p m d", p=P)
        out_tok = out.rearrange("(m p) d -> p m d", p=P)
        bc_dram = nc.dram_tensor("bc_rows", [2 * NST, TOK], F32, kind="Internal").ap()
        acs_dram = nc.dram_tensor("acs_rows", [2, NHEAD, TOK], F32, kind="Internal").ap()
        x_dram = nc.dram_tensor("x_kept", [TOK, DM], F32, kind="Internal").ap().rearrange("(m p) d -> p m d", p=P)

        cst = sb(top, "cst", [P, C_N])
        eps = sb(top, "eps", [P, 4])
        ident = cst[:, C_ID:C_ID + P]
        ones_col = cst[:, C_ONE:C_ONE + 1]
        s_cst, s_eps = sem("cst_in"), sem("eps_set")

        def norm_stage(tag, x, o, load_x, xT, rms, keep, quant=False):
            with scope() as c:
                h = keep if keep is not None else sb(c, tag + "h", [P, MT, DM])
                h2 = sb(c, tag + "h2", [P, MT, DM]) if rms else h
                st = sb(c, tag + "st", [P, MT, 6])
                mv = sb(c, tag + "mv", [P, MT, 2])
                sd = sb(c, tag + "sd", [P, MT])
                rs = sb(c, tag + "rs", [P, MT])
                qa = sb(c, tag + "qa", [P, MT, KD])
                qs = sb(c, tag + "qs", [P, MT, KD])
                qr = sb(c, tag + "qr", [P, MT, KD])
                sq = sb(c, tag + "sq", [P, DM])
                nw = sb(c, tag + "nw", [P, KD])
                tb = banks(c, tag + "tb", MT)
                s_chain, s_var, s_sd, s_h = sem(tag + "dve"), sem(tag + "var"), sem(tag + "sd"), sem(tag + "h_ready")
                s_x = sem(tag + "x_in") if load_x or rms else None
                s_keep = sem(tag + "kept") if rms or xT is None else None
                s_xr = sem(tag + "x_ready") if rms else None
                s_t, s_hi, s_lo = ((sem(tag + "turned"), sem(tag + "hi"), sem(tag + "lo")) if xT is not None
                                   else (None, None, None))
                rounds = (1 if o is not None else 0) + (1 if xT is not None else 0)

                with nc.Block() as block:
                    @block.sync
                    def _(sp):
                        if load_x:
                            for m in range(MT):
                                sp.dma_start(x[:, m, :], x_tok[:, m, :]).then_inc(s_x, 16)
                        if rms:
                            sp.dma_start(nw[:], I["norm_w1"]).then_inc(s_x, 16)
                            sp.wait_ge(s_xr, 1)
                            sp.dma_start(x_dram, x[:]).then_inc(s_keep, 16)
                            sp.wait_ge(s_keep, 16)
                        if xT is None:
                            for m in range(MT):
                                sp.wait_ge(s_h, m + 1)
                                sp.dma_start(out_tok[:, m, :], x[:, m, :]).then_inc(s_keep, 16)
                            sp.wait_ge(s_keep, 16 * MT)

                    @block.vector
                    def _(dve):
                        ch = Chain(dve, s_chain)

                        def normalise(src, dst, n, last=None):
                            for m in range(MT):
                                if n == 0 and load_x:
                                    dve.wait_ge(s_x, 16 * MT)
                                ch.mark(dve.bn_stats(st[:, m, :], src[:, m, :]))
                            ch.wait()
                            for m in range(MT):
                                i = dve.bn_aggr(mv[:, m, :], st[:, m, :])
                                ch.mark(i) if m < MT - 1 else i.then_inc(s_var, 1)
                            dve.wait_ge(s_sd, n + 1)
                            ch.link(dve.reciprocal(rs[:], sd[:]))
                            for m in range(MT):
                                i = dve.tensor_scalar(dst[:, m, :], src[:, m, :], mv[:, m, 0:1], rs[:, m:m + 1],
                                                      ALU.subtract, ALU.mult)
                                last(i) if last else ch.mark(i)
                            if not last:
                                ch.wait()

                        n = 0
                        if o is not None:
                            normalise(o, o, 0)
                            n = 1
                            if load_x:
                                dve.wait_ge(s_x, 16 * MT)
                            for m in range(MT):
                                i = dve.tensor_tensor(x[:, m, :], x[:, m, :], o[:, m, :], ALU.add)
                                if xT is None:
                                    i.then_inc(s_h, 1)
                                else:
                                    ch.mark(i)
                            if xT is None:
                                return
                            ch.wait()
                            if rms:
                                dve.engine_nop().then_inc(s_xr, 1)
                        direct = not rms and not quant
                        normalise(x, h, n, (lambda i: i.then_inc(s_h, 1)) if direct else None)
                        if rms:
                            for m in range(MT):
                                dve.tensor_tensor_reduce(sq[:], h[:, m, :], h[:, m, :], 1.0, 0.0, ALU.mult,
                                                         ALU.add, mv[:, m, 0:1]).then_inc(s_chain, 1)
                                ch.n += 1
                                ch.wait()
                            dve.tensor_copy(qs[:, :, 0], mv[:, :, 0]).then_inc(s_var, 1)
                            dve.wait_ge(s_sd, n + 2)
                            ch.link(dve.reciprocal(rs[:], sd[:]))
                            for m in range(MT):
                                dve.tensor_scalar(h2[:, m, :], h[:, m, :], rs[:, m:m + 1], None,
                                                  ALU.mult).then_inc(s_h, 1)
                            dve.wait_ge(s_x, 16 * ((MT if load_x else 0) + 1))
                        if quant:
                            hq = h[:].rearrange("p m (b k) -> p (m b) k", k=QB)
                            fl = lambda a: a[:].rearrange("p m b -> p (m b)")
                            ch.link(dve.tensor_reduce(fl(qa), hq, AX_X, ALU.max, apply_absolute_value=True))
                            ch.link(dve.tensor_scalar(fl(qs), fl(qa), 1.0 / FP8_MAX, Q_EPS, ALU.mult, ALU.add))
                            ch.link(dve.reciprocal(fl(qr), fl(qs)))
                            for m in range(MT):
                                for b in range(KD):
                                    i = dve.tensor_scalar(h[:, m, b * QB:(b + 1) * QB], h[:, m, b * QB:(b + 1) * QB],
                                                          qr[:, m, b:b + 1], qs[:, m, b:b + 1], ALU.mult, ALU.mult)
                                i.then_inc(s_h, 1)
                        for m in range(MT):
                            dve.wait_ge(s_hi, m + 1)
                            src = tb[m][:].rearrange("p (k t) -> p k t", k=KD)
                            hi = xT[0][:, :, m * P:(m + 1) * P]
                            lo = xT[1][:, :, m * P:(m + 1) * P]
                            if rms:
                                for k in range(KD):
                                    i = dve.scalar_tensor_tensor(
                                        out=lo[:, k, :], in0=src[:, k, :], scalar=nw[:, k:k + 1],
                                        in1=hi[:, k, :].bitcast(F32), op0=ALU.mult, op1=ALU.subtract)
                            else:
                                i = dve.tensor_tensor(lo, src, hi.bitcast(F32), ALU.subtract)
                            i.then_inc(s_lo, 1)

                    @block.scalar
                    def _(act):
                        for n in range(rounds):
                            act.wait_ge(s_var, n + 1)
                            act.activation(sd[:], mv[:, :, 1], ACT.Sqrt, bias=eps[:, 0:1]).then_inc(s_sd, 1)
                        if rms:
                            act.wait_ge(s_var, rounds + 1)
                            act.activation(sd[:], qs[:, :, 0], ACT.Sqrt, bias=eps[:, 2:3],
                                           scale=1.0 / DM).then_inc(s_sd, 1)
                            act.wait_ge(s_x, 16 * ((MT if load_x else 0) + 1))
                        if xT is None:
                            return
                        for m in range(MT):
                            act.wait_ge(s_t, m + 1)
                            src = tb[m][:].rearrange("p (k t) -> p k t", k=KD)
                            hi = xT[0][:, :, m * P:(m + 1) * P]
                            if rms:
                                for k in range(KD):
                                    i = act.activation(hi[:, k, :], src[:, k, :], ACT.Copy, scale=nw[:, k:k + 1])
                            else:
                                i = act.activation(hi, src, ACT.Copy)
                            i.then_inc(s_hi, 1)

                    @block.tensor
                    def _(pe):
                        if xT is None:
                            return
                        for m in range(MT):
                            pe.wait_ge(s_h, m + 1)
                            for k in range(KD):
                                i = pe.transpose(tb[m][:, k * P:(k + 1) * P], h2[:, m, k * P:(k + 1) * P], ident)
                            i.then_inc(s_t, 1)

        with nc.Block() as block:
            @block.sync
            def _(sp):
                sp.dma_start(cst[:], I["consts"]).then_inc(s_cst, 16)
                sp.wait_ge(s_cst, 16)

            @block.vector
            def _(dve):
                for i, v in enumerate((LN_EPS, SCAN_EPS, MIX_EPS, 1.0)):
                    dve.memset(eps[:, i:i + 1], v).then_inc(s_eps, 1)
                dve.wait_ge(s_eps, 4)

        with scope() as c0:
            xc = sb(c0, "xc", [P, CD, TOK])
            with scope() as c1:
                sz = sb(c1, "sz", [P, CD, TOK])
                dt = sb(c1, "dt", [P, CD, TOK])
                with scope() as c2:
                    xT = (sb(c2, "xTh", [P, KD, TOK], F32R), sb(c2, "xTl", [P, KD, TOK], F32R))
                    with scope() as c3:
                        x = sb(c3, "x0", [P, MT, DM])
                        norm_stage("n0_", x, None, True, xT, False, None)
                    scan_in_proj(nc, sem, sb, banks, I, xT, xc, sz)
                scan_params(nc, sem, sb, banks, I, xc, dt, cst, eps, bc_dram)
                selective_scan(nc, sem, sb, banks, I, xc, dt, sz, ident, bc_dram)
            with scope() as c2:
                x = sb(c2, "x1", [P, MT, DM])
                o = sb(c2, "o1", [P, MT, DM])
                scan_out_proj(nc, sem, sb, banks, I, xc, o)
                xT = (sb(c2, "xT1h", [P, KD, TOK], F32R), sb(c2, "xT1l", [P, KD, TOK], F32R))
                norm_stage("n1_", x, o, True, xT, False, None)
                experts(nc, sem, sb, banks, I, xT, o, ident)
                s_move = sem("moved")
                o_dram = nc.dram_tensor("o_kept", [TOK, DM], F32, kind="Internal").ap().rearrange(
                    "(m p) d -> p m d", p=P)
                with nc.Block() as block:
                    @block.sync
                    def _(sp):
                        sp.dma_start(x_dram, x[:]).then_inc(s_move, 16)
                        sp.dma_start(o_dram, o[:]).then_inc(s_move, 16)
                        sp.wait_ge(s_move, 32)
        with scope() as c0:
            acc = sb(c0, "acc", [P, MT, DM])
            with scope() as c1:
                xT = (sb(c1, "xT2h", [P, KD, TOK], F32R), sb(c1, "xT2l", [P, KD, TOK], F32R))
                with scope() as c2:
                    x = sb(c2, "x2", [P, MT, DM])
                    o = sb(c2, "o2", [P, MT, DM])
                    with nc.Block() as block:
                        @block.sync
                        def _(sp):
                            sp.dma_start(x[:], x_dram).then_inc(s_move, 16)
                            sp.dma_start(o[:], o_dram).then_inc(s_move, 16)
                            sp.wait_ge(s_move, 64)
                    norm_stage("n2_", x, o, False, xT, True, acc)
                mixer(nc, sem, sb, banks, I, xT, acc, cst, eps, acs_dram)
            with scope() as c1:
                x = sb(c1, "x3", [P, MT, DM])
                with nc.Block() as block:
                    @block.sync
                    def _(sp):
                        sp.dma_start(x[:], x_dram).then_inc(s_move, 16)
                        sp.wait_ge(s_move, 80)
                xT = (sb(c1, "xT3h", [P, KD, TOK], F32R), sb(c1, "xT3l", [P, KD, TOK], F32R))
                norm_stage("n3_", x, acc, False, xT, False, None, quant=True)
                o = sb(c1, "o3", [P, MT, DM])
                ffn(nc, sem, sb, banks, I, xT, o, ident)
                norm_stage("n4_", x, o, False, None, False, None)


def conv_half(dve, ch, cv, src, w, b):
    c3 = cv.rearrange("p (b t) -> p b t", t=SEQ)
    s3 = src.rearrange("p (b t) -> p b t", t=SEQ)
    ch.link(dve.tensor_scalar(cv, src, w[:, TAPS - 1:TAPS], b, ALU.mult, ALU.add))
    for s in range(1, TAPS):
        i = dve.scalar_tensor_tensor(out=c3[:, :, s:], in0=s3[:, :, :SEQ - s], scalar=w[:, TAPS - 1 - s:TAPS - s],
                                     in1=c3[:, :, s:], op0=ALU.mult, op1=ALU.add)
        if s < TAPS - 1:
            ch.link(i)
    return i


def rows3(ap):
    return ap.rearrange("a p k n -> (a p) k n")


def scan_in_proj(nc, sem, sb, banks, I, xT, xc, sz):
    with ExitStack() as c:
        ws = [sb(c, f"ip_ws{i}", [P, KD, 2 * P]) for i in range(2)]
        wh = [sb(c, f"ip_wh{i}", [P, KD, 2 * P], F32R) for i in range(2)]
        wl = [sb(c, f"ip_wl{i}", [P, KD, 2 * P], F32R) for i in range(2)]
        cw = sb(c, "ip_cw", [P, CD, TAPS])
        cb = sb(c, "ip_cb", [P, CD])
        cv = [sb(c, f"ip_cv{i}", [P, HALF]) for i in range(NH)]
        pb = banks(c, "ip_pb", 8)
        s_tab, s_w = sem("ip_tab"), [sem("ip_w0"), sem("ip_w1")]
        s_hi, s_lo, s_proj, s_gate = sem("ip_hi"), sem("ip_lo"), sem("ip_proj"), sem("pool_gate")
        s_cv, s_sx, s_sz, s_ch = sem("ip_conv"), sem("ip_silu_x"), sem("ip_silu_z"), sem("ip_dve")
        links = TAPS - 1
        with nc.Block() as block:
            @block.sync
            def _(sp):
                sp.dma_start(cw[:], I["conv_w0"]).then_inc(s_tab, 16)
                sp.dma_start(cb[:], I["conv_b0"]).then_inc(s_tab, 16)
                with sp.Fori(0, CD // 2) as i:
                    for q in range(2):
                        sp.wait_ge(s_lo, i * 2 + (q + 1))
                        sp.dma_start(ws[q][:], rows3(I["w_in0"][bass.ds(i * 2 + q, 1)])).then_inc(s_w[q], 16)

            @block.gpsimd
            def _(pool):
                pool.sem_inc(s_lo, 2)
                with pool.Fori(0, CD // 2) as i:
                    for q in range(2):
                        pool.wait_ge(s_w[q], i * 16 + 16)
                        pool.wait_ge(s_proj, i * 8 + (4 * q + 4))
                        pool.sem_inc(s_gate, 1)
                        pool.tensor_scalar(wh[q][:], ws[q][:], 1.0, 0.0, ALU.mult, ALU.add).then_inc(s_hi, 1)

                        pool.wait_ge(s_hi, i * 2 + (q + 1))
                        pool.tensor_tensor(wl[q][:], ws[q][:], wh[q][:].bitcast(F32), ALU.subtract
                                           ).then_inc(s_lo, 1)

            @block.tensor
            def _(pe):
                pe.sem_inc(s_proj, 8)
                with pe.Fori(0, CD // 2) as i:
                    for q in range(2):
                        pe.wait_ge(s_lo, i * 2 + (q + 3))
                        for j in range(4):
                            pe.wait_ge(s_cv if j < 2 else s_sz, i * 4 + (2 * q + j % 2 + 1))
                            n0 = P * (j // 2)
                            t0 = HALF * (j % 2)
                            for k in range(KD):
                                last = mm3(pe, pb[4 * q + j][:],
                                           (wh[q][:, k, n0:n0 + P], wl[q][:, k, n0:n0 + P]),
                                           (xT[0][:, k, t0:t0 + HALF], xT[1][:, k, t0:t0 + HALF]),
                                           k == 0, k == KD - 1)
                            last.then_inc(s_proj, 1)

            @block.vector
            def _(dve):
                dve.sem_inc(s_cv, 4)
                dve.wait_ge(s_tab, 32)
                with dve.Fori(0, CD // 2) as i:
                    ch = Chain(dve, s_ch, i * (4 * links))
                    for q in range(2):
                        for j in range(2):
                            dve.wait_ge(s_proj, i * 8 + (4 * q + j + 9))
                            dve.wait_ge(s_sx, i * 4 + (2 * q + j + 1))
                            conv_half(dve, ch, cv[j][:], pb[4 * q + j][:],
                                      cw[:, bass.ds(i * 2 + q, 1), :].rearrange("p a k -> p (a k)"),
                                      cb[:, bass.ds(i * 2 + q, 1)]).then_inc(s_cv, 1)

            @block.scalar
            def _(act):
                act.sem_inc(s_sx, 2)
                act.sem_inc(s_sz, 4)
                with act.Fori(0, CD // 2) as i:
                    for q in range(2):
                        for j in range(2):
                            act.wait_ge(s_cv, i * 4 + (2 * q + j + 5))
                            act.wait_ge(s_tab, 32)
                            act.activation(xc[:, bass.ds(i * 2 + q, 1), j * HALF:(j + 1) * HALF],
                                           cv[j][:].unsqueeze(1), ACT.Silu).then_inc(s_sx, 1)
                        for j in range(2):
                            act.wait_ge(s_proj, i * 8 + (4 * q + j + 11))
                            act.wait_ge(s_tab, 32)
                            act.activation(sz[:, bass.ds(i * 2 + q, 1), j * HALF:(j + 1) * HALF],
                                           pb[4 * q + 2 + j][:].unsqueeze(1), ACT.Silu).then_inc(s_sz, 1)


def scan_params(nc, sem, sb, banks, I, xc, dt, cst, eps, bc_dram):
    with ExitStack() as c:
        R = RNK + 2 * NST
        xp = sb(c, "sp_xp", [P, CD, R])
        dp = sb(c, "sp_dp", [RNK, DIN])
        db = sb(c, "sp_db", [P, CD])
        lw = sb(c, "sp_lw", [R, 1])
        p0 = sb(c, "sp_p0", [R, TOK])
        sq = sb(c, "sp_sq", [R, TOK])
        sd = sb(c, "sp_sd", [R, TOK])
        rs = sb(c, "sp_rs", [R, TOK])
        bcn = sb(c, "sp_bcn", [R, TOK])
        rl = sb(c, "sp_rl", [P, CD, TOK])
        pp = banks(c, "sp_pp", 2)
        pq = banks(c, "sp_pq", 2)
        pd = banks(c, "sp_pd", 4)
        s_in, s_pp, s_cp, s_sq, s_ss = sem("sp_in"), sem("sp_proj"), sem("sp_copied"), sem("sp_sq"), sem("sp_sums")
        s_sd, s_rs, s_bcn, s_out = sem("sp_sd"), sem("sp_rs"), sem("sp_normed"), sem("sp_bc_out")
        s_pd, s_act, s_ln, s_dt = sem("sp_dtproj"), sem("sp_act"), sem("sp_ln"), sem("sp_dt")
        with nc.Block() as block:
            @block.sync
            def _(sp):
                for t, n in ((xp, "x_proj"), (dp, "dt_proj"), (db, "dt_bias0"), (lw, "ln_w0")):
                    sp.dma_start(t[:], I[n]).then_inc(s_in, 16)
                sp.wait_ge(s_bcn, 2)
                sp.dma_start(bc_dram, bcn[RNK:R, :]).then_inc(s_out, 16)
                sp.wait_ge(s_out, 16)

            @block.tensor
            def _(pe):
                pe.wait_ge(s_in, 64)
                for h in range(NH):
                    for k in range(CD):
                        i = pe.matmul(pp[h][0:R, :], xp[:, k, :], xc[:, k, h * HALF:(h + 1) * HALF],
                                      start=k == 0, stop=k == CD - 1)
                    i.then_inc(s_pp, 1)
                for h in range(NH):
                    pe.wait_ge(s_sq, h + 1)
                    pe.matmul(pq[h][0:R, :], cst[0:R, C_BLK:C_BLK + R], sq[:, h * HALF:(h + 1) * HALF],
                              start=True, stop=True).then_inc(s_ss, 1)
                pe.wait_ge(s_bcn, 2)
                for k in range(CD):
                    for h in range(NH):
                        n = 2 * k + h
                        if n >= 4:
                            pe.wait_ge(s_act, 2 * (n - 3))
                        pe.matmul(pd[n % 4][:], dp[:, k * P:(k + 1) * P], bcn[0:RNK, h * HALF:(h + 1) * HALF],
                                  start=True, stop=True).then_inc(s_pd, 1)

            @block.vector
            def _(dve):
                for h in range(NH):
                    dve.wait_ge(s_pp, h + 1)
                    dve.tensor_copy(p0[:, h * HALF:(h + 1) * HALF], pp[h][0:R, :]).then_inc(s_cp, 1)
                for h in range(NH):
                    t = slice(h * HALF, (h + 1) * HALF)
                    dve.wait_ge(s_sd, h + 1)
                    dve.reciprocal(rs[:, t], sd[:, t]).then_inc(s_rs, 1)
                    dve.wait_ge(s_rs, h + 1)
                    dve.scalar_tensor_tensor(out=bcn[:, t], in0=p0[:, t], scalar=lw[:, 0:1], in1=rs[:, t],
                                             op0=ALU.mult, op1=ALU.mult).then_inc(s_bcn, 1)
                for k in range(CD):
                    dve.wait_ge(s_ln, k + 1)
                    dve.tensor_tensor(dt[:, k, :], dt[:, k, :], rl[:, k, :], ALU.add).then_inc(s_dt, 1)
                dve.wait_ge(s_dt, CD)

            @block.scalar
            def _(act):
                for h in range(NH):
                    t = slice(h * HALF, (h + 1) * HALF)
                    act.wait_ge(s_cp, h + 1)
                    act.activation(sq[:, t], p0[:, t], ACT.Square).then_inc(s_sq, 1)
                act.wait_ge(s_in, 64)
                for h in range(NH):
                    t = slice(h * HALF, (h + 1) * HALF)
                    act.wait_ge(s_ss, h + 1)
                    act.activation(sd[:, t], pq[h][0:R, :], ACT.Sqrt, bias=eps[0:R, 1:2],
                                   scale=cst[0:R, C_INV:C_INV + 1]).then_inc(s_sd, 1)
                for k in range(CD):
                    for h in range(NH):
                        t = slice(h * HALF, (h + 1) * HALF)
                        n = 2 * k + h
                        act.wait_ge(s_pd, n + 1)
                        act.activation(dt[:, k, t], pd[n % 4][:], ACT.Abs, bias=db[:, k:k + 1]).then_inc(s_act, 1)
                        act.activation(rl[:, k, t], pd[n % 4][:], ACT.Relu, bias=db[:, k:k + 1]).then_inc(s_act, 1)
                act.wait_ge(s_act, 4 * CD)
                for k in range(CD):
                    act.activation(dt[:, k, :], dt[:, k, :], ACT.Exp, scale=-1.0).then_inc(s_act, 1)
                for k in range(CD):
                    act.wait_ge(s_act, 4 * CD + k + 1)
                    act.activation(dt[:, k, :], dt[:, k, :], ACT.Ln, bias=eps[:, 3:4]).then_inc(s_ln, 1)


def selective_scan(nc, sem, sb, banks, I, xc, dt, sz, ident, bc_dram):
    RA, RB = 4, 2
    with ExitStack() as c:
        bcb = sb(c, "ss_bc", [P, 2 * NST, HALF])
        al = sb(c, "ss_al", [P, CD, NST])
        na = sb(c, "ss_na", [P, CD, NST])
        dd = sb(c, "ss_d", [P, CD])
        dbx = [sb(c, f"ss_dbx{i}", [P, HALF]) for i in range(RB)]
        hh = [sb(c, f"ss_h{i}", [P, HALF]) for i in range(RB)]
        pr = [sb(c, f"ss_pr{i}", [P, HALF]) for i in range(RB)]
        da = banks(c, "ss_da", RA)
        u, = banks(c, "ss_u", 1)
        yb, = banks(c, "ss_y", 1)
        s_in, s_bc = sem("ss_in"), sem("ss_bc_in")
        s_a, s_z, s_da, s_u, s_dbx, s_h = (sem("ss_a"), sem("ss_zero"), sem("ss_decay"), sem("ss_u_ready"),
                                           sem("ss_dbx_ready"), sem("ss_h_ready"))
        s_pr, s_y, s_y1, s_fin = sem("ss_prod"), sem("ss_summed"), sem("ss_y1"), sem("ss_done")
        UH = CD * NST
        with nc.Block() as block:
            @block.sync
            def _(sp):
                sp.dma_start(al[:], I["a_log0"]).then_inc(s_in, 16)
                sp.dma_start(dd[:], I["d_0"]).then_inc(s_in, 16)
                for half in range(NH):
                    if half:
                        sp.wait_ge(s_pr, RB + UH)
                        sp.wait_ge(s_h, RA + UH)
                    for r in range(0, 2 * NST, 8):
                        src = bc_dram[r:r + 8, half * HALF:(half + 1) * HALF]
                        sp.dma_start(bcb[:, r:r + 8, :], src.partition_broadcast(P)).then_inc(s_bc, 16)

            @block.scalar
            def _(act):
                act.wait_ge(s_in, 32)
                act.activation(al[:], al[:], ACT.Exp).then_inc(s_a, 1)
                act.wait_ge(s_a, 1)
                act.activation(na[:], al[:], ACT.Copy, scale=-1.0).then_inc(s_a, 1)
                act.wait_ge(s_a, 2)
                act.wait_ge(s_z, RA)
                for half in range(NH):
                    with act.Fori(0, CD) as k:
                        for n in range(NST):
                            act.wait_ge(s_h, k * NST + (half * UH + n + 1))
                            act.wait_ge(s_in, 32)
                            src = dt[:, bass.ds(k, 1), half * HALF:(half + 1) * HALF].rearrange(
                                "p a (b t) -> p (a b) t", t=SEQ)
                            act.activation(da[n % RA][:].rearrange("p (b t) -> p b t", t=SEQ)[:, :, 1:],
                                           src[:, :, 1:], ACT.Exp,
                                           scale=na[:, bass.ds(k, 1), n:n + 1].rearrange("p a n -> p (a n)")
                                           ).then_inc(s_da, 1)

            @block.vector
            def _(dve):
                dve.sem_inc(s_h, RA)
                dve.sem_inc(s_fin, 1)
                for i in range(RA):
                    dve.memset(da[i][:].rearrange("p (b t) -> p b t", t=SEQ)[:, :, 0:1], 0.0).then_inc(s_z, 1)
                dve.wait_ge(s_in, 32)
                for half in range(NH):
                    t = slice(half * HALF, (half + 1) * HALF)
                    dve.wait_ge(s_bc, 64 * (half + 1))
                    with dve.Fori(0, CD) as k:
                        base = k * NST + half * UH

                        def inputs(n):
                            dve.wait_ge(s_h, base + (n + RA - RB + 1))
                            dve.tensor_tensor(dbx[n % RB][:], u[:], bcb[:, n, :], ALU.mult).then_inc(s_dbx, 1)

                        def flat(a):
                            return a[:, bass.ds(k, 1), t].rearrange("p a t -> p (a t)")

                        dve.tensor_tensor(u[:], flat(dt), flat(xc), ALU.mult).then_inc(s_u, 1)
                        dve.wait_ge(s_u, k + (half * CD + 1))
                        inputs(0)
                        for n in range(NST):
                            if n + 1 < NST:
                                inputs(n + 1)
                            dve.wait_ge(s_dbx, base + (n + 1))
                            dve.wait_ge(s_da, base + (n + 1))
                            dve.wait_ge(s_pr, base + (n + 1))
                            dve.tensor_tensor_scan(hh[n % RB][:], da[n % RA][:], dbx[n % RB][:], 0.0,
                                                   ALU.mult, ALU.add).then_inc(s_h, 1)
                        dve.wait_ge(s_y, base + (RB + NST))
                        dve.wait_ge(s_h, base + (RA + NST))
                        dve.scalar_tensor_tensor(out=dbx[0][:], in0=flat(xc), scalar=dd[:, bass.ds(k, 1)],
                                                 in1=yb[:], op0=ALU.mult, op1=ALU.add).then_inc(s_y1, 1)
                        dve.wait_ge(s_y1, k + (half * CD + 1))
                        dve.tensor_tensor(flat(xc), dbx[0][:], flat(sz), ALU.mult).then_inc(s_fin, 1)
                        dve.wait_ge(s_fin, k + (half * CD + 2))

            @block.gpsimd
            def _(pool):
                pool.sem_inc(s_pr, RB)
                for half in range(NH):
                    pool.wait_ge(s_bc, 64 * (half + 1))
                    with pool.Fori(0, CD) as k:
                        base = k * NST + half * UH
                        for n in range(NST):
                            pool.wait_ge(s_h, base + (RA + n + 1))
                            pool.wait_ge(s_y, base + (n + 1))
                            pool.tensor_tensor(pr[n % RB][:], hh[n % RB][:], bcb[:, NST + n, :], ALU.mult
                                               ).then_inc(s_pr, 1)

            @block.tensor
            def _(pe):
                pe.sem_inc(s_y, RB)
                for half in range(NH):
                    with pe.Fori(0, CD) as k:
                        base = k * NST + half * UH
                        pe.wait_ge(s_fin, k + (half * CD + 1))
                        for n in range(NST):
                            pe.wait_ge(s_pr, base + (RB + n + 1))
                            pe.matmul(yb[:], ident, pr[n % RB][:], start=n == 0, stop=n == NST - 1
                                      ).then_inc(s_y, 1)


def scan_out_proj(nc, sem, sb, banks, I, xc, o):
    with ExitStack() as c:
        wo = sb(c, "op_w", [P, CD, DM])
        ob = banks(c, "op_b", 8)
        s_w, s_o, s_c = sem("op_w_in"), sem("op_mm"), sem("op_copied")
        with nc.Block() as block:
            @block.sync
            def _(sp):
                sp.dma_start(wo[:], I["w_out0"]).then_inc(s_w, 16)

            @block.tensor
            def _(pe):
                pe.wait_ge(s_w, 16)
                for m in range(MT):
                    for k in range(CD):
                        i = pe.matmul(ob[m][:], xc[:, k, m * P:(m + 1) * P], wo[:, k, :],
                                      start=k == 0, stop=k == CD - 1)
                    i.then_inc(s_o, 1)

            @block.scalar
            def _(act):
                for m in range(MT):
                    act.wait_ge(s_o, m + 1)
                    act.activation(o[:, m, :], ob[m][:], ACT.Copy).then_inc(s_c, 1)
                act.wait_ge(s_c, MT)


def experts(nc, sem, sb, banks, I, xT, o, ident):
    with ExitStack() as c:
        N2 = NE * ER + GW
        N = DM + N2
        ws = sb(c, "ex_ws", [P, KD, N])
        wh = sb(c, "ex_wh", [P, KD, N], F32R)
        wl = sb(c, "ex_wl", [P, KD, N], F32R)
        bb = sb(c, "ex_bb", [P, DM])
        bt = sb(c, "ex_bt", [P, 1])
        bw = sb(c, "ex_bw", [NE * ER, DM])
        hg = sb(c, "ex_hg", [P, MT, N2])
        mx = sb(c, "ex_mx", [P, MT])
        e = sb(c, "ex_e", [P, MT, NE])
        th = sb(c, "ex_th", [P, MT])
        sm = sb(c, "ex_sm", [P, MT])
        zr = sb(c, "ex_zr", [P, MT])
        hT = sb(c, "ex_hT", [P, TOK])
        pa = banks(c, "ex_pa", 4)
        pb = banks(c, "ex_pb", 4)
        s_w, s_b, s_hi, s_lo = sem("ex_w_in"), sem("ex_b_in"), sem("ex_hi"), sem("ex_lo")
        s_p, s_g, s_ch, s_d, s_e = sem("ex_rank"), sem("ex_copied"), sem("ex_dve"), sem("ex_arg"), sem("ex_exp")
        s_hw, s_t, s_hT, s_base, s_o = (sem("ex_hw"), sem("ex_turned"), sem("ex_hT_ready"), sem("ex_base"),
                                        sem("ex_out"))

        def last(a):
            return a[:].unsqueeze(2)

        with nc.Block() as block:
            @block.sync
            def _(sp):
                sp.dma_start(ws[:], I["w_ex"]).then_inc(s_w, 16)
                sp.dma_start(bb[:], I["b_base"].partition_broadcast(P).rearrange("p a n -> p (a n)")
                             ).then_inc(s_b, 16)
                sp.dma_start(bt[:], I["b_thr"].partition_broadcast(P).rearrange("p a n -> p (a n)")
                             ).then_inc(s_b, 16)
                sp.dma_start(bw[:], I["w_up"]).then_inc(s_b, 16)

            @block.scalar
            def _(act):
                act.wait_ge(s_w, 16)
                for k in range(KD):
                    act.activation(wh[:, k, :], ws[:, k, :], ACT.Copy).then_inc(s_hi, 1)
                act.wait_ge(s_b, 48)
                act.wait_ge(s_d, 1)
                act.activation(th[:], hg[:, :, NE * ER + NE], ACT.Sigmoid, bias=bt[:, 0:1]).then_inc(s_e, 1)
                act.activation(e[:], e[:], ACT.Exp).then_inc(s_e, 1)
                for m in range(MT):
                    act.wait_ge(s_t, m + 1)
                    act.activation(hT[:, m * P:(m + 1) * P], pb[m % 4][:, 0:P], ACT.Copy).then_inc(s_hT, 1)

            @block.tensor
            def _(pe):
                pe.wait_ge(s_lo, KD)
                for m in range(MT):
                    if m >= 4:
                        pe.wait_ge(s_g, m - 3)
                    for k in range(KD):
                        t = slice(m * P, (m + 1) * P)
                        i = mm3(pe, pb[m % 4][:, 0:N2], (xT[0][:, k, t], xT[1][:, k, t]),
                                (wh[:, k, DM:], wl[:, k, DM:]), k == 0, k == KD - 1)
                    i.then_inc(s_p, 1)

                def base(m, stop):
                    t = slice(m * P, (m + 1) * P)
                    for k in range(KD):
                        mm3(pe, pa[m % 4][:], (xT[0][:, k, t], xT[1][:, k, t]),
                            (wh[:, k, 0:DM], wl[:, k, 0:DM]), k == 0, False)

                for m in range(4):
                    base(m, False)
                pe.wait_ge(s_g, MT)
                pe.wait_ge(s_b, 48)
                for m in range(MT):
                    pe.wait_ge(s_hw, m + 1)
                    if m >= 4:
                        pe.wait_ge(s_hT, m - 3)
                    pe.transpose(pb[m % 4][:, 0:P], hg[:, m, 0:NE * ER], ident).then_inc(s_t, 1)
                for m in range(MT):
                    if m >= 4:
                        pe.wait_ge(s_o, m - 3)
                        base(m, False)
                    pe.wait_ge(s_hT, m + 1)
                    pe.matmul(pa[m % 4][:], hT[:, m * P:(m + 1) * P], bw[:], start=False, stop=True
                              ).then_inc(s_base, 1)

            @block.vector
            def _(dve):
                for k in range(KD):
                    dve.wait_ge(s_hi, k + 1)
                    dve.tensor_tensor(wl[:, k, :], ws[:, k, :], wh[:, k, :].bitcast(F32), ALU.subtract
                                      ).then_inc(s_lo, 1)
                for m in range(MT):
                    dve.wait_ge(s_p, m + 1)
                    dve.tensor_copy(hg[:, m, :], pb[m % 4][:, 0:N2]).then_inc(s_g, 1)
                dve.wait_ge(s_g, MT)
                ch = Chain(dve, s_ch)
                g = hg[:, :, NE * ER:NE * ER + NE]
                bc = [P, MT, NE]
                ch.link(dve.tensor_reduce(mx[:], g, AX_X, ALU.max))
                dve.tensor_tensor(e[:], g, last(mx).to_broadcast(bc), ALU.subtract).then_inc(s_d, 1)
                dve.wait_ge(s_e, 2)
                ch.link(dve.tensor_reduce(sm[:], e[:], AX_X, ALU.add))
                ch.mark(dve.tensor_scalar(th[:], th[:], MAX_THR, None, ALU.mult))
                ch.link(dve.reciprocal(sm[:], sm[:]))
                ch.link(dve.tensor_tensor(e[:], e[:], last(sm).to_broadcast(bc), ALU.mult))
                ch.link(dve.tensor_tensor(e[:], e[:], last(th).to_broadcast(bc), ALU.subtract))
                ch.link(dve.tensor_scalar(e[:], e[:], 0.0, None, ALU.max))
                ch.link(dve.tensor_reduce(sm[:], e[:], AX_X, ALU.add))
                ch.link(dve.tensor_scalar(zr[:], sm[:], 0.0, None, ALU.is_equal))
                ch.link(dve.tensor_tensor(sm[:], sm[:], zr[:], ALU.add))
                ch.link(dve.reciprocal(sm[:], sm[:]))
                ch.link(dve.tensor_tensor(e[:], e[:], last(sm).to_broadcast(bc), ALU.mult))
                for m in range(MT):
                    hv = hg[:, m, 0:NE * ER].rearrange("p (e r) -> p e r", r=ER)
                    ev = e[:, m, :].unsqueeze(2).to_broadcast([P, NE, ER])
                    dve.scalar_tensor_tensor(out=hv, in0=hv, scalar=MOE_SCALE, in1=ev, op0=ALU.mult,
                                             op1=ALU.mult).then_inc(s_hw, 1)
                dve.wait_ge(s_b, 48)
                for m in range(MT):
                    dve.wait_ge(s_base, m + 1)
                    dve.tensor_tensor(o[:, m, :], pa[m % 4][:], bb[:], ALU.add).then_inc(s_o, 1)
                dve.wait_ge(s_o, MT)


def mixer(nc, sem, sb, banks, I, xT, acc, cst, eps, acs_dram):
    with ExitStack() as c:
        nacs = sb(c, "mx_nacs", [P, MT, NHEAD])
        dtT = sb(c, "mx_dtT", [P, MT, NHEAD])
        mixer_steps(nc, sem, sb, banks, I, xT, cst, eps, acs_dram, nacs, dtT)
        mixer_groups(nc, sem, sb, banks, I, xT, acc, cst, eps, acs_dram, nacs, dtT)


def mixer_steps(nc, sem, sb, banks, I, xT, cst, eps, acs_dram, nacs, dtT):
    ident = cst[:, C_ID:C_ID + P]
    with ExitStack() as c:
        ws = sb(c, "st_ws", [P, KD, P])
        wh = sb(c, "st_wh", [P, KD, P], F32R)
        wl = sb(c, "st_wl", [P, KD, P], F32R)
        db = sb(c, "st_db", [P, 1])
        al = sb(c, "st_al", [P, 1])
        na = sb(c, "st_na", [P, 1])
        ab = sb(c, "st_ab", [P, TOK])
        rl = sb(c, "st_rl", [P, TOK])
        dt = sb(c, "st_dt", [P, TOK])
        da = sb(c, "st_da", [P, TOK])
        go = sb(c, "st_go", [P, TOK])
        acs = sb(c, "st_acs", [P, TOK])
        ah = sb(c, "st_ah", [P, TOK], F32R)
        alo = sb(c, "st_al_lo", [P, TOK], F32R)
        pd = banks(c, "st_pd", 2)
        pa = banks(c, "st_pa", 2)
        pt = banks(c, "st_pt", 2)
        s_in, s_hi, s_lo, s_p, s_act, s_ch, s_go = (sem("st_in"), sem("st_hi"), sem("st_lo"), sem("st_proj"),
                                                    sem("st_act"), sem("st_dve"), sem("st_go_set"))
        s_dt, s_acs, s_t, s_rows, s_out, s_end = (sem("st_dt_ready"), sem("st_acs_ready"), sem("st_turned"),
                                                  sem("st_rows"), sem("st_rows_out"), sem("st_end"))
        with nc.Block() as block:
            @block.sync
            def _(sp):
                sp.dma_start(ws[:], I["w_dt1"]).then_inc(s_in, 16)
                sp.dma_start(db[:], I["dt_bias1"]).then_inc(s_in, 16)
                sp.dma_start(al[:], I["a_log1"]).then_inc(s_in, 16)
                sp.wait_ge(s_rows, 2)
                sp.dma_start(acs_dram[0], ah[:].bitcast(F32)).then_inc(s_out, 16)
                sp.dma_start(acs_dram[1], alo[:].bitcast(F32)).then_inc(s_out, 16)
                sp.wait_ge(s_out, 32)

            @block.gpsimd
            def _(pool):
                pool.memset(go[:], 1.0).then_inc(s_go, 1)
                pool.wait_ge(s_go, 1)
                pool.memset(go[:].rearrange("p (b t) -> p b t", t=SEQ)[:, :, 0:1], 0.0).then_inc(s_go, 1)

            @block.tensor
            def _(pe):
                pe.wait_ge(s_lo, 1)
                for h in range(NH):
                    t = slice(h * HALF, (h + 1) * HALF)
                    for k in range(KD):
                        i = mm3(pe, pd[h][:], (wh[:, k, :], wl[:, k, :]), (xT[0][:, k, t], xT[1][:, k, t]),
                                k == 0, k == KD - 1)
                    i.then_inc(s_p, 1)
                for src, s_ready, dst in ((dt, s_dt, pt), (acs, s_acs, pa)):
                    pe.wait_ge(s_ready, 1)
                    for m in range(MT):
                        i = pe.transpose(dst[m // 4][:, (m % 4) * P:(m % 4 + 1) * P], src[:, m * P:(m + 1) * P], ident)
                        if m % 4 == 3:
                            i.then_inc(s_t, 1)

            @block.scalar
            def _(act):
                act.wait_ge(s_in, 48)
                act.activation(wh[:], ws[:], ACT.Copy).then_inc(s_hi, 1)
                for h in range(NH):
                    t = slice(h * HALF, (h + 1) * HALF)
                    act.wait_ge(s_p, h + 1)
                    act.activation(ab[:, t], pd[h][:], ACT.Abs, bias=db[:, 0:1]).then_inc(s_act, 1)
                    act.activation(rl[:, t], pd[h][:], ACT.Relu, bias=db[:, 0:1]).then_inc(s_act, 1)
                act.wait_ge(s_act, 4)
                act.activation(ab[:], ab[:], ACT.Exp, scale=-1.0).then_inc(s_act, 1)
                act.activation(al[:], al[:], ACT.Exp).then_inc(s_act, 1)
                act.wait_ge(s_act, 6)
                act.activation(na[:], al[:], ACT.Copy, scale=-1.0).then_inc(s_act, 1)
                act.activation(ab[:], ab[:], ACT.Ln, bias=eps[:, 3:4]).then_inc(s_act, 1)
                for h in range(2):
                    act.wait_ge(s_t, 3 + h)
                    act.activation(nacs[:, 4 * h:4 * h + 4, :], pa[h][:].rearrange("p (m t) -> p m t", t=P),
                                   ACT.Copy, scale=-1.0).then_inc(s_end, 1)
                act.wait_ge(s_end, 2)

            @block.vector
            def _(dve):
                dve.wait_ge(s_in, 48)
                dve.wait_ge(s_hi, 1)
                dve.tensor_tensor(wl[:], ws[:], wh[:].bitcast(F32), ALU.subtract).then_inc(s_lo, 1)
                dve.wait_ge(s_act, 8)
                dve.tensor_tensor(dt[:], ab[:], rl[:], ALU.add).then_inc(s_dt, 1)
                dve.wait_ge(s_dt, 1)
                ch = Chain(dve, s_ch)
                ch.link(dve.tensor_scalar(da[:], dt[:], na[:, 0:1], None, ALU.mult))
                dve.wait_ge(s_go, 2)
                dve.tensor_tensor_scan(acs[:], go[:], da[:], 0.0, ALU.mult, ALU.add).then_inc(s_acs, 1)
                dve.wait_ge(s_acs, 1)
                dve.tensor_copy(ah[:], acs[:]).then_inc(s_rows, 1)
                dve.wait_ge(s_rows, 1)
                dve.tensor_tensor(alo[:], acs[:], ah[:].bitcast(F32), ALU.subtract).then_inc(s_rows, 1)
                for h in range(2):
                    dve.wait_ge(s_t, 1 + h)
                    ch.link(dve.tensor_copy(dtT[:, 4 * h:4 * h + 4, :], pt[h][:].rearrange("p (m t) -> p m t", t=P)))


def mixer_groups(nc, sem, sb, banks, I, xT, acc, cst, eps, acs_dram, nacs, dtT):
    ident = cst[:, C_ID:C_ID + P]
    BLK = 3 * P
    NW = NG * (PAIRS + 1) + 1
    PS = PAIRS + 1
    with ExitStack() as c:
        ws = [sb(c, f"mg_ws{i}", [P, KD, 2 * P]) for i in range(2)]
        wh = [sb(c, f"mg_wh{i}", [P, KD, 2 * P], F32R) for i in range(2)]
        wl = [sb(c, f"mg_wl{i}", [P, KD, 2 * P], F32R) for i in range(2)]
        wos = [sb(c, f"mg_wos{i}", [P, DM]) for i in range(2)]
        wog = sb(c, "mg_wog", [P, PAIRS, DM])
        yb = sb(c, "mg_y", [P, PAIRS, TOK])
        cbt = sb(c, "mg_cb", [P, BATCH, BLK])
        hT = [sb(c, f"mg_hT{i}", [P, TOK]) for i in range(2)]
        sg = sb(c, "mg_sg", [P, TOK])
        cv = [sb(c, f"mg_cv{i}", [P, HALF]) for i in range(NH)]
        hc = sb(c, "mg_hc", [P, MT, P])
        sq = sb(c, "mg_sq", [P, TOK])
        ssq = sb(c, "mg_ssq", [P, TOK])
        ee = [sb(c, f"mg_e{i}", [P, BLK]) for i in range(2)]
        mm = [sb(c, f"mg_m{i}", [P, BLK]) for i in range(2)]
        rows = [sb(c, f"mg_rows{i}", [2, 2, TOK], F32R) for i in range(2)]
        ones = sb(c, "mg_ones", [2, P], F32R)
        idr = sb(c, "mg_idr", [P, P], F32R)
        mask = sb(c, "mg_mask", [P, 2 * P], F32R)
        cwh = sb(c, "mg_cwh", [P, NW, TAPS])
        cbh = sb(c, "mg_cbh", [P, NW])
        cwc = sb(c, "mg_cwc", [P, NG + 1, TAPS])
        cbc = sb(c, "mg_cbc", [P, NG + 1])
        dp = sb(c, "mg_dp", [P, NG * PAIRS])
        gn = sb(c, "mg_gn", [P, NG * PAIRS])
        sd = sb(c, "mg_sd", [P, MT])
        rs = sb(c, "mg_rs", [P, MT])
        pb = banks(c, "mg_pb", 4)
        tb, = banks(c, "mg_tb", 1)
        gb, = banks(c, "mg_gb", 1)
        py = banks(c, "mg_py", 2)
        s_tab, s_const = sem("mg_tab"), sem("mg_const")
        s_w, s_wo, s_row = ([sem("mg_w0"), sem("mg_w1")], [sem("mg_wo0"), sem("mg_wo1")],
                            [sem("mg_row0"), sem("mg_row1")])
        s_hi, s_lo, s_proj, s_cv, s_ch = sem("mg_hi"), sem("mg_lo"), sem("mg_proj"), sem("mg_conv"), sem("mg_dve")
        s_silu, s_cb, s_cbe = sem("mg_silu"), sem("mg_cb_mm"), sem("mg_cb_copied")
        s_gt, s_t, s_hc, s_seg, s_e = (sem("mg_gate"), sem("mg_turned"), sem("mg_hc_ready"), sem("mg_seg"),
                                       sem("mg_exp"))
        s_m, s_y, s_y1, s_y2, s_sq = sem("mg_m_ready"), sem("mg_y_mm"), sem("mg_y1"), sem("mg_y2"), sem("mg_sq_sum")
        s_wog, s_out, s_ss, s_sd, s_rs, s_acc = (sem("mg_wog_ready"), sem("mg_out"), sem("mg_ss"), sem("mg_sd"),
                                                 sem("mg_rs"), sem("mg_acc"))
        s_sqt, s_gate = sem("mg_sq_tmp"), sem("pool_gate")
        CVG = 4 + 2 * PAIRS
        U = 2 * BATCH
        links = TAPS - 1

        def prior(back):
            return 4 - back

        with nc.Block() as block:
            @block.sync
            def _(sp):
                for t, n in ((cwh, "cwh1"), (cbh, "cbh1"), (cwc, "cwc1"), (cbc, "cbc1"), (dp, "d_1"), (gn, "gn_1")):
                    sp.dma_start(t[:], I[n]).then_inc(s_tab, 16)

                def load_w(q, w, n_lo):
                    sp.wait_ge(s_lo, n_lo)
                    sp.dma_start(ws[q][:], rows3(I["w_in1"][bass.ds(w, 1)])).then_inc(s_w[q], 16)

                sp.dma_start(ws[0][:], I["w_in1"][0]).then_inc(s_w[0], 16)
                sp.dma_start(ws[1][:], I["w_in1"][2]).then_inc(s_w[1], 16)
                sp.wait_ge(s_lo, 4)
                sp.dma_start(ws[0][:], I["w_in1"][1]).then_inc(s_w[0], 16)
                with sp.Fori(0, NG) as g:
                    w0 = g * PS + 1
                    for q in range(PAIRS):
                        par = q % 2
                        p = g * PAIRS + q
                        sp.wait_ge(s_seg, p * U + U)
                        sp.dma_start(rows[par][:].bitcast(F32), acs_dram[:, bass.ds(p * 2, 2), :]).then_inc(s_row[par], 16)
                        sp.wait_ge(s_wog, p + 1)
                        sp.dma_start(wos[par][:], I["w_out1"][bass.ds(p, 1)].rearrange("a p n -> (a p) n")
                                     ).then_inc(s_wo[par], 16)
                        w = w0 + (q + 2)
                        load_w(par if q < 7 else 0, w, w + prior(2 if q < 7 else 1))
                    load_w(1, w0 + 10, w0 + (10 + prior(3)))

            @block.gpsimd
            def _(pool):
                pool.sem_inc(s_lo, 3)
                pool.sem_inc(s_sqt, 1)

                def split(q, w, n_proj, landed):
                    pool.wait_ge(s_w[q], landed)
                    pool.wait_ge(s_proj, n_proj)
                    pool.sem_inc(s_gate, 1)
                    pool.tensor_scalar(wh[q][:], ws[q][:], 1.0, 0.0, ALU.mult, ALU.add).then_inc(s_hi, 1)
                    pool.wait_ge(s_hi, w + 1)
                    pool.tensor_tensor(wl[q][:], ws[q][:], wh[q][:].bitcast(F32), ALU.subtract).then_inc(s_lo, 1)

                split(0, 0, 12, 16)
                split(0, 1, 12 + 4, 32)
                split(1, 2, 12, 16)
                with pool.Fori(0, NG) as g:
                    w0 = g * PS + 1
                    pool.wait_ge(s_ss, g + 1)
                    pool.sem_inc(s_gate, 1)
                    pool.memset(ssq[:], 0.0).then_inc(s_sq, 1)
                    for q in range(PAIRS):
                        w = w0 + (q + 2)
                        if q == 7:
                            landed = g * 80 + 16 * (2 + 5)
                        elif q % 2 == 0:
                            landed = g * 80 + 16 * (2 + q // 2 + 1)
                        else:
                            landed = g * 64 + 16 * (1 + q // 2 + 1)
                        k = 2 if q < 7 else 1
                        split(q % 2 if q < 7 else 0, w, (w + prior(k)) * 4, landed)
                        pool.wait_ge(s_y2, g * 16 + (2 * q + 5))
                        pool.wait_ge(s_sq, g * PS + (q + 1))
                        yv = yb[:, q, :]
                        pool.tensor_tensor(sq[:], yv, yv, ALU.mult).then_inc(s_sqt, 1)
                        pool.wait_ge(s_sqt, g * PAIRS + (q + 2))
                        pool.tensor_tensor(ssq[:], ssq[:], sq[:], ALU.add).then_inc(s_sq, 1)
                    split(1, w0 + 10, (w0 + (10 + prior(3))) * 4, g * 64 + 16 * 5)

            @block.tensor
            def _(pe):
                pe.sem_inc(s_proj, 12)
                pe.sem_inc(s_seg, 2 * U)
                pe.sem_inc(s_ss, 1)
                pe.sem_inc(s_out, MT)
                pe.sem_inc(s_y, 2)
                pe.wait_ge(s_const, 3)
                chunks = [[0, 1, 2], [3], [4], [5], [6], [7], [], []]

                def proj(q, j, ks):
                    t0 = HALF * (j % 2)
                    n0 = P * (j // 2)
                    for k in ks:
                        i = mm3(pe, pb[j][:], (wh[q][:, k, n0:n0 + P], wl[q][:, k, n0:n0 + P]),
                                (xT[0][:, k, t0:t0 + HALF], xT[1][:, k, t0:t0 + HALF]), k == 0, k == KD - 1)
                    if ks[-1] == KD - 1:
                        i.then_inc(s_proj, 1)

                pe.wait_ge(s_lo, 4)
                for j in range(4):
                    proj(0, j, range(KD))
                with pe.Fori(0, NG) as g:
                    w0 = g * PS + 1
                    pe.wait_ge(s_silu, g * CVG + 6)
                    for b in range(BATCH):
                        bank = (tb, gb, py[0], py[1])[b]
                        B, C = hT[0], sg
                        t = b * SEQ
                        pe.matmul(bank[:, 0:P], B[:, t:t + P], C[:, t:t + P], start=True, stop=True)
                        pe.matmul(bank[:, P:2 * P], B[:, t + P:t + SEQ], C[:, t + P:t + SEQ], start=True, stop=True)
                        pe.matmul(bank[:, 2 * P:BLK], B[:, t:t + P], C[:, t + P:t + SEQ], start=True, stop=True
                                  ).then_inc(s_cb, 1)
                    pe.wait_ge(s_lo, w0 + 4)
                    for j in range(4):
                        proj(0, j, range(KD))
                    with pe.Fori(0, PAIRS // 2) as qq:
                        for par in range(2):
                            q = qq * 2 + par
                            p = g * PAIRS + q

                            def y_mm(u):
                                b, hh = u // 2, u % 2
                                pe.wait_ge(s_m, p * U + (u + 3))
                                if u == 0:
                                    pe.wait_ge(s_hc, p * 2 + 2)
                                if u % 4 == 0:
                                    pe.wait_ge(s_y1, p * 2 + (u // 4 + 1))
                                    if u == 0:
                                        pe.wait_ge(s_cbe, g * 4 + 4)
                                r = slice(hh * HP, (hh + 1) * HP)
                                o0 = (b % 2) * SEQ
                                kern = mm[u % 2]
                                m01 = kern[:].rearrange("p (a n) -> p a n", n=P)[:, 0:3:2, :]
                                bank = py[b // 2]
                                pe.matmul(bank[r, o0:o0 + SEQ], hc[:, 2 * b, r], m01, start=True, stop=False)
                                pe.matmul(bank[r, o0 + P:o0 + SEQ], hc[:, 2 * b + 1, r], kern[:, P:2 * P],
                                          start=False, stop=True).then_inc(s_y, 1)

                            def turn(h):
                                pe.wait_ge(s_silu, g * CVG + (q * 2 + (h + 7)))
                                if h:
                                    pe.wait_ge(s_hc, p * 2 + 1)
                                for m in range(4):
                                    mt = 4 * h + m
                                    i = pe.transpose(tb[:, m * P:(m + 1) * P], hT[par][:, mt * P:(mt + 1) * P], ident)
                                i.then_inc(s_t, 1)

                            def chunk(n):
                                j = n // 2
                                if n == 0:
                                    pe.wait_ge(s_lo, w0 + (q + 5))
                                if n % 2 == 0:
                                    if j < 2:
                                        pe.wait_ge(s_cv, g * CVG + (q * 2 + (4 + j + 1)))
                                    else:
                                        pe.wait_ge(s_gt, p * 2 + (j - 2 + 1))
                                proj(1 - par, j, range(2 * (n % 2), 2 * (n % 2) + 2))

                            for u in range(U):
                                b, hh = u // 2, u % 2
                                if u == 0:
                                    pe.wait_ge(s_row[par], g * 64 + (qq * 16 + 16))
                                    pe.wait_ge(s_cbe, g * 4 + 4)
                                pe.wait_ge(s_e, (p * U + u) * 2 + 2)
                                rv = rows[par][:, hh, b * SEQ:(b + 1) * SEQ]
                                pe.matmul(gb[:, 0:2 * P], ones[:], rv, start=True, stop=False)
                                pe.matmul(gb[:, 0:2 * P], idr[:], mask[:], start=False, stop=True)
                                pe.matmul(gb[:, 2 * P:BLK], ones[:], rv[:, P:], start=True, stop=True
                                          ).then_inc(s_seg, 1)
                                for n in chunks[u]:
                                    chunk(n)
                                    if n in (1, 2):
                                        turn(n - 1)
                                if u > 0:
                                    y_mm(u - 1)
                            y_mm(U - 1)
                    obs = (pb[0], pb[1], py[0], py[1])
                    pe.wait_ge(s_cv, g * CVG + (4 + 2 * PAIRS + 2))
                    pe.wait_ge(s_y1, g * 16 + 18)
                    pe.wait_ge(s_y2, g * 16 + 19)
                    pe.wait_ge(s_wog, g * PAIRS + (PAIRS + 2))
                    for m in range(MT):
                        if m >= 4:
                            pe.wait_ge(s_acc, g * MT + (m - 3))
                        for k in range(PAIRS):
                            i = pe.matmul(obs[m % 4][:], yb[:, k, m * P:(m + 1) * P], wog[:, k, :],
                                          start=k == 0, stop=k == PAIRS - 1)
                        i.then_inc(s_out, 1)
                        if m == 0:
                            pe.wait_ge(s_sq, g * PS + PS)
                            for n in range(MT):
                                i = pe.matmul(tb[:, n:n + 1], ssq[:, n * P:(n + 1) * P], cst[:, C_ONE:C_ONE + 1],
                                              start=True, stop=True)
                            i.then_inc(s_ss, 1)
                    pe.wait_ge(s_acc, g * MT + MT)

            @block.vector
            def _(dve):
                dve.sem_inc(s_y1, 2)
                dve.sem_inc(s_y2, 3)
                dve.sem_inc(s_m, 2)
                dve.wait_ge(s_tab, 96)
                dve.memset(ones[:].bitcast(F32), 1.0).then_inc(s_const, 1)
                dve.tensor_copy(idr[:], ident).then_inc(s_const, 1)
                dve.tensor_copy(mask[:], cst[:, C_MASK:C_MASK + 2 * P]).then_inc(s_const, 1)

                def conv(ch, j, n_proj, n_read, w, b):
                    dve.wait_ge(s_proj, n_proj)
                    dve.wait_ge(s_silu, n_read)
                    conv_half(dve, ch, cv[j % 2][:], pb[j][:], w, b).then_inc(s_cv, 1)

                def hid_w(w):
                    return cwh[:, bass.ds(w, 1), :].rearrange("p a k -> p (a k)"), cbh[:, bass.ds(w, 1)]

                def c_w(g):
                    return cwc[:, bass.ds(g, 1), :].rearrange("p a k -> p (a k)"), cbc[:, bass.ds(g, 1)]

                ch = Chain(dve, s_ch)
                for j in range(4):
                    conv(ch, j, 12 + j + 1, j + 1, *(hid_w(0) if j < 2 else c_w(0)))
                with dve.Fori(0, NG) as g:
                    w0 = g * PS + 1
                    for b in range(BATCH):
                        bank = (tb, gb, py[0], py[1])[b]
                        dve.wait_ge(s_cb, g * 4 + (b + 1))
                        dve.tensor_copy(cbt[:, b, :], bank[:, 0:BLK]).then_inc(s_cbe, 1)
                    base = g * (CVG * links) + 4 * links
                    ch = Chain(dve, s_ch, base)
                    for j in range(2):
                        conv(ch, j, (w0 + 3) * 4 + (j + 1), g * CVG + (4 + j + 1), *hid_w(w0))
                    with dve.Fori(0, PAIRS // 2) as qq:
                        for par in range(2):
                            q = qq * 2 + par
                            p = g * PAIRS + q
                            ch = Chain(dve, s_ch, base + (q * (2 * links) + 2 * links))
                            for h in range(2):
                                dve.wait_ge(s_t, p * 2 + (h + 1))
                                dve.wait_ge(s_y, p * U + 2)
                                dst = hc[:, 4 * h:4 * h + 4, :].rearrange("p m (a c) -> p m a c", c=HP)
                                src = tb[:].rearrange("p (m a c) -> p m a c", a=2, c=HP)
                                dtv = dtT[:, 4 * h:4 * h + 4, bass.ds(p * 2, 2)].unsqueeze(3).to_broadcast(
                                    [P, 4, 2, HP])
                                dve.tensor_tensor(dst, src, dtv, ALU.mult).then_inc(s_hc, 1)

                            def out_half(h):
                                t = slice(h * HALF, (h + 1) * HALF)
                                dve.wait_ge(s_y, p * U + (4 * h + 6))
                                dve.scalar_tensor_tensor(out=hT[par][:, t], in0=hT[par][:, t],
                                                         scalar=dp[:, bass.ds(p, 1)], in1=py[h][:], op0=ALU.mult,
                                                         op1=ALU.add).then_inc(s_y1, 1)
                                dve.wait_ge(s_y1, p * 2 + (h + 3))
                                dve.wait_ge(s_gt, p * 2 + 2)
                                dve.wait_ge(s_out, g * MT + MT)
                                dve.tensor_tensor(yb[:, bass.ds(q, 1), t].rearrange("p a t -> p (a t)"),
                                                  hT[par][:, t], sg[:, t], ALU.mult).then_inc(s_y2, 1)

                            for u in range(U):
                                dve.wait_ge(s_e, (p * U + u) * 2 + 4)
                                dve.wait_ge(s_y, p * U + (u + 1))
                                dve.tensor_tensor(mm[u % 2][:], ee[u % 2][:], cbt[:, u // 2, :], ALU.mult
                                                  ).then_inc(s_m, 1)
                                if u in (3, 5):
                                    j = (u - 3) // 2
                                    conv(ch, j, (w0 + 4 + q) * 4 + (j + 1), g * CVG + (q * 2 + (6 + j + 1)),
                                         *hid_w(w0 + q + 1))
                                if u == 6:
                                    out_half(0)
                            out_half(1)
                    ch = Chain(dve, s_ch, base + (2 * PAIRS + 2) * links)
                    for j in range(2, 4):
                        conv(ch, j, (w0 + 11) * 4 + (j + 1), g * CVG + (4 + 2 * PAIRS + j + 1), *c_w(g + 1))
                    dve.wait_ge(s_sd, g + 1)
                    dve.reciprocal(rs[:], sd[:]).then_inc(s_rs, 1)
                    dve.wait_ge(s_rs, g + 1)
                    obs = (pb[0], pb[1], py[0], py[1])
                    for m in range(MT):
                        dve.wait_ge(s_out, g * MT + (MT + m + 1))
                        dve.scalar_tensor_tensor(out=acc[:, m, :], in0=obs[m % 4][:], scalar=rs[:, m:m + 1],
                                                 in1=acc[:, m, :], op0=ALU.mult, op1=ALU.add).then_inc(s_acc, 1)
                    dve.wait_ge(s_acc, g * MT + MT)

            @block.scalar
            def _(act):
                act.sem_inc(s_silu, 2)
                act.sem_inc(s_e, 2)
                act.sem_inc(s_wog, 2)
                act.wait_ge(s_tab, 96)

                def silu(n_cv, j, dst):
                    act.wait_ge(s_cv, n_cv)
                    act.activation(dst[:, (j % 2) * HALF:(j % 2 + 1) * HALF], cv[j % 2][:], ACT.Silu
                                   ).then_inc(s_silu, 1)

                for j in range(4):
                    silu(j + 1, j, hT[0] if j < 2 else sg)
                with act.Fori(0, NG) as g:
                    w0 = g * PS + 1
                    act.wait_ge(s_cb, g * 4 + 4)
                    with act.Fori(0, PAIRS // 2) as qq:
                        for par in range(2):
                            q = qq * 2 + par
                            p = g * PAIRS + q
                            for j in range(2):
                                act.wait_ge(s_y2, p * 2 + 1)
                                silu(g * CVG + (q * 2 + (5 + j)), j, hT[par])
                            for j in range(2, 4):
                                act.wait_ge(s_proj, (w0 + q + 3) * 4 + (j + 1))
                                act.wait_ge(s_y2, p * 2 + 3)
                                act.activation(sg[:, (j - 2) * HALF:(j - 1) * HALF], pb[j][:], ACT.Silu
                                               ).then_inc(s_gt, 1)
                            for u in range(U):
                                b, hh = u // 2, u % 2
                                act.wait_ge(s_seg, p * U + (u + 2 * U + 1))
                                act.wait_ge(s_m, p * U + (u + 1))
                                e3 = ee[u % 2][:].rearrange("p (a n) -> p a n", n=P)
                                g3 = gb[:, 0:BLK].rearrange("p (a n) -> p a n", n=P)
                                for a, jc in ((slice(0, 3, 2), 0), (slice(1, 2), 1)):
                                    act.activation(e3[:, a, :], g3[:, a, :], ACT.Exp,
                                                   bias=nacs[:, 2 * b + jc, bass.ds(p * 2 + hh, 1)]
                                                   ).then_inc(s_e, 1)
                                if u == 3:
                                    act.wait_ge(s_wo[par], g * 64 + (qq * 16 + 16))
                                    act.wait_ge(s_out, g * MT + MT)
                                    act.wait_ge(s_tab, 96)
                                    act.activation(wog[:, bass.ds(q, 1), :], wos[par][:].unsqueeze(1), ACT.Copy,
                                                   scale=gn[:, bass.ds(p, 1)]).then_inc(s_wog, 1)
                    act.wait_ge(s_y2, g * 16 + 19)
                    for j in range(4):
                        silu(g * CVG + (21 + j), j, hT[0] if j < 2 else sg)
                    act.wait_ge(s_ss, g + 2)
                    act.activation(sd[:], tb[:, 0:MT], ACT.Sqrt, bias=eps[:, 2:3], scale=1.0 / GRP).then_inc(s_sd, 1)


def ffn(nc, sem, sb, banks, I, xT, o, ident):
    with ExitStack() as c:
        CW = 2 * QB
        ws = sb(c, "ff_ws", [P, 2, KD, CW])
        w2s = sb(c, "ff_w2s", [P, 2, DM])
        wh = [sb(c, f"ff_wh{i}", [P, 2, KD, CW], F32R) for i in range(2)]
        wl = [sb(c, f"ff_wl{i}", [P, 2, KD, CW], F32R) for i in range(2)]
        w2h = [sb(c, f"ff_w2h{i}", [P, 2, DM], F32R) for i in range(2)]
        w2l = [sb(c, f"ff_w2l{i}", [P, 2, DM], F32R) for i in range(2)]
        sc = sb(c, "ff_sc", [P, 2, FC, KD, 2])
        sc2 = sb(c, "ff_sc2", [P, FC, 2, KD])
        g = [sb(c, f"ff_g{i}", [P, CW]) for i in range(2)]
        h = [sb(c, f"ff_h{i}", [P, CW]) for i in range(2)]
        qa = [sb(c, f"ff_qa{i}", [P, 2]) for i in range(2)]
        qs = [sb(c, f"ff_qs{i}", [P, 2]) for i in range(2)]
        qr = [sb(c, f"ff_qr{i}", [P, 2]) for i in range(2)]
        hh = [sb(c, f"ff_hh{i}", [P, CW], F32R) for i in range(2)]
        hl = [sb(c, f"ff_hl{i}", [P, CW], F32R) for i in range(2)]
        pg = banks(c, "ff_pg", 3)
        pt = banks(c, "ff_pt", 2)
        po = banks(c, "ff_po", 2)
        s_sc, s_w, s_dq, s_hi, s_lo = sem("ff_sc_in"), sem("ff_w_in"), sem("ff_dequant"), sem("ff_hi"), sem("ff_lo")
        s_gu, s_g, s_h0, s_h, s_ch = sem("ff_gu"), sem("ff_silu"), sem("ff_h0"), sem("ff_h_ready"), sem("ff_dve")
        s_gate = sem("pool_gate")
        s_t, s_hh, s_hl, s_o, s_acc, s_z = (sem("ff_turned"), sem("ff_hh_ready"), sem("ff_hl_ready"), sem("ff_out"),
                                            sem("ff_acc"), sem("ff_zeroed"))
        LINKS = 4

        def chunks(eng, body):
            with eng.Fori(0, FC // 2) as i:
                for par in range(2):
                    body(i * 2 + par, par)
            body(FC - 1, 0)

        with nc.Block() as block:
            @block.sync
            def _(sp):
                sp.dma_start(sc[:], I["w13_scale"].partition_broadcast(P).rearrange(
                    "p a (s f k b) -> p (a s) f k b", s=2, f=FC, k=KD)).then_inc(s_sc, 16)
                sp.dma_start(sc2[:], I["w2_scale"].partition_broadcast(P).rearrange(
                    "p a (f b n) -> p (a f) b n", f=FC, b=2)).then_inc(s_sc, 16)

                def body(f, par):
                    sp.wait_ge(s_lo, f * 2 + 2)
                    sp.dma_start(ws[:], I["w13"][bass.ds(f, 1)].rearrange("a p s k n -> (a p) s k n")
                                 ).then_inc(s_w, 16)
                    sp.dma_start(w2s[:], I["w2"][bass.ds(f, 1)].rearrange("a p b n -> (a p) b n")).then_inc(s_w, 16)
                chunks(sp, body)

            @block.gpsimd
            def _(pool):
                pool.sem_inc(s_lo, 2)

                def body(f, par):
                    pool.wait_ge(s_dq, f * 3 + 3)
                    pool.wait_ge(s_o, f * MT + 1)
                    fl = lambda a: a[:].rearrange("p a k n -> p (a k n)")
                    f2 = lambda a: a[:].rearrange("p a n -> p (a n)")
                    pool.sem_inc(s_gate, 1)
                    pool.tensor_scalar(fl(wh[par]), fl(ws), 1.0, 0.0, ALU.mult, ALU.add).then_inc(s_hi, 1)
                    pool.tensor_scalar(f2(w2h[par]), f2(w2s), 1.0, 0.0, ALU.mult, ALU.add).then_inc(s_hi, 1)
                    pool.wait_ge(s_hi, f * 2 + 2)
                    pool.tensor_tensor(fl(wl[par]), fl(ws), fl(wh[par]).bitcast(F32), ALU.subtract).then_inc(s_lo, 1)
                    pool.tensor_tensor(f2(w2l[par]), f2(w2s), f2(w2h[par]).bitcast(F32), ALU.subtract
                                       ).then_inc(s_lo, 1)
                chunks(pool, body)

            @block.tensor
            def _(pe):
                pe.sem_inc(s_o, MT + 1)

                def body(f, par):
                    base = f * MT

                    def turn(m):
                        pe.wait_ge(s_h, base + (m + 1))
                        pe.wait_ge(s_hl, base + (m + 1))
                        for b in range(2):
                            i = pe.transpose(pt[m % 2][:, b * QB:(b + 1) * QB], h[m % 2][:, b * QB:(b + 1) * QB],
                                             ident)
                        i.then_inc(s_t, 1)

                    def down(m):
                        pe.wait_ge(s_hl, base + (m + 3))
                        pe.wait_ge(s_acc, base + (m + 1))
                        for b in range(2):
                            r = slice(b * QB, (b + 1) * QB)
                            i = mm3(pe, po[m % 2][:], (hh[m % 2][:, r], hl[m % 2][:, r]),
                                    (w2h[par][:, b, :], w2l[par][:, b, :]), b == 0, b == 1)
                        i.then_inc(s_o, 1)

                    pe.wait_ge(s_lo, f * 2 + 4)
                    for m in range(MT):
                        pe.wait_ge(s_h0, base + (m + 1))
                        t = slice(m * P, (m + 1) * P)
                        for s in range(2):
                            for k in range(KD):
                                i = mm3(pe, pg[m % 2][:, s * CW:(s + 1) * CW], (xT[0][:, k, t], xT[1][:, k, t]),
                                        (wh[par][:, s, k, :], wl[par][:, s, k, :]), k == 0, k == KD - 1)
                        i.then_inc(s_gu, 1)
                        if m >= 1:
                            turn(m - 1)
                        if m >= 2:
                            down(m - 2)
                    turn(MT - 1)
                    down(MT - 2)
                    down(MT - 1)
                chunks(pe, body)

            @block.scalar
            def _(act):
                def body(f, par):
                    base = f * MT

                    def hi(m):
                        act.wait_ge(s_t, base + (m + 1))
                        act.wait_ge(s_o, base + (m + MT))
                        act.activation(hh[m % 2][:], pt[m % 2][:, 0:CW], ACT.Copy).then_inc(s_hh, 1)
                    for m in range(MT):
                        act.wait_ge(s_gu, base + (m + 1))
                        act.wait_ge(s_h0, base + (m + 1))
                        act.activation(g[m % 2][:], pg[m % 2][:, 0:CW], ACT.Silu).then_inc(s_g, 1)
                        if m >= 1:
                            hi(m - 1)
                    hi(MT - 1)
                chunks(act, body)

            @block.vector
            def _(dve):
                dve.sem_inc(s_h0, 2)
                dve.sem_inc(s_hl, 2)
                dve.sem_inc(s_acc, 2)
                dve.memset(o[:], 0.0).then_inc(s_z, 1)
                dve.wait_ge(s_sc, 32)
                dve.wait_ge(s_z, 1)

                def body(f, par):
                    base = f * MT
                    dve.wait_ge(s_w, f * 32 + 32)
                    for s in range(2):
                        wv = ws[:, s].rearrange("p k (b n) -> p (k b) n", n=QB)
                        scv = sc[:, s, bass.ds(f, 1)].rearrange("p a k b -> p (a k b)")
                        dve.tensor_tensor(wv, wv, scv.unsqueeze(2).to_broadcast([P, 2 * KD, QB]), ALU.mult
                                          ).then_inc(s_dq, 1)
                    wv = w2s[:].rearrange("p b (o n) -> p (b o) n", n=QB)
                    scv = sc2[:, bass.ds(f, 1)].rearrange("p a b o -> p (a b o)")
                    dve.tensor_tensor(wv, wv, scv.unsqueeze(2).to_broadcast([P, 2 * KD, QB]), ALU.mult
                                      ).then_inc(s_dq, 1)
                    ch = Chain(dve, s_ch, f * (MT * LINKS))

                    def lo(m):
                        dve.wait_ge(s_hh, base + (m + 1))
                        dve.tensor_tensor(hl[m % 2][:], pt[m % 2][:, 0:CW], hh[m % 2][:].bitcast(F32), ALU.subtract
                                          ).then_inc(s_hl, 1)

                    def add(m):
                        dve.wait_ge(s_o, base + (m + MT + 2))
                        dve.tensor_tensor(o[:, m, :], o[:, m, :], po[m % 2][:], ALU.add).then_inc(s_acc, 1)

                    for m in range(MT):
                        i = m % 2
                        dve.wait_ge(s_g, base + (m + 1))
                        dve.wait_ge(s_t, base + m) if m else None
                        hv = h[i][:].rearrange("p (b n) -> p b n", n=QB)
                        dve.tensor_tensor(h[i][:], g[i][:], pg[i][:, CW:2 * CW], ALU.mult).then_inc(s_h0, 1)
                        dve.wait_ge(s_h0, base + (m + 3))
                        ch.link(dve.tensor_reduce(qa[i][:], hv, AX_X, ALU.max, apply_absolute_value=True))
                        ch.link(dve.tensor_scalar(qs[i][:], qa[i][:], 1.0 / FP8_MAX, Q_EPS, ALU.mult, ALU.add))
                        ch.link(dve.reciprocal(qr[i][:], qs[i][:]))
                        ch.link(dve.tensor_tensor(hv, hv, qr[i][:].unsqueeze(2).to_broadcast([P, 2, QB]), ALU.mult))
                        dve.tensor_tensor(hv, hv, qs[i][:].unsqueeze(2).to_broadcast([P, 2, QB]), ALU.mult
                                          ).then_inc(s_h, 1)
                        if m >= 1:
                            lo(m - 1)
                        if m >= 2:
                            add(m - 2)
                    lo(MT - 1)
                    add(MT - 2)
                    add(MT - 1)
                chunks(dve, body)
                dve.wait_ge(s_acc, FC * MT + 2)


def laid_out(a):
    import numpy as np

    f = lambda n: np.asarray(a[n])
    z = lambda *s: np.zeros(s, np.float32)

    def ktile(w, n):
        return w.reshape(-1, n, KD, P).transpose(0, 3, 2, 1)

    def col(v, n):
        return v.reshape(n, P).T

    consts = z(P, C_N)
    consts[:, C_ID:C_ID + P] = np.eye(P)
    tri = np.where(np.arange(P)[:, None] > np.arange(P)[None, :], -1e30, 0.0)
    consts[:, C_MASK:C_MASK + P] = tri
    consts[:, C_MASK + P:C_MASK + 2 * P] = tri
    edges = (0, RNK, RNK + NST, RNK + 2 * NST)
    for lo, hi in zip(edges, edges[1:]):
        consts[lo:hi, C_BLK + lo:C_BLK + hi] = 1.0
        consts[lo:hi, C_INV] = 1.0 / (hi - lo)
    consts[:, C_ONE] = 1.0

    w0 = f("L0_attn_in_proj_w").T
    w0 = np.concatenate([w0[:DIN].reshape(CD, P, DM), w0[DIN:].reshape(CD, P, DM)], 1)
    ex = np.concatenate([f("L0_ffn_W_base"), f("L0_ffn_A_w").reshape(NE * ER, DM), f("L0_ffn_W_gate"),
                         f("L0_ffn_W_thr")[None], z(1, DM)])

    w1 = f("L1_attn_in_proj_w")
    gate, hid = w1[:DI1].reshape(NG, PAIRS, P, DM), w1[DI1:2 * DI1].reshape(NG, PAIRS, P, DM)
    pad = z(1, P, DM)
    B = np.concatenate([w1[2 * DI1:2 * DI1 + NG * NS].reshape(NG, P, DM), pad])
    C = np.concatenate([w1[2 * DI1 + NG * NS:2 * DI1 + 2 * NG * NS].reshape(NG, P, DM), pad])
    dtw = w1[2 * DI1 + 2 * NG * NS:]
    steps = [np.concatenate([B[0], C[0]])]
    for g in range(NG):
        steps += [np.concatenate([hid[g, q], gate[g, q]]) for q in range(PAIRS)]
        steps.append(np.concatenate([B[g + 1], C[g + 1]]))
    steps += [z(2 * P, DM)] * 2
    cw, cb = f("L1_attn_conv_w"), f("L1_attn_conv_b")
    ch = cw[:DI1].reshape(NG, PAIRS, P, TAPS)
    cB = np.concatenate([cw[DI1:DI1 + NG * NS].reshape(NG, P, TAPS), z(1, P, TAPS)])
    cC = np.concatenate([cw[DI1 + NG * NS:].reshape(NG, P, TAPS), z(1, P, TAPS)])
    bh = cb[:DI1].reshape(NG, PAIRS, P)
    bB = np.concatenate([cb[DI1:DI1 + NG * NS].reshape(NG, P), z(1, P)])
    bC = np.concatenate([cb[DI1 + NG * NS:].reshape(NG, P), z(1, P)])
    cwh, cbh = [cB[0]], [bB[0]]
    for g in range(NG):
        cwh += list(ch[g]) + [cB[g + 1]]
        cbh += list(bh[g]) + [bB[g + 1]]

    def chunks(w):
        return w.reshape(FC, 2 * QB, KD, P).transpose(0, 3, 2, 1)

    def scales(s):
        return s.reshape(FC, 2, KD).transpose(0, 2, 1)

    return {
        "consts": consts,
        "x": f("L0_attn_hidden_states").reshape(TOK, DM),
        "w_in0": ktile(w0.reshape(-1, DM), 2 * P),
        "conv_w0": f("L0_attn_conv_w").reshape(CD, P, TAPS).transpose(1, 0, 2),
        "conv_b0": col(f("L0_attn_conv_b"), CD),
        "x_proj": f("L0_attn_x_proj_w").T.reshape(CD, P, -1).transpose(1, 0, 2),
        "dt_proj": f("L0_attn_dt_proj_w").T,
        "dt_bias0": col(f("L0_attn_dt_bias"), CD),
        "ln_w0": np.concatenate([f("L0_attn_dt_ln_w"), f("L0_attn_B_ln_w"), f("L0_attn_C_ln_w")])[:, None],
        "a_log0": f("L0_attn_A_log").reshape(CD, P, NST).transpose(1, 0, 2),
        "d_0": col(f("L0_attn_D_param"), CD),
        "w_out0": f("L0_attn_out_proj_w").T.reshape(CD, P, DM).transpose(1, 0, 2),
        "w_ex": ktile(ex, len(ex))[0],
        "b_base": f("L0_ffn_b_base")[None],
        "b_thr": f("L0_ffn_b_thr")[None],
        "w_up": f("L0_ffn_B_w").transpose(0, 2, 1).reshape(NE * ER, DM),
        "norm_w1": col(f("L1_attn_norm_w"), KD),
        "w_dt1": ktile(dtw, P)[0],
        "dt_bias1": f("L1_attn_dt_bias")[:, None],
        "a_log1": f("L1_attn_A_log")[:, None],
        "w_in1": ktile(np.concatenate(steps), 2 * P),
        "cwh1": np.stack(cwh, 1), "cbh1": np.stack(cbh, 1),
        "cwc1": cC.transpose(1, 0, 2), "cbc1": bC.T,
        "d_1": col(np.repeat(f("L1_attn_Dp"), HP), NG * PAIRS),
        "gn_1": col(f("L1_attn_gnorm_w"), NG * PAIRS),
        "w_out1": f("L1_attn_out_proj_w").T.reshape(NG * PAIRS, P, DM),
        "w13": np.stack([chunks(f("L1_ffn_w1")), chunks(f("L1_ffn_w3"))], 2),
        "w13_scale": np.stack([scales(f("L1_ffn_w1_scale")), scales(f("L1_ffn_w3_scale"))]).reshape(1, -1),
        "w2": f("L1_ffn_w2").T.reshape(FC, 2, P, DM).transpose(0, 2, 1, 3),
        "w2_scale": f("L1_ffn_w2_scale").T.reshape(1, -1),
    }


def kernel(**inputs):
    import concourse.bacc as bacc
    import numpy as np
    from concourse.bass_utils import run_bass_kernel_spmd

    nc = bacc.Bacc("TRN2", target_bir_lowering=False, num_devices=1)
    arrays, aps = {}, {}
    for name, a in laid_out(inputs).items():
        a = np.ascontiguousarray(a, dtype=np.float32)
        arrays["in_" + name] = a
        aps[name] = nc.dram_tensor("in_" + name, a.shape, F32, kind="ExternalInput").ap()
    out = nc.dram_tensor("out_0", (TOK, DM), F32, kind="ExternalOutput").ap()
    build(nc, aps, out)
    r = run_bass_kernel_spmd(nc, [arrays], core_ids=[0])
    return r.results[0]["out_0"].reshape(BATCH, SEQ, DM)
```

```python
from contextlib import ExitStack

import concourse.bass as bass
from concourse import mybir

F32 = mybir.dt.float32
F32R = mybir.dt.float32r
ALU = mybir.AluOpType
ACT = mybir.ActivationFunctionType
AX_X = mybir.AxisListType.X

P = 128
BATCH, SEQ, DM = 4, 256, 512
TOK = BATCH * SEQ
MT = TOK // P
KD = DM // P
HALF = 512
NH = TOK // HALF
BPH = HALF // SEQ
LN_EPS = 1e-5

DIN, NST, RNK, TAPS = 1024, 16, 32, 4
CD = DIN // P
NX = RNK + 2 * NST
SCAN_EPS = 1e-6
NE, ER = 8, 16
MAX_THR, MOE_SCALE = 0.125, 2.0
GW = NE + 2
NHEAD, HP, NG, NS = 128, 64, 8, 128
DI1 = NHEAD * HP
PAIRS = DI1 // P // NG
GRP = DI1 // NG
MIX_EPS = 1e-5
INTER, QB, FP8_MAX, Q_EPS = 1792, 128, 448.0, 1e-12
FC = INTER // (2 * QB)

C_ID, C_MASK, C_BLK, C_INV, C_ONE = 0, 128, 384, 448, 449
C_N = 450


class Chain:

    def __init__(self, eng, sem, base=0):
        self.eng, self.sem, self.base, self.n = eng, sem, base, 0

    def mark(self, ins):
        self.n += 1
        ins.then_inc(self.sem, 1)
        return self.n

    def wait(self, n=None):
        self.eng.wait_ge(self.sem, self.base + (self.n if n is None else n))

    def link(self, ins):
        self.mark(ins)
        self.wait()


def mm3(pe, out, lhs, rhs, start, stop):
    pe.matmul(out, lhs[0], rhs[0], start=start, stop=False)
    pe.matmul(out, lhs[0], rhs[1], start=False, stop=False)
    return pe.matmul(out, lhs[1], rhs[0], start=False, stop=stop)


def build(nc, I, out):
    with ExitStack() as top:
        sems = {}

        def sem(name):
            if name not in sems:
                sems[name] = top.enter_context(nc.semaphore(name))
            return sems[name]

        def scope():
            return ExitStack()

        def sb(ctx, name, shape, dt=F32):
            return ctx.enter_context(nc.sbuf_tensor(name, shape, dt))

        def banks(ctx, name, n):
            return [ctx.enter_context(nc.psum_tensor(f"{name}{i}", [P, HALF], F32)) for i in range(n)]

        x_tok = I["x"].rearrange("(m p) d -> p m d", p=P)
        out_tok = out.rearrange("(m p) d -> p m d", p=P)
        bc_dram = nc.dram_tensor("bc_rows", [2 * NST, TOK], F32, kind="Internal").ap()
        acs_dram = nc.dram_tensor("acs_rows", [2, NHEAD, TOK], F32, kind="Internal").ap()
        x_dram = nc.dram_tensor("x_kept", [TOK, DM], F32, kind="Internal").ap().rearrange("(m p) d -> p m d", p=P)

        cst = sb(top, "cst", [P, C_N])
        eps = sb(top, "eps", [P, 4])
        ident = cst[:, C_ID:C_ID + P]
        ones_col = cst[:, C_ONE:C_ONE + 1]
        s_cst, s_eps = sem("cst_in"), sem("eps_set")

        norm_counts = {"chain": 0, "var": 0, "tiles": 0}

        def norm_stage(tag, x, o, load_x, xT, rms, keep, quant=False):
            with scope() as c:
                h = keep if keep is not None else sb(c, tag + "h", [P, MT, DM])
                h2 = sb(c, tag + "h2", [P, MT, DM]) if rms else h
                st = sb(c, tag + "st", [P, MT, 6])
                mv = sb(c, tag + "mv", [P, MT, 2])
                sd = sb(c, tag + "sd", [P, MT])
                rs = sb(c, tag + "rs", [P, MT])
                qa = sb(c, tag + "qa", [P, MT, KD])
                qs = sb(c, tag + "qs", [P, MT, KD])
                qr = sb(c, tag + "qr", [P, MT, KD])
                sq = sb(c, tag + "sq", [P, DM])
                nw = sb(c, tag + "nw", [P, KD])
                tb = banks(c, tag + "tb", MT)
                s_chain, s_var, s_sd, s_h = sem("norm_dve"), sem("norm_var"), sem("norm_sd"), sem("norm_h_ready")
                s_x = sem(tag + "x_in") if load_x or rms else None
                s_keep = sem(tag + "kept") if rms or xT is None else None
                s_xr = sem(tag + "x_ready") if rms else None
                s_t, s_hi, s_lo = sem("norm_turned"), sem("norm_hi"), sem("norm_lo")
                rounds = (1 if o is not None else 0) + (1 if xT is not None else 0)

                n0 = dict(norm_counts)
                norm_counts["var"] += rounds + (1 if rms else 0)
                norm_counts["tiles"] += MT
                v0, m0 = n0["var"], n0["tiles"]

                with nc.Block() as block:
                    @block.sync
                    def _(sp):
                        if load_x:
                            for m in range(MT):
                                sp.dma_start(x[:, m, :], x_tok[:, m, :]).then_inc(s_x, 16)
                        if rms:
                            sp.dma_start(nw[:], I["norm_w1"]).then_inc(s_x, 16)
                            sp.wait_ge(s_xr, 1)
                            sp.dma_start(x_dram, x[:]).then_inc(s_keep, 16)
                            sp.wait_ge(s_keep, 16)
                        if xT is None:
                            for m in range(MT):
                                sp.wait_ge(s_h, m0 + m + 1)
                                sp.dma_start(out_tok[:, m, :], x[:, m, :]).then_inc(s_keep, 16)
                            sp.wait_ge(s_keep, 16 * MT)

                    @block.vector
                    def _(dve):
                        ch = Chain(dve, s_chain, n0["chain"])

                        def normalise(src, dst, n, last=None):
                            for m in range(MT):
                                if n == 0 and load_x:
                                    dve.wait_ge(s_x, 16 * MT)
                                ch.mark(dve.bn_stats(st[:, m, :], src[:, m, :]))
                            ch.wait()
                            for m in range(MT):
                                i = dve.bn_aggr(mv[:, m, :], st[:, m, :])
                                ch.mark(i) if m < MT - 1 else i.then_inc(s_var, 1)
                            dve.wait_ge(s_sd, v0 + n + 1)
                            ch.link(dve.reciprocal(rs[:], sd[:]))
                            for m in range(MT):
                                i = dve.tensor_scalar(dst[:, m, :], src[:, m, :], mv[:, m, 0:1], rs[:, m:m + 1],
                                                      ALU.subtract, ALU.mult)
                                last(i) if last else ch.mark(i)
                            if not last:
                                ch.wait()

                        n = 0
                        if o is not None:
                            normalise(o, o, 0)
                            n = 1
                            if load_x:
                                dve.wait_ge(s_x, 16 * MT)
                            for m in range(MT):
                                i = dve.tensor_tensor(x[:, m, :], x[:, m, :], o[:, m, :], ALU.add)
                                if xT is None:
                                    i.then_inc(s_h, 1)
                                else:
                                    ch.mark(i)
                            if xT is None:
                                norm_counts["chain"] += ch.n
                                return
                            ch.wait()
                            if rms:
                                dve.engine_nop().then_inc(s_xr, 1)
                        direct = not rms and not quant
                        normalise(x, h, n, (lambda i: i.then_inc(s_h, 1)) if direct else None)
                        if rms:
                            for m in range(MT):
                                dve.tensor_tensor_reduce(sq[:], h[:, m, :], h[:, m, :], 1.0, 0.0, ALU.mult,
                                                         ALU.add, mv[:, m, 0:1]).then_inc(s_chain, 1)
                                ch.n += 1
                                ch.wait()
                            dve.tensor_copy(qs[:, :, 0], mv[:, :, 0]).then_inc(s_var, 1)
                            dve.wait_ge(s_sd, v0 + n + 2)
                            ch.link(dve.reciprocal(rs[:], sd[:]))
                            for m in range(MT):
                                dve.tensor_scalar(h2[:, m, :], h[:, m, :], rs[:, m:m + 1], None,
                                                  ALU.mult).then_inc(s_h, 1)
                            dve.wait_ge(s_x, 16 * ((MT if load_x else 0) + 1))
                        if quant:
                            hq = h[:].rearrange("p m (b k) -> p (m b) k", k=QB)
                            fl = lambda a: a[:].rearrange("p m b -> p (m b)")
                            ch.link(dve.tensor_reduce(fl(qa), hq, AX_X, ALU.max, apply_absolute_value=True))
                            ch.link(dve.tensor_scalar(fl(qs), fl(qa), 1.0 / FP8_MAX, Q_EPS, ALU.mult, ALU.add))
                            ch.link(dve.reciprocal(fl(qr), fl(qs)))
                            for m in range(MT):
                                for b in range(KD):
                                    i = dve.tensor_scalar(h[:, m, b * QB:(b + 1) * QB], h[:, m, b * QB:(b + 1) * QB],
                                                          qr[:, m, b:b + 1], qs[:, m, b:b + 1], ALU.mult, ALU.mult)
                                i.then_inc(s_h, 1)
                        norm_counts["chain"] += ch.n
                        for m in range(MT):
                            dve.wait_ge(s_hi, m0 + m + 1)
                            src = tb[m][:].rearrange("p (k t) -> p k t", k=KD)
                            hi = xT[0][:, :, m * P:(m + 1) * P]
                            lo = xT[1][:, :, m * P:(m + 1) * P]
                            if rms:
                                for k in range(KD):
                                    i = dve.scalar_tensor_tensor(
                                        out=lo[:, k, :], in0=src[:, k, :], scalar=nw[:, k:k + 1],
                                        in1=hi[:, k, :].bitcast(F32), op0=ALU.mult, op1=ALU.subtract)
                            else:
                                i = dve.tensor_tensor(lo, src, hi.bitcast(F32), ALU.subtract)
                            i.then_inc(s_lo, 1)

                    @block.scalar
                    def _(act):
                        for n in range(rounds):
                            act.wait_ge(s_var, v0 + n + 1)
                            act.activation(sd[:], mv[:, :, 1], ACT.Sqrt, bias=eps[:, 0:1]).then_inc(s_sd, 1)
                        if rms:
                            act.wait_ge(s_var, v0 + rounds + 1)
                            act.activation(sd[:], qs[:, :, 0], ACT.Sqrt, bias=eps[:, 2:3],
                                           scale=1.0 / DM).then_inc(s_sd, 1)
                            act.wait_ge(s_x, 16 * ((MT if load_x else 0) + 1))
                        if xT is None:
                            return
                        for m in range(MT):
                            act.wait_ge(s_t, m0 + m + 1)
                            src = tb[m][:].rearrange("p (k t) -> p k t", k=KD)
                            hi = xT[0][:, :, m * P:(m + 1) * P]
                            if rms:
                                for k in range(KD):
                                    i = act.activation(hi[:, k, :], src[:, k, :], ACT.Copy, scale=nw[:, k:k + 1])
                            else:
                                i = act.activation(hi, src, ACT.Copy)
                            i.then_inc(s_hi, 1)

                    @block.tensor
                    def _(pe):
                        if xT is None:
                            return
                        for m in range(MT):
                            pe.wait_ge(s_h, m0 + m + 1)
                            for k in range(KD):
                                i = pe.transpose(tb[m][:, k * P:(k + 1) * P], h2[:, m, k * P:(k + 1) * P], ident)
                            i.then_inc(s_t, 1)

        with nc.Block() as block:
            @block.sync
            def _(sp):
                sp.dma_start(cst[:], I["consts"]).then_inc(s_cst, 16)
                sp.wait_ge(s_cst, 16)

            @block.vector
            def _(dve):
                for i, v in enumerate((LN_EPS, SCAN_EPS, MIX_EPS, 1.0)):
                    dve.memset(eps[:, i:i + 1], v).then_inc(s_eps, 1)
                dve.wait_ge(s_eps, 4)

        with scope() as c0:
            o = sb(c0, "o1", [P, MT, DM])
            with scope() as c1:
                xc = sb(c1, "xc", [P, CD, TOK])
                sz = sb(c1, "sz", [P, CD, TOK])
                with scope() as cdt:
                    dt = sb(cdt, "dt", [P, CD, TOK])
                    with scope() as c2:
                        xT = (sb(c2, "xTh", [P, KD, TOK], F32R), sb(c2, "xTl", [P, KD, TOK], F32R))
                        with scope() as c3:
                            x = sb(c3, "x0", [P, MT, DM])
                            norm_stage("n0_", x, None, True, xT, False, None)
                        scan_in_proj(nc, sem, sb, banks, I, xT, xc, sz)
                    scan_params(nc, sem, sb, banks, I, xc, dt, cst, eps, bc_dram)
                    selective_scan(nc, sem, sb, banks, I, xc, dt, ident, bc_dram)
                scan_out_proj(nc, sem, sb, banks, I, xc, sz, o)
            with scope() as c2:
                x = sb(c2, "x1", [P, MT, DM])
                xT = (sb(c2, "xT1h", [P, KD, TOK], F32R), sb(c2, "xT1l", [P, KD, TOK], F32R))
                norm_stage("n1_", x, o, True, xT, False, None)
                experts(nc, sem, sb, banks, I, xT, o, ident)
                s_move = sem("moved")
                o_dram = nc.dram_tensor("o_kept", [TOK, DM], F32, kind="Internal").ap().rearrange(
                    "(m p) d -> p m d", p=P)
                with nc.Block() as block:
                    @block.sync
                    def _(sp):
                        sp.dma_start(x_dram, x[:]).then_inc(s_move, 16)
                        sp.dma_start(o_dram, o[:]).then_inc(s_move, 16)
                        sp.wait_ge(s_move, 32)
        with scope() as c0:
            acc = sb(c0, "acc", [P, MT, DM])
            with scope() as c1:
                xT = (sb(c1, "xT2h", [P, KD, TOK], F32R), sb(c1, "xT2l", [P, KD, TOK], F32R))
                with scope() as c2:
                    x = sb(c2, "x2", [P, MT, DM])
                    o = sb(c2, "o2", [P, MT, DM])
                    with nc.Block() as block:
                        @block.sync
                        def _(sp):
                            sp.dma_start(x[:], x_dram).then_inc(s_move, 16)
                            sp.dma_start(o[:], o_dram).then_inc(s_move, 16)
                            sp.wait_ge(s_move, 64)
                    norm_stage("n2_", x, o, False, xT, True, acc)
                mixer(nc, sem, sb, banks, I, xT, acc, cst, eps, acs_dram)
            with scope() as c1:
                x = sb(c1, "x3", [P, MT, DM])
                with nc.Block() as block:
                    @block.sync
                    def _(sp):
                        sp.dma_start(x[:], x_dram).then_inc(s_move, 16)
                        sp.wait_ge(s_move, 80)
                xT = (sb(c1, "xT3h", [P, KD, TOK], F32R), sb(c1, "xT3l", [P, KD, TOK], F32R))
                norm_stage("n3_", x, acc, False, xT, False, None, quant=True)
                o = sb(c1, "o3", [P, MT, DM])
                ffn(nc, sem, sb, banks, I, xT, o, ident)
                norm_stage("n4_", x, o, False, None, False, None)


def conv_half(dve, ch, cv, src, w, b):
    c3 = cv.rearrange("p (b t) -> p b t", t=SEQ)
    s3 = src.rearrange("p (b t) -> p b t", t=SEQ)
    ch.link(dve.tensor_scalar(cv, src, w[:, TAPS - 1:TAPS], b, ALU.mult, ALU.add))
    for s in range(1, TAPS):
        i = dve.scalar_tensor_tensor(out=c3[:, :, s:], in0=s3[:, :, :SEQ - s], scalar=w[:, TAPS - 1 - s:TAPS - s],
                                     in1=c3[:, :, s:], op0=ALU.mult, op1=ALU.add)
        if s < TAPS - 1:
            ch.link(i)
    return i


def rows3(ap):
    return ap.rearrange("a p k n -> (a p) k n")


def scan_in_proj(nc, sem, sb, banks, I, xT, xc, sz):
    with ExitStack() as c:
        ws = [sb(c, f"ip_ws{i}", [P, KD, 2 * P]) for i in range(2)]
        wh = [sb(c, f"ip_wh{i}", [P, KD, 2 * P], F32R) for i in range(2)]
        wl = [sb(c, f"ip_wl{i}", [P, KD, 2 * P], F32R) for i in range(2)]
        cw = sb(c, "ip_cw", [P, CD, TAPS])
        cb = sb(c, "ip_cb", [P, CD])
        cv = [sb(c, f"ip_cv{i}", [P, HALF]) for i in range(NH)]
        pb = banks(c, "ip_pb", 8)
        s_tab, s_w = sem("ip_tab"), [sem("ip_w0"), sem("ip_w1")]
        s_hi, s_lo, s_proj, s_gate = sem("ip_hi"), sem("ip_lo"), sem("ip_proj"), sem("pool_gate")
        s_cv, s_sx, s_sz, s_ch = sem("ip_conv"), sem("ip_silu_x"), sem("ip_silu_z"), sem("ip_dve")
        links = TAPS - 1
        with nc.Block() as block:
            @block.sync
            def _(sp):
                sp.dma_start(cw[:], I["conv_w0"]).then_inc(s_tab, 16)
                sp.dma_start(cb[:], I["conv_b0"]).then_inc(s_tab, 16)
                with sp.Fori(0, CD // 2) as i:
                    for q in range(2):
                        sp.wait_ge(s_lo, i * 2 + (q + 1))
                        sp.dma_start(ws[q][:], rows3(I["w_in0"][bass.ds(i * 2 + q, 1)])).then_inc(s_w[q], 16)

            @block.gpsimd
            def _(pool):
                pool.sem_inc(s_lo, 2)
                with pool.Fori(0, CD // 2) as i:
                    for q in range(2):
                        pool.wait_ge(s_w[q], i * 16 + 16)
                        pool.wait_ge(s_proj, i * 8 + (4 * q + 4))
                        pool.sem_inc(s_gate, 1)
                        pool.tensor_scalar(wh[q][:], ws[q][:], 1.0, 0.0, ALU.mult, ALU.add).then_inc(s_hi, 1)

                        pool.wait_ge(s_hi, i * 2 + (q + 1))
                        pool.tensor_tensor(wl[q][:], ws[q][:], wh[q][:].bitcast(F32), ALU.subtract
                                           ).then_inc(s_lo, 1)

            @block.tensor
            def _(pe):
                pe.sem_inc(s_proj, 8)
                with pe.Fori(0, CD // 2) as i:
                    for q in range(2):
                        pe.wait_ge(s_lo, i * 2 + (q + 3))
                        for j in range(4):
                            pe.wait_ge(s_cv if j < 2 else s_sz, i * 4 + (2 * q + j % 2 + 1))
                            n0 = P * (j // 2)
                            t0 = HALF * (j % 2)
                            for k in range(KD):
                                last = mm3(pe, pb[4 * q + j][:],
                                           (wh[q][:, k, n0:n0 + P], wl[q][:, k, n0:n0 + P]),
                                           (xT[0][:, k, t0:t0 + HALF], xT[1][:, k, t0:t0 + HALF]),
                                           k == 0, k == KD - 1)
                            last.then_inc(s_proj, 1)

            @block.vector
            def _(dve):
                dve.sem_inc(s_cv, 4)
                dve.wait_ge(s_tab, 32)
                with dve.Fori(0, CD // 2) as i:
                    ch = Chain(dve, s_ch, i * (4 * links))
                    for q in range(2):
                        for j in range(2):
                            dve.wait_ge(s_proj, i * 8 + (4 * q + j + 9))
                            dve.wait_ge(s_sx, i * 4 + (2 * q + j + 1))
                            conv_half(dve, ch, cv[j][:], pb[4 * q + j][:],
                                      cw[:, bass.ds(i * 2 + q, 1), :].rearrange("p a k -> p (a k)"),
                                      cb[:, bass.ds(i * 2 + q, 1)]).then_inc(s_cv, 1)

            @block.scalar
            def _(act):
                act.sem_inc(s_sx, 2)
                act.sem_inc(s_sz, 4)
                with act.Fori(0, CD // 2) as i:
                    for q in range(2):
                        for j in range(2):
                            act.wait_ge(s_cv, i * 4 + (2 * q + j + 5))
                            act.wait_ge(s_tab, 32)
                            act.activation(xc[:, bass.ds(i * 2 + q, 1), j * HALF:(j + 1) * HALF],
                                           cv[j][:].unsqueeze(1), ACT.Silu).then_inc(s_sx, 1)
                        for j in range(2):
                            act.wait_ge(s_proj, i * 8 + (4 * q + j + 11))
                            act.wait_ge(s_tab, 32)
                            act.activation(sz[:, bass.ds(i * 2 + q, 1), j * HALF:(j + 1) * HALF],
                                           pb[4 * q + 2 + j][:].unsqueeze(1), ACT.Silu).then_inc(s_sz, 1)


def scan_params(nc, sem, sb, banks, I, xc, dt, cst, eps, bc_dram):
    with ExitStack() as c:
        R = RNK + 2 * NST
        xp = sb(c, "sp_xp", [P, CD, R])
        dp = sb(c, "sp_dp", [RNK, DIN])
        db = sb(c, "sp_db", [P, CD])
        lw = sb(c, "sp_lw", [R, 1])
        p0 = sb(c, "sp_p0", [R, TOK])
        sq = sb(c, "sp_sq", [R, TOK])
        sd = sb(c, "sp_sd", [R, TOK])
        rs = sb(c, "sp_rs", [R, TOK])
        bcn = sb(c, "sp_bcn", [R, TOK])
        rl = sb(c, "sp_rl", [P, CD, TOK])
        pp = banks(c, "sp_pp", 2)
        pq = banks(c, "sp_pq", 2)
        pd = banks(c, "sp_pd", 4)
        s_in, s_pp, s_cp, s_sq, s_ss = sem("sp_in"), sem("sp_proj"), sem("sp_copied"), sem("sp_sq"), sem("sp_sums")
        s_sd, s_rs, s_bcn, s_out = sem("sp_sd"), sem("sp_rs"), sem("sp_normed"), sem("sp_bc_out")
        s_pd, s_act, s_ln, s_dt = sem("sp_dtproj"), sem("sp_act"), sem("sp_ln"), sem("sp_dt")
        with nc.Block() as block:
            @block.sync
            def _(sp):
                for t, n in ((xp, "x_proj"), (dp, "dt_proj"), (db, "dt_bias0"), (lw, "ln_w0")):
                    sp.dma_start(t[:], I[n]).then_inc(s_in, 16)
                sp.wait_ge(s_bcn, 2)
                sp.dma_start(bc_dram, bcn[RNK:R, :]).then_inc(s_out, 16)
                sp.wait_ge(s_out, 16)

            @block.tensor
            def _(pe):
                pe.wait_ge(s_in, 64)
                for h in range(NH):
                    for k in range(CD):
                        i = pe.matmul(pp[h][0:R, :], xp[:, k, :], xc[:, k, h * HALF:(h + 1) * HALF],
                                      start=k == 0, stop=k == CD - 1)
                    i.then_inc(s_pp, 1)
                for h in range(NH):
                    pe.wait_ge(s_sq, h + 1)
                    pe.matmul(pq[h][0:R, :], cst[0:R, C_BLK:C_BLK + R], sq[:, h * HALF:(h + 1) * HALF],
                              start=True, stop=True).then_inc(s_ss, 1)
                pe.wait_ge(s_bcn, 2)
                for k in range(CD):
                    for h in range(NH):
                        n = 2 * k + h
                        if n >= 4:
                            pe.wait_ge(s_act, 2 * (n - 3))
                        pe.matmul(pd[n % 4][:], dp[:, k * P:(k + 1) * P], bcn[0:RNK, h * HALF:(h + 1) * HALF],
                                  start=True, stop=True).then_inc(s_pd, 1)

            @block.vector
            def _(dve):
                for h in range(NH):
                    dve.wait_ge(s_pp, h + 1)
                    dve.tensor_copy(p0[:, h * HALF:(h + 1) * HALF], pp[h][0:R, :]).then_inc(s_cp, 1)
                for h in range(NH):
                    t = slice(h * HALF, (h + 1) * HALF)
                    dve.wait_ge(s_sd, h + 1)
                    dve.reciprocal(rs[:, t], sd[:, t]).then_inc(s_rs, 1)
                    dve.wait_ge(s_rs, h + 1)
                    dve.scalar_tensor_tensor(out=bcn[:, t], in0=p0[:, t], scalar=lw[:, 0:1], in1=rs[:, t],
                                             op0=ALU.mult, op1=ALU.mult).then_inc(s_bcn, 1)
                for k in range(CD):
                    dve.wait_ge(s_ln, k + 1)
                    dve.tensor_tensor(dt[:, k, :], dt[:, k, :], rl[:, k, :], ALU.add).then_inc(s_dt, 1)
                dve.wait_ge(s_dt, CD)

            @block.scalar
            def _(act):
                for h in range(NH):
                    t = slice(h * HALF, (h + 1) * HALF)
                    act.wait_ge(s_cp, h + 1)
                    act.activation(sq[:, t], p0[:, t], ACT.Square).then_inc(s_sq, 1)
                act.wait_ge(s_in, 64)
                for h in range(NH):
                    t = slice(h * HALF, (h + 1) * HALF)
                    act.wait_ge(s_ss, h + 1)
                    act.activation(sd[:, t], pq[h][0:R, :], ACT.Sqrt, bias=eps[0:R, 1:2],
                                   scale=cst[0:R, C_INV:C_INV + 1]).then_inc(s_sd, 1)
                for k in range(CD):
                    for h in range(NH):
                        t = slice(h * HALF, (h + 1) * HALF)
                        n = 2 * k + h
                        act.wait_ge(s_pd, n + 1)
                        act.activation(dt[:, k, t], pd[n % 4][:], ACT.Abs, bias=db[:, k:k + 1]).then_inc(s_act, 1)
                        act.activation(rl[:, k, t], pd[n % 4][:], ACT.Relu, bias=db[:, k:k + 1]).then_inc(s_act, 1)
                act.wait_ge(s_act, 4 * CD)
                for k in range(CD):
                    act.activation(dt[:, k, :], dt[:, k, :], ACT.Exp, scale=-1.0).then_inc(s_act, 1)
                for k in range(CD):
                    act.wait_ge(s_act, 4 * CD + k + 1)
                    act.activation(dt[:, k, :], dt[:, k, :], ACT.Ln, bias=eps[:, 3:4]).then_inc(s_ln, 1)


def selective_scan(nc, sem, sb, banks, I, xc, dt, ident, bc_dram):
    RA = 4
    with ExitStack() as c:
        bcb = sb(c, "ss_bc", [P, 2 * NST, HALF])
        al = sb(c, "ss_al", [P, CD, NST])
        na = sb(c, "ss_na", [P, CD, NST])
        dd = sb(c, "ss_d", [P, CD])
        dg = sb(c, "ss_dg", [P, P])
        dbx = [sb(c, f"ss_dbx{i}", [P, HALF]) for i in range(2)]
        hh = [sb(c, f"ss_h{i}", [P, HALF]) for i in range(RA)]
        pr = [sb(c, f"ss_pr{i}", [P, HALF]) for i in range(2)]
        da = banks(c, "ss_da", RA)
        u, = banks(c, "ss_u", 1)
        yb, = banks(c, "ss_y", 1)
        s_in = sem("ss_in")
        s_bc = [sem(f"ss_bc_in{i}") for i in range(NST // 4)]
        s_a, s_z, s_da, s_u, s_dbx, s_h = (sem("ss_a"), sem("ss_zero"), sem("ss_decay"), sem("ss_u_ready"),
                                           sem("ss_dbx_ready"), sem("ss_h_ready"))
        s_pr, s_y, s_dg, s_fin = sem("ss_prod"), sem("ss_summed"), sem("ss_diag"), sem("ss_done")
        UH = CD * NST
        BR = 4

        def rows_landed(eng, half, n):
            if n % BR == 0:
                eng.wait_ge(s_bc[n // BR], 32 * (half + 1))

        def tiles(eng, body):
            with eng.Fori(0, CD - 1) as k:
                body(k, False)
            body(CD - 1, True)

        with nc.Block() as block:
            @block.sync
            def _(sp):
                sp.dma_start(al[:], I["a_log0"]).then_inc(s_in, 16)
                sp.dma_start(dd[:], I["d_0"]).then_inc(s_in, 16)
                for half in range(NH):
                    for r0 in range(0, NST, BR):
                        if half:
                            sp.wait_ge(s_dbx, UH - NST + r0 + BR)
                        for r in (r0, NST + r0):
                            if half and r >= NST:
                                sp.wait_ge(s_pr, RA + UH - NST + r0 + BR)
                            src = bc_dram[r:r + BR, half * HALF:(half + 1) * HALF]
                            sp.dma_start(bcb[:, r:r + BR, :], src.partition_broadcast(P)).then_inc(s_bc[r0 // BR], 16)

            @block.scalar
            def _(act):
                act.wait_ge(s_in, 32)
                act.activation(al[:], al[:], ACT.Exp).then_inc(s_a, 1)
                act.wait_ge(s_a, 1)
                act.activation(na[:], al[:], ACT.Copy, scale=-1.0).then_inc(s_a, 1)
                act.wait_ge(s_a, 2)
                act.wait_ge(s_z, RA)
                for half in range(NH):
                    t = slice(half * HALF, (half + 1) * HALF)

                    def decay(k, n):
                        act.wait_ge(s_h, k * NST + (half * UH + n + 1))
                        act.wait_ge(s_a, 2)
                        src = dt[:, bass.ds(k, 1), t].rearrange("p a (b t) -> p (a b) t", t=SEQ)
                        act.activation(da[n % RA][:].rearrange("p (b t) -> p b t", t=SEQ)[:, :, 1:],
                                       src[:, :, 1:], ACT.Exp,
                                       scale=na[:, bass.ds(k, 1), n:n + 1].rearrange("p a n -> p (a n)")
                                       ).then_inc(s_da, 1)

                    def diag(k):
                        act.activation(dg[:], ident, ACT.Copy, scale=dd[:, bass.ds(k, 1)]).then_inc(s_dg, 1)

                    def body(k, last):
                        for n in range(RA, NST):
                            decay(k, n)
                        if not last:
                            for n in range(RA):
                                decay(k + 1, n)
                        act.wait_ge(s_y, (k + half * CD) * (NST + 1) + (2 + NST + 1))
                        act.activation(xc[:, bass.ds(k, 1), t], yb[:].unsqueeze(1), ACT.Copy).then_inc(s_fin, 1)
                        if not last:
                            diag(k + 1)

                    diag(0)
                    for n in range(RA):
                        decay(0, n)
                    tiles(act, body)
                act.wait_ge(s_fin, NH * CD)

            @block.vector
            def _(dve):
                dve.sem_inc(s_h, RA)
                for i in range(RA):
                    dve.memset(da[i][:].rearrange("p (b t) -> p b t", t=SEQ)[:, :, 0:1], 0.0).then_inc(s_z, 1)
                dve.wait_ge(s_in, 32)
                for half in range(NH):
                    t = slice(half * HALF, (half + 1) * HALF)

                    def inputs(k, n):
                        dve.wait_ge(s_h, (k * NST) + (half * UH + n + RA - 1))
                        rows_landed(dve, half, n)
                        dve.tensor_tensor(dbx[n % 2][:], u[:], bcb[:, n, :], ALU.mult).then_inc(s_dbx, 1)

                    def dt_x(k):
                        flat = lambda a: a[:, bass.ds(k, 1), t].rearrange("p a t -> p (a t)")
                        dve.wait_ge(s_dbx, k * NST + half * UH) if half or not isinstance(k, int) else None
                        dve.tensor_tensor(u[:], flat(dt), flat(xc), ALU.mult).then_inc(s_u, 1)

                    def body(k, last):
                        base = k * NST + half * UH
                        for n in range(NST):
                            if n + 1 < NST:
                                inputs(k, n + 1)
                            elif not last:
                                dve.wait_ge(s_u, k + (half * CD + 2))
                                inputs(k + 1, 0)
                            dve.wait_ge(s_dbx, base + (n + 1))
                            dve.wait_ge(s_da, base + (n + 1))
                            dve.wait_ge(s_pr, base + (n + 1))
                            dve.tensor_tensor_scan(hh[n % RA][:], da[n % RA][:], dbx[n % 2][:], 0.0,
                                                   ALU.mult, ALU.add).then_inc(s_h, 1)
                            if n == NST - 2 and not last:
                                dt_x(k + 1)

                    dt_x(0)
                    dve.wait_ge(s_u, half * CD + 1)
                    inputs(0, 0)
                    tiles(dve, body)

            @block.gpsimd
            def _(pool):
                pool.sem_inc(s_pr, RA)
                for half in range(NH):
                    with pool.Fori(0, CD) as k:
                        base = k * NST + half * UH
                        for n in range(NST):
                            pool.wait_ge(s_h, base + (RA + n + 1))
                            rows_landed(pool, half, n)
                            pool.wait_ge(s_y, k * (NST + 1) + (half * CD * (NST + 1) + n + (1 if n < 2 else 2)))
                            pool.tensor_tensor(pr[n % 2][:], hh[n % RA][:], bcb[:, NST + n, :], ALU.mult
                                               ).then_inc(s_pr, 1)

            @block.tensor
            def _(pe):
                pe.sem_inc(s_y, 2)
                for half in range(NH):
                    t = slice(half * HALF, (half + 1) * HALF)
                    with pe.Fori(0, CD) as k:
                        base = k * NST + half * UH
                        pe.wait_ge(s_dg, k + (half * CD + 1))
                        pe.matmul(yb[:], dg[:], xc[:, bass.ds(k, 1), t].rearrange("p a t -> p (a t)"),
                                  start=True, stop=False).then_inc(s_y, 1)
                        for n in range(NST):
                            pe.wait_ge(s_pr, base + (RA + n + 1))
                            pe.matmul(yb[:], ident, pr[n % 2][:], start=False, stop=n == NST - 1
                                      ).then_inc(s_y, 1)


def scan_out_proj(nc, sem, sb, banks, I, xc, sz, o):
    with ExitStack() as c:
        wo = sb(c, "op_w", [P, CD, DM])
        wh = sb(c, "op_wh", [P, CD, DM], F32R)
        wl = sb(c, "op_wl", [P, CD, DM], F32R)
        yh = [sb(c, f"op_yh{i}", [P, TOK], F32R) for i in range(CD)]
        yl = [sb(c, f"op_yl{i}", [P, TOK], F32R) for i in range(2)]
        ob = banks(c, "op_b", MT)
        s_w, s_o, s_c, s_y, s_hi, s_lo, s_wh, s_wl = (sem("op_w_in"), sem("op_mm"), sem("op_copied"), sem("op_y"),
                                                      sem("op_hi"), sem("op_lo"), sem("op_w_hi"), sem("op_w_lo"))
        with nc.Block() as block:
            @block.sync
            def _(sp):
                for k in range(CD):
                    sp.dma_start(wo[:, k, :], I["w_out0"][:, k, :]).then_inc(s_w, 16)

            @block.gpsimd
            def _(pool):
                pool.wait_ge(s_w, 16 * CD)
                for k in range(CD):
                    pool.wait_ge(s_wh, k + 1)
                    pool.tensor_tensor(wl[:, k, :], wo[:, k, :], wh[:, k, :].bitcast(F32), ALU.subtract
                                       ).then_inc(s_wl, 1)

            @block.tensor
            def _(pe):
                for k in range(CD):
                    pe.wait_ge(s_lo, k + 1)
                    pe.wait_ge(s_wl, k + 1)
                    for m in range(MT):
                        r = slice(m * P, (m + 1) * P)
                        i = mm3(pe, ob[m][:], (yh[k][:, r], yl[k % 2][:, r]), (wh[:, k, :], wl[:, k, :]),
                                k == 0, k == CD - 1)
                        if k == CD - 1 or m == MT - 1:
                            i.then_inc(s_o, 1)

            @block.scalar
            def _(act):
                for k in range(CD):
                    if k == 0:
                        act.wait_ge(s_w, 16 * CD)
                    act.activation(wh[:, k, :], wo[:, k, :], ACT.Copy).then_inc(s_wh, 1)
                    act.wait_ge(s_y, k + 1)
                    act.activation(yh[k][:], xc[:, k, :], ACT.Copy).then_inc(s_hi, 1)
                for m in range(MT):
                    act.wait_ge(s_o, CD + m)
                    act.activation(o[:, m, :], ob[m][:], ACT.Copy).then_inc(s_c, 1)
                act.wait_ge(s_c, MT)

            @block.vector
            def _(dve):
                def gated(k):
                    dve.tensor_tensor(xc[:, k, :], xc[:, k, :], sz[:, k, :], ALU.mult).then_inc(s_y, 1)

                gated(0)
                for k in range(CD):
                    if k + 1 < CD:
                        gated(k + 1)
                    dve.wait_ge(s_hi, k + 1)
                    dve.wait_ge(s_y, k + 1)
                    if k >= 2:
                        dve.wait_ge(s_o, k - 1)
                    dve.tensor_tensor(yl[k % 2][:], xc[:, k, :], yh[k][:].bitcast(F32), ALU.subtract
                                      ).then_inc(s_lo, 1)


def experts(nc, sem, sb, banks, I, xT, o, ident):
    with ExitStack() as c:
        N2 = NE * ER + GW
        N = DM + N2
        ws = sb(c, "ex_ws", [P, KD, N])
        wh = sb(c, "ex_wh", [P, KD, N], F32R)
        wl = sb(c, "ex_wl", [P, KD, N], F32R)
        bb = sb(c, "ex_bb", [P, DM])
        bt = sb(c, "ex_bt", [P, 1])
        bw = sb(c, "ex_bw", [NE * ER, DM])
        hg = sb(c, "ex_hg", [P, MT, N2])
        mx = sb(c, "ex_mx", [P, MT])
        e = sb(c, "ex_e", [P, MT, NE])
        th = sb(c, "ex_th", [P, MT])
        sm = sb(c, "ex_sm", [P, MT])
        zr = sb(c, "ex_zr", [P, MT])
        hT = sb(c, "ex_hT", [P, TOK])
        pa = banks(c, "ex_pa", 4)
        pb = banks(c, "ex_pb", 4)
        s_w, s_b, s_hi, s_lo = sem("ex_w_in"), sem("ex_b_in"), sem("ex_hi"), sem("ex_lo")
        s_p, s_g, s_ch, s_d, s_e = sem("ex_rank"), sem("ex_copied"), sem("ex_dve"), sem("ex_arg"), sem("ex_exp")
        s_hw, s_t, s_hT, s_base, s_o = (sem("ex_hw"), sem("ex_turned"), sem("ex_hT_ready"), sem("ex_base"),
                                        sem("ex_out"))

        def last(a):
            return a[:].unsqueeze(2)

        with nc.Block() as block:
            @block.sync
            def _(sp):
                sp.dma_start(ws[:], I["w_ex"]).then_inc(s_w, 16)
                sp.dma_start(bb[:], I["b_base"].partition_broadcast(P).rearrange("p a n -> p (a n)")
                             ).then_inc(s_b, 16)
                sp.dma_start(bt[:], I["b_thr"].partition_broadcast(P).rearrange("p a n -> p (a n)")
                             ).then_inc(s_b, 16)
                sp.dma_start(bw[:], I["w_up"]).then_inc(s_b, 16)

            @block.scalar
            def _(act):
                act.wait_ge(s_w, 16)
                for k in range(KD):
                    act.activation(wh[:, k, :], ws[:, k, :], ACT.Copy).then_inc(s_hi, 1)
                act.wait_ge(s_b, 48)
                act.wait_ge(s_d, 1)
                act.activation(th[:], hg[:, :, NE * ER + NE], ACT.Sigmoid, bias=bt[:, 0:1]).then_inc(s_e, 1)
                act.activation(e[:], e[:], ACT.Exp).then_inc(s_e, 1)
                for m in range(MT):
                    act.wait_ge(s_t, m + 1)
                    act.activation(hT[:, m * P:(m + 1) * P], pb[m % 4][:, 0:P], ACT.Copy).then_inc(s_hT, 1)

            @block.tensor
            def _(pe):
                pe.wait_ge(s_lo, KD)
                for m in range(MT):
                    if m >= 4:
                        pe.wait_ge(s_g, m - 3)
                    for k in range(KD):
                        t = slice(m * P, (m + 1) * P)
                        i = mm3(pe, pb[m % 4][:, 0:N2], (xT[0][:, k, t], xT[1][:, k, t]),
                                (wh[:, k, DM:], wl[:, k, DM:]), k == 0, k == KD - 1)
                    i.then_inc(s_p, 1)

                def base(m, stop):
                    t = slice(m * P, (m + 1) * P)
                    for k in range(KD):
                        mm3(pe, pa[m % 4][:], (xT[0][:, k, t], xT[1][:, k, t]),
                            (wh[:, k, 0:DM], wl[:, k, 0:DM]), k == 0, False)

                for m in range(4):
                    base(m, False)
                pe.wait_ge(s_g, MT)
                pe.wait_ge(s_b, 48)
                for m in range(MT):
                    pe.wait_ge(s_hw, m + 1)
                    if m >= 4:
                        pe.wait_ge(s_hT, m - 3)
                    pe.transpose(pb[m % 4][:, 0:P], hg[:, m, 0:NE * ER], ident).then_inc(s_t, 1)
                for m in range(MT):
                    if m >= 4:
                        pe.wait_ge(s_o, m - 3)
                        base(m, False)
                    pe.wait_ge(s_hT, m + 1)
                    pe.matmul(pa[m % 4][:], hT[:, m * P:(m + 1) * P], bw[:], start=False, stop=True
                              ).then_inc(s_base, 1)

            @block.vector
            def _(dve):
                for k in range(KD):
                    dve.wait_ge(s_hi, k + 1)
                    dve.tensor_tensor(wl[:, k, :], ws[:, k, :], wh[:, k, :].bitcast(F32), ALU.subtract
                                      ).then_inc(s_lo, 1)
                for m in range(MT):
                    dve.wait_ge(s_p, m + 1)
                    dve.tensor_copy(hg[:, m, :], pb[m % 4][:, 0:N2]).then_inc(s_g, 1)
                dve.wait_ge(s_g, MT)
                ch = Chain(dve, s_ch)
                g = hg[:, :, NE * ER:NE * ER + NE]
                bc = [P, MT, NE]
                ch.link(dve.tensor_reduce(mx[:], g, AX_X, ALU.max))
                dve.tensor_tensor(e[:], g, last(mx).to_broadcast(bc), ALU.subtract).then_inc(s_d, 1)
                dve.wait_ge(s_e, 2)
                ch.link(dve.tensor_reduce(sm[:], e[:], AX_X, ALU.add))
                ch.mark(dve.tensor_scalar(th[:], th[:], MAX_THR, None, ALU.mult))
                ch.link(dve.reciprocal(sm[:], sm[:]))
                ch.link(dve.tensor_tensor(e[:], e[:], last(sm).to_broadcast(bc), ALU.mult))
                ch.link(dve.tensor_tensor(e[:], e[:], last(th).to_broadcast(bc), ALU.subtract))
                ch.link(dve.tensor_scalar(e[:], e[:], 0.0, None, ALU.max))
                ch.link(dve.tensor_reduce(sm[:], e[:], AX_X, ALU.add))
                ch.link(dve.tensor_scalar(zr[:], sm[:], 0.0, None, ALU.is_equal))
                ch.link(dve.tensor_tensor(sm[:], sm[:], zr[:], ALU.add))
                ch.link(dve.reciprocal(sm[:], sm[:]))
                ch.link(dve.tensor_tensor(e[:], e[:], last(sm).to_broadcast(bc), ALU.mult))
                for m in range(MT):
                    hv = hg[:, m, 0:NE * ER].rearrange("p (e r) -> p e r", r=ER)
                    ev = e[:, m, :].unsqueeze(2).to_broadcast([P, NE, ER])
                    dve.scalar_tensor_tensor(out=hv, in0=hv, scalar=MOE_SCALE, in1=ev, op0=ALU.mult,
                                             op1=ALU.mult).then_inc(s_hw, 1)
                dve.wait_ge(s_b, 48)
                for m in range(MT):
                    dve.wait_ge(s_base, m + 1)
                    dve.tensor_tensor(o[:, m, :], pa[m % 4][:], bb[:], ALU.add).then_inc(s_o, 1)
                dve.wait_ge(s_o, MT)


def mixer(nc, sem, sb, banks, I, xT, acc, cst, eps, acs_dram):
    with ExitStack() as c:
        nacs = sb(c, "mx_nacs", [P, MT, NHEAD])
        dtT = sb(c, "mx_dtT", [P, MT, NHEAD])
        mixer_steps(nc, sem, sb, banks, I, xT, cst, eps, acs_dram, nacs, dtT)
        mixer_groups(nc, sem, sb, banks, I, xT, acc, cst, eps, acs_dram, nacs, dtT)


def mixer_steps(nc, sem, sb, banks, I, xT, cst, eps, acs_dram, nacs, dtT):
    ident = cst[:, C_ID:C_ID + P]
    with ExitStack() as c:
        ws = sb(c, "st_ws", [P, KD, P])
        wh = sb(c, "st_wh", [P, KD, P], F32R)
        wl = sb(c, "st_wl", [P, KD, P], F32R)
        db = sb(c, "st_db", [P, 1])
        al = sb(c, "st_al", [P, 1])
        na = sb(c, "st_na", [P, 1])
        ab = sb(c, "st_ab", [P, TOK])
        rl = sb(c, "st_rl", [P, TOK])
        dt = sb(c, "st_dt", [P, TOK])
        da = sb(c, "st_da", [P, TOK])
        go = sb(c, "st_go", [P, TOK])
        acs = sb(c, "st_acs", [P, TOK])
        ah = sb(c, "st_ah", [P, TOK], F32R)
        alo = sb(c, "st_al_lo", [P, TOK], F32R)
        pd = banks(c, "st_pd", 2)
        pa = banks(c, "st_pa", 2)
        pt = banks(c, "st_pt", 2)
        s_in, s_hi, s_lo, s_p, s_act, s_ch, s_go = (sem("st_in"), sem("st_hi"), sem("st_lo"), sem("st_proj"),
                                                    sem("st_act"), sem("st_dve"), sem("st_go_set"))
        s_dt, s_acs, s_t, s_rows, s_out, s_end = (sem("st_dt_ready"), sem("st_acs_ready"), sem("st_turned"),
                                                  sem("st_rows"), sem("st_rows_out"), sem("st_end"))
        with nc.Block() as block:
            @block.sync
            def _(sp):
                sp.dma_start(ws[:], I["w_dt1"]).then_inc(s_in, 16)
                sp.dma_start(db[:], I["dt_bias1"]).then_inc(s_in, 16)
                sp.dma_start(al[:], I["a_log1"]).then_inc(s_in, 16)
                sp.wait_ge(s_rows, 2)
                sp.dma_start(acs_dram[0], ah[:].bitcast(F32)).then_inc(s_out, 16)
                sp.dma_start(acs_dram[1], alo[:].bitcast(F32)).then_inc(s_out, 16)
                sp.wait_ge(s_out, 32)

            @block.gpsimd
            def _(pool):
                pool.memset(go[:], 1.0).then_inc(s_go, 1)
                pool.wait_ge(s_go, 1)
                pool.memset(go[:].rearrange("p (b t) -> p b t", t=SEQ)[:, :, 0:1], 0.0).then_inc(s_go, 1)

            @block.tensor
            def _(pe):
                pe.wait_ge(s_lo, 1)
                for h in range(NH):
                    t = slice(h * HALF, (h + 1) * HALF)
                    for k in range(KD):
                        i = mm3(pe, pd[h][:], (wh[:, k, :], wl[:, k, :]), (xT[0][:, k, t], xT[1][:, k, t]),
                                k == 0, k == KD - 1)
                    i.then_inc(s_p, 1)
                for src, s_ready, dst in ((dt, s_dt, pt), (acs, s_acs, pa)):
                    pe.wait_ge(s_ready, 1)
                    for m in range(MT):
                        i = pe.transpose(dst[m // 4][:, (m % 4) * P:(m % 4 + 1) * P], src[:, m * P:(m + 1) * P], ident)
                        if m % 4 == 3:
                            i.then_inc(s_t, 1)

            @block.scalar
            def _(act):
                act.wait_ge(s_in, 48)
                act.activation(wh[:], ws[:], ACT.Copy).then_inc(s_hi, 1)
                for h in range(NH):
                    t = slice(h * HALF, (h + 1) * HALF)
                    act.wait_ge(s_p, h + 1)
                    act.activation(ab[:, t], pd[h][:], ACT.Abs, bias=db[:, 0:1]).then_inc(s_act, 1)
                    act.activation(rl[:, t], pd[h][:], ACT.Relu, bias=db[:, 0:1]).then_inc(s_act, 1)
                act.wait_ge(s_act, 4)
                act.activation(ab[:], ab[:], ACT.Exp, scale=-1.0).then_inc(s_act, 1)
                act.activation(al[:], al[:], ACT.Exp).then_inc(s_act, 1)
                act.wait_ge(s_act, 6)
                act.activation(na[:], al[:], ACT.Copy, scale=-1.0).then_inc(s_act, 1)
                act.activation(ab[:], ab[:], ACT.Ln, bias=eps[:, 3:4]).then_inc(s_act, 1)
                for h in range(2):
                    act.wait_ge(s_t, 3 + h)
                    act.activation(nacs[:, 4 * h:4 * h + 4, :], pa[h][:].rearrange("p (m t) -> p m t", t=P),
                                   ACT.Copy, scale=-1.0).then_inc(s_end, 1)
                act.wait_ge(s_end, 2)

            @block.vector
            def _(dve):
                dve.wait_ge(s_in, 48)
                dve.wait_ge(s_hi, 1)
                dve.tensor_tensor(wl[:], ws[:], wh[:].bitcast(F32), ALU.subtract).then_inc(s_lo, 1)
                dve.wait_ge(s_act, 8)
                dve.tensor_tensor(dt[:], ab[:], rl[:], ALU.add).then_inc(s_dt, 1)
                dve.wait_ge(s_dt, 1)
                ch = Chain(dve, s_ch)
                ch.link(dve.tensor_scalar(da[:], dt[:], na[:, 0:1], None, ALU.mult))
                dve.wait_ge(s_go, 2)
                dve.tensor_tensor_scan(acs[:], go[:], da[:], 0.0, ALU.mult, ALU.add).then_inc(s_acs, 1)
                dve.wait_ge(s_acs, 1)
                dve.tensor_copy(ah[:], acs[:]).then_inc(s_rows, 1)
                dve.wait_ge(s_rows, 1)
                dve.tensor_tensor(alo[:], acs[:], ah[:].bitcast(F32), ALU.subtract).then_inc(s_rows, 1)
                for h in range(2):
                    dve.wait_ge(s_t, 1 + h)
                    ch.link(dve.tensor_copy(dtT[:, 4 * h:4 * h + 4, :], pt[h][:].rearrange("p (m t) -> p m t", t=P)))


def mixer_groups(nc, sem, sb, banks, I, xT, acc, cst, eps, acs_dram, nacs, dtT):
    ident = cst[:, C_ID:C_ID + P]
    BLK = 3 * P
    NW = NG * (PAIRS + 1) + 1
    PS = PAIRS + 1
    with ExitStack() as c:
        ws = sb(c, "mg_ws", [P, KD, 2 * P])
        wh = [sb(c, f"mg_wh{i}", [P, KD, 2 * P], F32R) for i in range(2)]
        wl = [sb(c, f"mg_wl{i}", [P, KD, 2 * P], F32R) for i in range(2)]
        wos = sb(c, "mg_wos", [P, DM])
        wogh = sb(c, "mg_wogh", [P, PAIRS, DM], F32R)
        wogl = sb(c, "mg_wogl", [P, PAIRS, DM], F32R)
        yb = sb(c, "mg_y", [P, PAIRS, TOK])
        yh = [sb(c, f"mg_yh{i}", [P, PAIRS, P], F32R) for i in range(2)]
        yl = [sb(c, f"mg_yl{i}", [P, PAIRS, P], F32R) for i in range(2)]
        cbt = sb(c, "mg_cb", [P, BATCH, BLK])
        hT = [sb(c, f"mg_hT{i}", [P, TOK]) for i in range(2)]
        sg = sb(c, "mg_sg", [P, TOK])
        hc = sb(c, "mg_hc", [P, MT, P])
        sq = sb(c, "mg_sq", [P, TOK])
        ssq = sb(c, "mg_ssq", [P, TOK])
        ee = [sb(c, f"mg_e{i}", [P, BLK]) for i in range(2)]
        mm = [sb(c, f"mg_m{i}", [P, BLK]) for i in range(2)]
        rows = [sb(c, f"mg_rows{i}", [2, 2, HALF], F32R) for i in range(NH)]
        ones = sb(c, "mg_ones", [2, P], F32R)
        idr = sb(c, "mg_idr", [P, P], F32R)
        mask = sb(c, "mg_mask", [P, P], F32R)
        cwh = sb(c, "mg_cwh", [P, NW, TAPS])
        cbh = sb(c, "mg_cbh", [P, NW])
        cwc = sb(c, "mg_cwc", [P, NG + 1, TAPS])
        cbc = sb(c, "mg_cbc", [P, NG + 1])
        dp = sb(c, "mg_dp", [P, NG * PAIRS])
        gn = sb(c, "mg_gn", [P, NG * PAIRS])
        sd = sb(c, "mg_sd", [P, MT])
        rs = sb(c, "mg_rs", [P, MT])
        pb = banks(c, "mg_pb", 4)
        tb, = banks(c, "mg_tb", 1)
        gb, = banks(c, "mg_gb", 1)
        py = banks(c, "mg_py", 2)
        s_tab, s_const = sem("mg_tab"), sem("mg_const")
        s_w, s_wo, s_row = sem("mg_w"), sem("mg_wo"), [sem("mg_row0"), sem("mg_row1")]
        s_tap, s_wgl, s_yh, s_yl = sem("mg_tap"), sem("mg_wogl_ready"), sem("mg_yh"), sem("mg_yl")
        s_hi, s_lo, s_proj, s_cv, s_ch = sem("mg_hi"), sem("mg_lo"), sem("mg_proj"), sem("mg_conv"), sem("mg_dve")
        s_silu, s_cb, s_cbe = sem("mg_silu"), sem("mg_cb_mm"), sem("mg_cb_copied")
        s_gt, s_t, s_hc, s_seg, s_e = (sem("mg_gate"), sem("mg_turned"), sem("mg_hc_ready"), sem("mg_seg"),
                                       sem("mg_exp"))
        s_m, s_y, s_y1, s_y2, s_sq = sem("mg_m_ready"), sem("mg_y_mm"), sem("mg_y1"), sem("mg_y2"), sem("mg_sq_sum")
        s_wog, s_out, s_ss, s_sd, s_rs, s_acc = (sem("mg_wog_ready"), sem("mg_out"), sem("mg_ss"), sem("mg_sd"),
                                                 sem("mg_rs"), sem("mg_acc"))
        s_sqt, s_gate, s_agate = sem("mg_sq_tmp"), sem("pool_gate"), sem("act_gate")
        CVG = 4 + 2 * PAIRS
        U = 2 * BATCH
        TAIL = 4 + 2 * PAIRS + 2
        LK = TAPS - 2

        def prior(back):
            return 4 - back

        with nc.Block() as block:
            @block.sync
            def _(sp):
                for t, n in ((cwh, "cwh1"), (cbh, "cbh1"), (cwc, "cwc1"), (cbc, "cbc1"), (dp, "d_1"), (gn, "gn_1")):
                    sp.dma_start(t[:], I[n]).then_inc(s_tab, 16)

                def load_w(w, n_lo):
                    sp.wait_ge(s_lo, n_lo)
                    sp.dma_start(ws[:], rows3(I["w_in1"][bass.ds(w, 1)])).then_inc(s_w, 16)

                sp.dma_start(ws[:], I["w_in1"][0]).then_inc(s_w, 16)
                load_w(1, 4)
                load_w(2, 5)
                with sp.Fori(0, NG) as g:
                    w0 = g * PS + 1
                    for q in range(PAIRS):
                        p = g * PAIRS + q

                        def load_rows(h):
                            sp.wait_ge(s_seg, p * U + 4 * (h + 1))
                            src = acs_dram[:, bass.ds(p * 2, 2), h * HALF:(h + 1) * HALF]
                            sp.dma_start(rows[h][:].bitcast(F32), src).then_inc(s_row[h], 16)

                        load_rows(0)
                        load_w(w0 + (q + 2), w0 + (q + 2 + 3))
                        sp.wait_ge(s_wgl, p + 1)
                        sp.dma_start(wos[:], I["w_out1"][bass.ds(p, 1)].rearrange("a p n -> (a p) n")
                                     ).then_inc(s_wo, 16)
                        load_rows(1)
                    load_w(w0 + 10, w0 + 13)

            @block.gpsimd
            def _(pool):
                pool.sem_inc(s_lo, 3)
                pool.sem_inc(s_sqt, 1)

                def split(q, w, n_proj):
                    pool.wait_ge(s_w, w * 16 + 16)
                    pool.wait_ge(s_proj, n_proj)
                    pool.sem_inc(s_gate, 1)
                    pool.tensor_scalar(wh[q][:], ws[:], 1.0, 0.0, ALU.mult, ALU.add).then_inc(s_hi, 1)
                    pool.wait_ge(s_hi, w + 1)
                    pool.tensor_tensor(wl[q][:], ws[:], wh[q][:].bitcast(F32), ALU.subtract).then_inc(s_lo, 1)

                split(0, 0, 12)
                split(0, 1, 12 + 4)
                split(1, 2, 12)
                with pool.Fori(0, NG) as g:
                    w0 = g * PS + 1
                    pool.wait_ge(s_ss, g + 1)
                    pool.sem_inc(s_gate, 1)
                    pool.memset(ssq[:], 0.0).then_inc(s_sq, 1)
                    for q in range(PAIRS):
                        w = w0 + (q + 2)
                        k = 2 if q < 7 else 1
                        split(q % 2 if q < 7 else 0, w, (w + prior(k)) * 4)
                        pool.wait_ge(s_y2, g * 16 + (2 * q + 5))
                        pool.wait_ge(s_sq, g * PS + (q + 1))
                        yv = yb[:, q, :]
                        pool.tensor_tensor(sq[:], yv, yv, ALU.mult).then_inc(s_sqt, 1)
                        pool.wait_ge(s_sqt, g * PAIRS + (q + 2))
                        pool.tensor_tensor(ssq[:], ssq[:], sq[:], ALU.add).then_inc(s_sq, 1)
                    split(1, w0 + 10, (w0 + (10 + prior(3))) * 4)

            @block.tensor
            def _(pe):
                pe.sem_inc(s_proj, 12)
                pe.sem_inc(s_seg, U)
                pe.sem_inc(s_ss, 1)
                pe.sem_inc(s_out, MT)
                pe.sem_inc(s_y, 2)
                pe.wait_ge(s_const, 3)
                pieces = [[0, 1], [2, 3], [4], [5], [6], [7], [8, 9, 10, 11, 12, 13], [14, 15]]

                def proj(q, j, ks):
                    t0 = HALF * (j % 2)
                    n0 = P * (j // 2)
                    for k in ks:
                        i = mm3(pe, pb[j][:], (wh[q][:, k, n0:n0 + P], wl[q][:, k, n0:n0 + P]),
                                (xT[0][:, k, t0:t0 + HALF], xT[1][:, k, t0:t0 + HALF]), k == 0, k == KD - 1)
                    if ks[-1] == KD - 1:
                        i.then_inc(s_proj, 1)

                pe.wait_ge(s_lo, 4)
                for j in range(4):
                    proj(0, j, range(KD))
                with pe.Fori(0, NG) as g:
                    w0 = g * PS + 1
                    pe.wait_ge(s_lo, w0 + 4)
                    pe.wait_ge(s_cv, g * CVG + 4)
                    proj(0, 2, range(KD))
                    pe.wait_ge(s_silu, g * CVG + 4)
                    pe.wait_ge(s_acc, g * MT + 1)
                    for b in range(BATCH):
                        bank = (tb, gb, py[0], py[1])[b]
                        B, C = hT[0], sg
                        t = b * SEQ
                        pe.matmul(bank[:, 0:P], B[:, t:t + P], C[:, t:t + P], start=True, stop=True)
                        pe.matmul(bank[:, P:2 * P], B[:, t + P:t + SEQ], C[:, t + P:t + SEQ], start=True, stop=True)
                        pe.matmul(bank[:, 2 * P:BLK], B[:, t:t + P], C[:, t + P:t + SEQ], start=True, stop=True
                                  ).then_inc(s_cb, 1)
                    for j in (0, 1, 3):
                        proj(0, j, range(KD))
                    with pe.Fori(0, PAIRS // 2) as qq:
                        for par in range(2):
                            q = qq * 2 + par
                            p = g * PAIRS + q

                            def y_mm(u):
                                b, hh = u // 2, u % 2
                                pe.wait_ge(s_m, p * U + (u + 3))
                                if u == 0:
                                    pe.wait_ge(s_hc, p * 2 + 2)
                                if u % 4 == 0:
                                    pe.wait_ge(s_y1, p * 2 + (u // 4 + 1))
                                    if u == 0:
                                        pe.wait_ge(s_cbe, g * 4 + 4)
                                r = slice(hh * HP, (hh + 1) * HP)
                                o0 = (b % 2) * SEQ
                                kern = mm[u % 2]
                                m01 = kern[:].rearrange("p (a n) -> p a n", n=P)[:, 0:3:2, :]
                                bank = py[b // 2]
                                pe.matmul(bank[r, o0:o0 + SEQ], hc[:, 2 * b, r], m01, start=True, stop=False)
                                pe.matmul(bank[r, o0 + P:o0 + SEQ], hc[:, 2 * b + 1, r], kern[:, P:2 * P],
                                          start=False, stop=True).then_inc(s_y, 1)

                            def turn(h):
                                pe.wait_ge(s_silu, g * CVG + (q * 2 + (h + 5)))
                                if h:
                                    pe.wait_ge(s_hc, p * 2 + 1)
                                for m in range(4):
                                    mt = 4 * h + m
                                    i = pe.transpose(tb[:, m * P:(m + 1) * P], hT[par][:, mt * P:(mt + 1) * P], ident)
                                i.then_inc(s_t, 1)

                            def piece(n):
                                j, k = n // KD, n % KD
                                if n == 0:
                                    pe.wait_ge(s_lo, w0 + (q + 5))
                                if k == 0:
                                    if j < 2:
                                        pe.wait_ge(s_cv, g * CVG + (q * 2 + (4 + j + 1)))
                                    else:
                                        pe.wait_ge(s_gt, p * 2 + (j - 2 + 1))
                                proj(1 - par, j, [k])

                            for u in range(U):
                                b, hh = u // 2, u % 2
                                if u == 0:
                                    pe.wait_ge(s_cbe, g * 4 + 4)
                                if u % 4 == 0:
                                    pe.wait_ge(s_row[u // 4], p * 16 + 16)
                                pe.wait_ge(s_e, (p * U + u) * 2 + 2)
                                r0 = (b % 2) * SEQ
                                rv = rows[u // 4][:, hh, r0:r0 + SEQ]
                                pe.matmul(gb[:, 0:2 * P], ones[:], rv, start=True, stop=False)
                                pe.matmul(gb[:, 0:2 * P], idr[:], mask[:].unsqueeze(1).to_broadcast([P, 2, P]),
                                          start=False, stop=True)
                                pe.matmul(gb[:, 2 * P:BLK], ones[:], rv[:, P:], start=True, stop=True
                                          ).then_inc(s_seg, 1)
                                if u == 0:
                                    turn(0)
                                if u == 6:
                                    y_mm(u - 1)
                                for n in pieces[u]:
                                    piece(n)
                                if u == 0:
                                    turn(1)
                                elif u != 6:
                                    y_mm(u - 1)
                            y_mm(U - 1)
                    obs = (pb[0], pb[1], py[0], py[1])
                    pe.wait_ge(s_cv, g * CVG + TAIL)
                    pe.wait_ge(s_y1, g * 16 + 18)
                    pe.wait_ge(s_wgl, g * PAIRS + (PAIRS + 1))
                    for m in range(MT):
                        pe.wait_ge(s_yl, g * MT + (m + 1))
                        if m >= 4:
                            pe.wait_ge(s_acc, g * MT + (m - 2))
                        for k in range(PAIRS):
                            i = mm3(pe, obs[m % 4][:], (yh[m % 2][:, k, :], yl[m % 2][:, k, :]),
                                    (wogh[:, k, :], wogl[:, k, :]), k == 0, k == PAIRS - 1)
                        i.then_inc(s_out, 1)
                        if m == 1:
                            pe.wait_ge(s_sq, g * PS + PS)
                            for n in range(MT):
                                i = pe.matmul(tb[:, n:n + 1], ssq[:, n * P:(n + 1) * P], cst[:, C_ONE:C_ONE + 1],
                                              start=True, stop=True)
                            i.then_inc(s_ss, 1)

            @block.vector
            def _(dve):
                dve.sem_inc(s_y1, 2)
                dve.sem_inc(s_y2, 3)
                dve.sem_inc(s_m, 2)
                dve.sem_inc(s_wgl, 1)
                dve.sem_inc(s_acc, 1)
                dve.wait_ge(s_tab, 96)
                dve.memset(ones[:].bitcast(F32), 1.0).then_inc(s_const, 1)
                dve.tensor_copy(idr[:], ident).then_inc(s_const, 1)
                dve.tensor_copy(mask[:], cst[:, C_MASK:C_MASK + P]).then_inc(s_const, 1)

                def tap(s, n, j, dst, w):
                    if s == 1:
                        dve.wait_ge(s_tap, n + 1)
                    else:
                        dve.wait_ge(s_ch, n * LK + (s - 1))
                    d3 = dst[:, (j % 2) * HALF:(j % 2 + 1) * HALF].rearrange("p (b t) -> p b t", t=SEQ)[:, :, s:]
                    s3 = pb[j][:].rearrange("p (b t) -> p b t", t=SEQ)[:, :, :SEQ - s]
                    i = dve.scalar_tensor_tensor(out=d3, in0=s3, scalar=w[:, TAPS - 1 - s:TAPS - s], in1=d3,
                                                 op0=ALU.mult, op1=ALU.add)
                    i.then_inc(s_ch if s < TAPS - 1 else s_cv, 1)

                def hid_w(w):
                    return cwh[:, bass.ds(w, 1), :].rearrange("p a k -> p (a k)")

                def c_w(g):
                    return cwc[:, bass.ds(g, 1), :].rearrange("p a k -> p (a k)")

                for j in range(4):
                    for s in range(1, TAPS):
                        tap(s, j, j, hT[0] if j < 2 else sg, hid_w(0) if j < 2 else c_w(0))
                with dve.Fori(0, NG) as g:
                    w0 = g * PS + 1
                    for b in range(BATCH):
                        bank = (tb, gb, py[0], py[1])[b]
                        dve.wait_ge(s_cb, g * 4 + (b + 1))
                        dve.tensor_copy(cbt[:, b, :], bank[:, 0:BLK]).then_inc(s_cbe, 1)
                    for j in range(2):
                        for s in range(1, TAPS):
                            tap(s, g * CVG + (4 + j), j, hT[0], hid_w(w0))
                    with dve.Fori(0, PAIRS // 2) as qq:
                        for par in range(2):
                            q = qq * 2 + par
                            p = g * PAIRS + q

                            def next_tap(s, j):
                                tap(s, g * CVG + (q * 2 + (6 + j)), j, hT[1 - par], hid_w(w0 + q + 1))

                            def skip(h):
                                t = slice(h * HALF, (h + 1) * HALF)
                                dve.wait_ge(s_y, p * U + (4 * h + 6))
                                dve.scalar_tensor_tensor(out=hT[par][:, t], in0=hT[par][:, t],
                                                         scalar=dp[:, bass.ds(p, 1)], in1=py[h][:], op0=ALU.mult,
                                                         op1=ALU.add).then_inc(s_y1, 1)

                            def gated(h):
                                t = slice(h * HALF, (h + 1) * HALF)
                                dve.wait_ge(s_y1, p * 2 + (h + 3))
                                dve.wait_ge(s_gt, p * 2 + (h + 1))
                                dve.wait_ge(s_out, g * MT + MT)
                                dve.tensor_tensor(yb[:, bass.ds(q, 1), t].rearrange("p a t -> p (a t)"),
                                                  hT[par][:, t], sg[:, t], ALU.mult).then_inc(s_y2, 1)

                            for h in range(2):
                                dve.wait_ge(s_t, p * 2 + (h + 1))
                                dve.wait_ge(s_y, p * U + 2)
                                dst = hc[:, 4 * h:4 * h + 4, :].rearrange("p m (a c) -> p m a c", c=HP)
                                src = tb[:].rearrange("p (m a c) -> p m a c", a=2, c=HP)
                                dtv = dtT[:, 4 * h:4 * h + 4, bass.ds(p * 2, 2)].unsqueeze(3).to_broadcast(
                                    [P, 4, 2, HP])
                                dve.tensor_tensor(dst, src, dtv, ALU.mult).then_inc(s_hc, 1)

                            for u in range(U):
                                dve.wait_ge(s_e, (p * U + u) * 2 + 4)
                                dve.wait_ge(s_y, p * U + (u + 1))
                                dve.tensor_tensor(mm[u % 2][:], ee[u % 2][:], cbt[:, u // 2, :], ALU.mult
                                                  ).then_inc(s_m, 1)
                                if u == 2:
                                    next_tap(1, 0)
                                    next_tap(2, 0)
                                if u == 3:
                                    next_tap(3, 0)
                                if u == 4:
                                    skip(0)
                                if u == 5:
                                    for s in range(1, TAPS):
                                        next_tap(s, 1)
                                if u == 6:
                                    gated(0)
                                    dve.wait_ge(s_wog, p + 1)
                                    dve.scalar_tensor_tensor(out=wogl[:, bass.ds(q, 1), :], in0=wos[:].unsqueeze(1),
                                                             scalar=gn[:, bass.ds(p, 1)],
                                                             in1=wogh[:, bass.ds(q, 1), :].bitcast(F32),
                                                             op0=ALU.mult, op1=ALU.subtract).then_inc(s_wgl, 1)
                            skip(1)
                            gated(1)

                    obs = (pb[0], pb[1], py[0], py[1])

                    def low(m):
                        dve.wait_ge(s_yh, g * MT + (m + 1))
                        dve.tensor_tensor(yl[m % 2][:], yb[:, :, m * P:(m + 1) * P], yh[m % 2][:].bitcast(F32),
                                          ALU.subtract).then_inc(s_yl, 1)

                    def add(m):
                        dve.wait_ge(s_out, g * MT + (MT + m + 1))
                        dve.scalar_tensor_tensor(out=acc[:, m, :], in0=obs[m % 4][:], scalar=rs[:, m:m + 1],
                                                 in1=acc[:, m, :], op0=ALU.mult, op1=ALU.add).then_inc(s_acc, 1)

                    low(0)
                    low(1)
                    for j in range(2, 4):
                        for s in range(1, TAPS):
                            tap(s, g * CVG + (TAIL + j - 2), j, sg, c_w(g + 1))
                    low(2)
                    low(3)
                    dve.wait_ge(s_sd, g + 1)
                    dve.reciprocal(rs[:], sd[:]).then_inc(s_rs, 1)
                    dve.wait_ge(s_rs, g + 1)
                    add(0)
                    add(1)
                    for m in range(4, MT):
                        low(m)
                        add(m - 2)
                    add(MT - 2)
                    add(MT - 1)
                    dve.wait_ge(s_acc, g * MT + (MT + 1))

            @block.scalar
            def _(act):
                act.sem_inc(s_e, 2)
                act.wait_ge(s_tab, 96)

                def first_tap(n_proj, j, dst, w, b):
                    act.wait_ge(s_proj, n_proj)
                    act.sem_inc(s_agate, 1)
                    act.activation(dst[:, (j % 2) * HALF:(j % 2 + 1) * HALF], pb[j][:], ACT.Identity, bias=b,
                                   scale=w[:, TAPS - 1:TAPS]).then_inc(s_tap, 1)

                def silu(n_cv, j, dst):
                    act.wait_ge(s_cv, n_cv)
                    t = slice((j % 2) * HALF, (j % 2 + 1) * HALF)
                    act.activation(dst[:, t], dst[:, t], ACT.Silu).then_inc(s_silu, 1)

                def hid_w(w):
                    return cwh[:, bass.ds(w, 1), :].rearrange("p a k -> p (a k)"), cbh[:, bass.ds(w, 1)]

                def c_w(g):
                    return cwc[:, bass.ds(g, 1), :].rearrange("p a k -> p (a k)"), cbc[:, bass.ds(g, 1)]

                for j in range(4):
                    first_tap(12 + j + 1, j, hT[0] if j < 2 else sg, *(hid_w(0) if j < 2 else c_w(0)))
                for j in range(4):
                    silu(j + 1, j, hT[0] if j < 2 else sg)
                with act.Fori(0, NG) as g:
                    w0 = g * PS + 1
                    act.wait_ge(s_cb, g * 4 + 4)
                    for j in range(2):
                        first_tap((w0 + 3) * 4 + (j + 2), j, hT[0], *hid_w(w0))
                    for j in range(2):
                        silu(g * CVG + (5 + j), j, hT[0])
                    with act.Fori(0, PAIRS // 2) as qq:
                        for par in range(2):
                            q = qq * 2 + par
                            p = g * PAIRS + q
                            for u in range(U):
                                b, hh = u // 2, u % 2
                                act.wait_ge(s_seg, p * U + (u + U + 1))
                                act.wait_ge(s_m, p * U + (u + 1))
                                e3 = ee[u % 2][:].rearrange("p (a n) -> p a n", n=P)
                                g3 = gb[:, 0:BLK].rearrange("p (a n) -> p a n", n=P)
                                for a, jc in ((slice(0, 3, 2), 0), (slice(1, 2), 1)):
                                    act.activation(e3[:, a, :], g3[:, a, :], ACT.Exp,
                                                   bias=nacs[:, 2 * b + jc, bass.ds(p * 2 + hh, 1)]
                                                   ).then_inc(s_e, 1)
                                if u in (2, 5):
                                    act.wait_ge(s_y2, p * 2 + 3)
                                    j = u // 5
                                    first_tap((w0 + 4 + q) * 4 + (j + 1), j, hT[1 - par], *hid_w(w0 + q + 1))
                                if u == 3:
                                    act.wait_ge(s_wo, p * 16 + 16)
                                    act.wait_ge(s_out, g * MT + MT)
                                    act.wait_ge(s_tab, 96)
                                    act.activation(wogh[:, bass.ds(q, 1), :], wos[:].unsqueeze(1), ACT.Copy,
                                                   scale=gn[:, bass.ds(p, 1)]).then_inc(s_wog, 1)
                                if u == 5:
                                    for j in range(2, 4):
                                        act.wait_ge(s_proj, (w0 + q + 3) * 4 + (j + 1))
                                        act.wait_ge(s_y2, p * 2 + 3)
                                        act.activation(sg[:, (j - 2) * HALF:(j - 1) * HALF], pb[j][:], ACT.Silu
                                                       ).then_inc(s_gt, 1)
                                    for j in range(2):
                                        silu(g * CVG + (q * 2 + (7 + j)), j, hT[1 - par])

                    def high(m):
                        act.wait_ge(s_y2, g * 16 + (18 if m < 4 else 19))
                        act.wait_ge(s_out, g * MT + (m + 7))
                        act.activation(yh[m % 2][:], yb[:, :, m * P:(m + 1) * P], ACT.Copy).then_inc(s_yh, 1)

                    high(0)
                    high(1)
                    act.wait_ge(s_y2, g * 16 + 19)
                    for j in range(2, 4):
                        first_tap((w0 + 11) * 4 + (j + 1), j, sg, *c_w(g + 1))
                    high(2)
                    for j in range(2, 4):
                        silu(g * CVG + (TAIL + j - 1), j, sg)
                    high(3)
                    act.wait_ge(s_ss, g + 2)
                    act.activation(sd[:], tb[:, 0:MT], ACT.Sqrt, bias=eps[:, 2:3], scale=1.0 / GRP).then_inc(s_sd, 1)
                    for m in range(4, MT):
                        high(m)


def ffn(nc, sem, sb, banks, I, xT, o, ident):
    with ExitStack() as c:
        CW = 2 * QB
        ws = sb(c, "ff_ws", [P, 2, KD, CW])
        w2s = sb(c, "ff_w2s", [P, 2, DM])
        wh = [sb(c, f"ff_wh{i}", [P, 2, KD, CW], F32R) for i in range(2)]
        wl = [sb(c, f"ff_wl{i}", [P, 2, KD, CW], F32R) for i in range(2)]
        w2h = [sb(c, f"ff_w2h{i}", [P, 2, DM], F32R) for i in range(2)]
        w2l = [sb(c, f"ff_w2l{i}", [P, 2, DM], F32R) for i in range(2)]
        sc = sb(c, "ff_sc", [P, 2, FC, KD, 2])
        sc2 = sb(c, "ff_sc2", [P, FC, 2, KD])
        g = [sb(c, f"ff_g{i}", [P, CW]) for i in range(2)]
        h = [sb(c, f"ff_h{i}", [P, CW]) for i in range(2)]
        qa = [sb(c, f"ff_qa{i}", [P, 2]) for i in range(2)]
        qs = [sb(c, f"ff_qs{i}", [P, 2]) for i in range(2)]
        qr = [sb(c, f"ff_qr{i}", [P, 2]) for i in range(2)]
        hh = [sb(c, f"ff_hh{i}", [P, CW], F32R) for i in range(2)]
        hl = [sb(c, f"ff_hl{i}", [P, CW], F32R) for i in range(2)]
        pg = banks(c, "ff_pg", 3)
        pt = banks(c, "ff_pt", 2)
        po = banks(c, "ff_po", 2)
        s_sc, s_w, s_dq, s_hi, s_lo = sem("ff_sc_in"), sem("ff_w_in"), sem("ff_dequant"), sem("ff_hi"), sem("ff_lo")
        s_gu, s_g, s_h0, s_h, s_ch = sem("ff_gu"), sem("ff_silu"), sem("ff_h0"), sem("ff_h_ready"), sem("ff_dve")
        s_gate = sem("pool_gate")
        s_t, s_hh, s_hl, s_o, s_acc, s_z = (sem("ff_turned"), sem("ff_hh_ready"), sem("ff_hl_ready"), sem("ff_out"),
                                            sem("ff_acc"), sem("ff_zeroed"))
        LINKS = 4

        def chunks(eng, body):
            with eng.Fori(0, FC // 2) as i:
                for par in range(2):
                    body(i * 2 + par, par)
            body(FC - 1, 0)

        with nc.Block() as block:
            @block.sync
            def _(sp):
                sp.dma_start(sc[:], I["w13_scale"].partition_broadcast(P).rearrange(
                    "p a (s f k b) -> p (a s) f k b", s=2, f=FC, k=KD)).then_inc(s_sc, 16)
                sp.dma_start(sc2[:], I["w2_scale"].partition_broadcast(P).rearrange(
                    "p a (f b n) -> p (a f) b n", f=FC, b=2)).then_inc(s_sc, 16)

                def body(f, par):
                    sp.wait_ge(s_lo, f * 2 + 2)
                    sp.dma_start(ws[:], I["w13"][bass.ds(f, 1)].rearrange("a p s k n -> (a p) s k n")
                                 ).then_inc(s_w, 16)
                    sp.dma_start(w2s[:], I["w2"][bass.ds(f, 1)].rearrange("a p b n -> (a p) b n")).then_inc(s_w, 16)
                chunks(sp, body)

            @block.gpsimd
            def _(pool):
                pool.sem_inc(s_lo, 2)

                def body(f, par):
                    pool.wait_ge(s_dq, f * 3 + 3)
                    pool.wait_ge(s_o, f * MT + 1)
                    fl = lambda a: a[:].rearrange("p a k n -> p (a k n)")
                    f2 = lambda a: a[:].rearrange("p a n -> p (a n)")
                    pool.sem_inc(s_gate, 1)
                    pool.tensor_scalar(fl(wh[par]), fl(ws), 1.0, 0.0, ALU.mult, ALU.add).then_inc(s_hi, 1)
                    pool.tensor_scalar(f2(w2h[par]), f2(w2s), 1.0, 0.0, ALU.mult, ALU.add).then_inc(s_hi, 1)
                    pool.wait_ge(s_hi, f * 2 + 2)
                    pool.tensor_tensor(fl(wl[par]), fl(ws), fl(wh[par]).bitcast(F32), ALU.subtract).then_inc(s_lo, 1)
                    pool.tensor_tensor(f2(w2l[par]), f2(w2s), f2(w2h[par]).bitcast(F32), ALU.subtract
                                       ).then_inc(s_lo, 1)
                chunks(pool, body)

            @block.tensor
            def _(pe):
                pe.sem_inc(s_o, MT + 1)

                def body(f, par):
                    base = f * MT

                    def turn(m):
                        pe.wait_ge(s_h, base + (m + 1))
                        pe.wait_ge(s_hl, base + (m + 1))
                        for b in range(2):
                            i = pe.transpose(pt[m % 2][:, b * QB:(b + 1) * QB], h[m % 2][:, b * QB:(b + 1) * QB],
                                             ident)
                        i.then_inc(s_t, 1)

                    def down(m):
                        pe.wait_ge(s_hl, base + (m + 3))
                        pe.wait_ge(s_acc, base + (m + 1))
                        for b in range(2):
                            r = slice(b * QB, (b + 1) * QB)
                            i = mm3(pe, po[m % 2][:], (hh[m % 2][:, r], hl[m % 2][:, r]),
                                    (w2h[par][:, b, :], w2l[par][:, b, :]), b == 0, b == 1)
                        i.then_inc(s_o, 1)

                    pe.wait_ge(s_lo, f * 2 + 4)
                    for m in range(MT):
                        pe.wait_ge(s_h0, base + (m + 1))
                        t = slice(m * P, (m + 1) * P)
                        for s in range(2):
                            for k in range(KD):
                                i = mm3(pe, pg[m % 2][:, s * CW:(s + 1) * CW], (xT[0][:, k, t], xT[1][:, k, t]),
                                        (wh[par][:, s, k, :], wl[par][:, s, k, :]), k == 0, k == KD - 1)
                        i.then_inc(s_gu, 1)
                        if m >= 1:
                            turn(m - 1)
                        if m >= 2:
                            down(m - 2)
                    turn(MT - 1)
                    down(MT - 2)
                    down(MT - 1)
                chunks(pe, body)

            @block.scalar
            def _(act):
                def body(f, par):
                    base = f * MT

                    def hi(m):
                        act.wait_ge(s_t, base + (m + 1))
                        act.wait_ge(s_o, base + (m + MT))
                        act.activation(hh[m % 2][:], pt[m % 2][:, 0:CW], ACT.Copy).then_inc(s_hh, 1)
                    for m in range(MT):
                        act.wait_ge(s_gu, base + (m + 1))
                        act.wait_ge(s_h0, base + (m + 1))
                        act.activation(g[m % 2][:], pg[m % 2][:, 0:CW], ACT.Silu).then_inc(s_g, 1)
                        if m >= 1:
                            hi(m - 1)
                    hi(MT - 1)
                chunks(act, body)

            @block.vector
            def _(dve):
                dve.sem_inc(s_h0, 2)
                dve.sem_inc(s_hl, 2)
                dve.sem_inc(s_acc, 2)
                dve.memset(o[:], 0.0).then_inc(s_z, 1)
                dve.wait_ge(s_sc, 32)
                dve.wait_ge(s_z, 1)

                def dequantise(f, part):
                    dve.wait_ge(s_w, f * 32 + 32)
                    if part < 2:
                        wv = ws[:, part].rearrange("p k (b n) -> p (k b) n", n=QB)
                        scv = sc[:, part, bass.ds(f, 1)].rearrange("p a k b -> p (a k b)")
                    else:
                        wv = w2s[:].rearrange("p b (o n) -> p (b o) n", n=QB)
                        scv = sc2[:, bass.ds(f, 1)].rearrange("p a b o -> p (a b o)")
                    dve.tensor_tensor(wv, wv, scv.unsqueeze(2).to_broadcast([P, 2 * KD, QB]), ALU.mult
                                      ).then_inc(s_dq, 1)

                for part in range(3):
                    dequantise(0, part)

                def body(f, par, last=False):
                    base = f * MT
                    ch = Chain(dve, s_ch, f * (MT * LINKS))

                    def lo(m):
                        dve.wait_ge(s_hh, base + (m + 1))
                        dve.tensor_tensor(hl[m % 2][:], pt[m % 2][:, 0:CW], hh[m % 2][:].bitcast(F32), ALU.subtract
                                          ).then_inc(s_hl, 1)

                    def add(m):
                        dve.wait_ge(s_o, base + (m + MT + 2))
                        dve.tensor_tensor(o[:, m, :], o[:, m, :], po[m % 2][:], ALU.add).then_inc(s_acc, 1)

                    for m in range(MT):
                        i = m % 2
                        dve.wait_ge(s_g, base + (m + 1))
                        dve.wait_ge(s_t, base + m) if m else None
                        hv = h[i][:].rearrange("p (b n) -> p b n", n=QB)
                        dve.tensor_tensor(h[i][:], g[i][:], pg[i][:, CW:2 * CW], ALU.mult).then_inc(s_h0, 1)
                        dve.wait_ge(s_h0, base + (m + 3))
                        ch.link(dve.tensor_reduce(qa[i][:], hv, AX_X, ALU.max, apply_absolute_value=True))
                        ch.link(dve.tensor_scalar(qs[i][:], qa[i][:], 1.0 / FP8_MAX, Q_EPS, ALU.mult, ALU.add))
                        ch.link(dve.reciprocal(qr[i][:], qs[i][:]))
                        ch.link(dve.tensor_tensor(hv, hv, qr[i][:].unsqueeze(2).to_broadcast([P, 2, QB]), ALU.mult))
                        dve.tensor_tensor(hv, hv, qs[i][:].unsqueeze(2).to_broadcast([P, 2, QB]), ALU.mult
                                          ).then_inc(s_h, 1)
                        if m >= 1:
                            lo(m - 1)
                        if m >= 2:
                            add(m - 2)
                        if 1 <= m <= 3 and not last:
                            dequantise(f + 1, m - 1)
                    lo(MT - 1)
                    add(MT - 2)
                    add(MT - 1)
                with dve.Fori(0, FC // 2) as i:
                    for par in range(2):
                        body(i * 2 + par, par)
                body(FC - 1, 0, True)
                dve.wait_ge(s_acc, FC * MT + 2)


def laid_out(a):
    import numpy as np

    f = lambda n: np.asarray(a[n])
    z = lambda *s: np.zeros(s, np.float32)

    def ktile(w, n):
        return w.reshape(-1, n, KD, P).transpose(0, 3, 2, 1)

    def col(v, n):
        return v.reshape(n, P).T

    consts = z(P, C_N)
    consts[:, C_ID:C_ID + P] = np.eye(P)
    tri = np.where(np.arange(P)[:, None] > np.arange(P)[None, :], -1e30, 0.0)
    consts[:, C_MASK:C_MASK + P] = tri
    consts[:, C_MASK + P:C_MASK + 2 * P] = tri
    edges = (0, RNK, RNK + NST, RNK + 2 * NST)
    for lo, hi in zip(edges, edges[1:]):
        consts[lo:hi, C_BLK + lo:C_BLK + hi] = 1.0
        consts[lo:hi, C_INV] = 1.0 / (hi - lo)
    consts[:, C_ONE] = 1.0

    w0 = f("L0_attn_in_proj_w").T
    w0 = np.concatenate([w0[:DIN].reshape(CD, P, DM), w0[DIN:].reshape(CD, P, DM)], 1)
    ex = np.concatenate([f("L0_ffn_W_base"), f("L0_ffn_A_w").reshape(NE * ER, DM), f("L0_ffn_W_gate"),
                         f("L0_ffn_W_thr")[None], z(1, DM)])

    w1 = f("L1_attn_in_proj_w")
    gate, hid = w1[:DI1].reshape(NG, PAIRS, P, DM), w1[DI1:2 * DI1].reshape(NG, PAIRS, P, DM)
    pad = z(1, P, DM)
    B = np.concatenate([w1[2 * DI1:2 * DI1 + NG * NS].reshape(NG, P, DM), pad])
    C = np.concatenate([w1[2 * DI1 + NG * NS:2 * DI1 + 2 * NG * NS].reshape(NG, P, DM), pad])
    dtw = w1[2 * DI1 + 2 * NG * NS:]
    steps = [np.concatenate([B[0], C[0]])]
    for g in range(NG):
        steps += [np.concatenate([hid[g, q], gate[g, q]]) for q in range(PAIRS)]
        steps.append(np.concatenate([B[g + 1], C[g + 1]]))
    steps += [z(2 * P, DM)] * 2
    cw, cb = f("L1_attn_conv_w"), f("L1_attn_conv_b")
    ch = cw[:DI1].reshape(NG, PAIRS, P, TAPS)
    cB = np.concatenate([cw[DI1:DI1 + NG * NS].reshape(NG, P, TAPS), z(1, P, TAPS)])
    cC = np.concatenate([cw[DI1 + NG * NS:].reshape(NG, P, TAPS), z(1, P, TAPS)])
    bh = cb[:DI1].reshape(NG, PAIRS, P)
    bB = np.concatenate([cb[DI1:DI1 + NG * NS].reshape(NG, P), z(1, P)])
    bC = np.concatenate([cb[DI1 + NG * NS:].reshape(NG, P), z(1, P)])
    cwh, cbh = [cB[0]], [bB[0]]
    for g in range(NG):
        cwh += list(ch[g]) + [cB[g + 1]]
        cbh += list(bh[g]) + [bB[g + 1]]

    def chunks(w):
        return w.reshape(FC, 2 * QB, KD, P).transpose(0, 3, 2, 1)

    def scales(s):
        return s.reshape(FC, 2, KD).transpose(0, 2, 1)

    return {
        "consts": consts,
        "x": f("L0_attn_hidden_states").reshape(TOK, DM),
        "w_in0": ktile(w0.reshape(-1, DM), 2 * P),
        "conv_w0": f("L0_attn_conv_w").reshape(CD, P, TAPS).transpose(1, 0, 2),
        "conv_b0": col(f("L0_attn_conv_b"), CD),
        "x_proj": f("L0_attn_x_proj_w").T.reshape(CD, P, -1).transpose(1, 0, 2),
        "dt_proj": f("L0_attn_dt_proj_w").T,
        "dt_bias0": col(f("L0_attn_dt_bias"), CD),
        "ln_w0": np.concatenate([f("L0_attn_dt_ln_w"), f("L0_attn_B_ln_w"), f("L0_attn_C_ln_w")])[:, None],
        "a_log0": f("L0_attn_A_log").reshape(CD, P, NST).transpose(1, 0, 2),
        "d_0": col(f("L0_attn_D_param"), CD),
        "w_out0": f("L0_attn_out_proj_w").T.reshape(CD, P, DM).transpose(1, 0, 2),
        "w_ex": ktile(ex, len(ex))[0],
        "b_base": f("L0_ffn_b_base")[None],
        "b_thr": f("L0_ffn_b_thr")[None],
        "w_up": f("L0_ffn_B_w").transpose(0, 2, 1).reshape(NE * ER, DM),
        "norm_w1": col(f("L1_attn_norm_w"), KD),
        "w_dt1": ktile(dtw, P)[0],
        "dt_bias1": f("L1_attn_dt_bias")[:, None],
        "a_log1": f("L1_attn_A_log")[:, None],
        "w_in1": ktile(np.concatenate(steps), 2 * P),
        "cwh1": np.stack(cwh, 1), "cbh1": np.stack(cbh, 1),
        "cwc1": cC.transpose(1, 0, 2), "cbc1": bC.T,
        "d_1": col(np.repeat(f("L1_attn_Dp"), HP), NG * PAIRS),
        "gn_1": col(f("L1_attn_gnorm_w"), NG * PAIRS),
        "w_out1": f("L1_attn_out_proj_w").T.reshape(NG * PAIRS, P, DM),
        "w13": np.stack([chunks(f("L1_ffn_w1")), chunks(f("L1_ffn_w3"))], 2),
        "w13_scale": np.stack([scales(f("L1_ffn_w1_scale")), scales(f("L1_ffn_w3_scale"))]).reshape(1, -1),
        "w2": f("L1_ffn_w2").T.reshape(FC, 2, P, DM).transpose(0, 2, 1, 3),
        "w2_scale": f("L1_ffn_w2_scale").T.reshape(1, -1),
    }


def kernel(**inputs):
    import concourse.bacc as bacc
    import numpy as np
    from concourse.bass_utils import run_bass_kernel_spmd

    nc = bacc.Bacc("TRN2", target_bir_lowering=False, num_devices=1)
    arrays, aps = {}, {}
    for name, a in laid_out(inputs).items():
        a = np.ascontiguousarray(a, dtype=np.float32)
        arrays["in_" + name] = a
        aps[name] = nc.dram_tensor("in_" + name, a.shape, F32, kind="ExternalInput").ap()
    out = nc.dram_tensor("out_0", (TOK, DM), F32, kind="ExternalOutput").ap()
    build(nc, aps, out)
    r = run_bass_kernel_spmd(nc, [arrays], core_ids=[0])
    return r.results[0]["out_0"].reshape(BATCH, SEQ, DM)
```
